# Optimizing a Trainium2 kernel written in Bass

```python
import numpy as np
import jax
import jax.numpy as jnp

def _softmax(x, axis=-1):
    return jax.nn.softmax(x, axis=axis)

def _gelu(x):
    return jax.nn.gelu(x, approximate=True)

def _silu(x):
    return jax.nn.silu(x)

def _sigmoid(x):
    return jax.nn.sigmoid(x)

def _layernorm(x, axis=-1, eps=1e-05):
    m = jnp.mean(x, axis=axis, keepdims=True)
    v = jnp.var(x, axis=axis, keepdims=True)
    return (x - m) / jnp.sqrt(v + eps)

def _scatter_add(tgt, idx, src, axis=0):
    return tgt.at[idx].add(src)

def _segment_sum(src, seg, n):
    return jax.ops.segment_sum(src, seg, n)
kernel_name = 'mk_lm_tower_d1_tok_ids256_r4_8137df'

def setup_inputs(seed: int=0):
    np.random.seed(seed)
    _w = jnp.asarray

    def _rec_inputs():
        import jax
        import jax.numpy as jnp
        _rk = jax.random.key(seed)
        x = jax.random.randint(jax.random.fold_in(_rk, 1), (128, 200), 0, 50001, jnp.int32)
        return x
    x = _rec_inputs()

    def _L0_tok_setup():
        import jax, jax.numpy as jnp
        import numpy as np
        L = 2
        MAXLEN = 200
        HID = 64
        DFF = 4 * HID
        NITEM = 50001
        EPS = 1e-12

        def _ln(x, w, b):
            u = jnp.mean(x, axis=-1, keepdims=True)
            s = jnp.mean((x - u) ** 2, axis=-1, keepdims=True)
            return w * (x - u) / jnp.sqrt(s + EPS) + b
        key = jax.random.key(seed)
        ks = jax.random.split(key, 12)
        inp = {'input_ids': jax.random.randint(ks[0], (128, MAXLEN), 0, NITEM, dtype=jnp.int64), 'item_emb': jax.random.normal(ks[1], (NITEM, HID), jnp.float32) * 0.02, 'pos_emb': jax.random.normal(ks[2], (MAXLEN, HID), jnp.float32) * 0.02, 'ln0_w': jnp.ones((HID,), jnp.float32), 'ln0_b': jnp.zeros((HID,), jnp.float32), 'cw': jax.random.normal(ks[3], (L, MAXLEN // 2 + 1, HID, 2), jnp.float32) * 0.02, 'fln_w': jnp.ones((L, HID), jnp.float32), 'fln_b': jnp.zeros((L, HID), jnp.float32), 'd1_w': jax.random.normal(ks[4], (L, HID, DFF), jnp.float32) * 0.02, 'd1_b': jnp.zeros((L, DFF), jnp.float32), 'd2_w': jax.random.normal(ks[5], (L, DFF, HID), jnp.float32) * 0.02, 'd2_b': jnp.zeros((L, HID), jnp.float32), 'iln_w': jnp.ones((L, HID), jnp.float32), 'iln_b': jnp.zeros((L, HID), jnp.float32)}
        return inp
    _L0_tok_all = _L0_tok_setup()
    _L0_tok_in = {k: v for k, v in _L0_tok_all.items() if k in ('item_emb', 'pos_emb', 'ln0_w', 'ln0_b', 'cw', 'fln_w', 'fln_b', 'd1_w', 'd1_b', 'd2_w', 'd2_b', 'iln_w', 'iln_b')}
    del _L0_tok_all

    def _L0_attn_setup():
        import jax, jax.numpy as jnp
        import numpy as np
        import math
        NUM_HEADS = 8
        HEAD_SIZE = 32

        def get_alibi_slopes(n_heads):

            def pow2_slopes(n):
                start = 2.0 ** (-2.0 ** (-(math.log2(n) - 3)))
                ratio = start
                return [start * ratio ** i for i in range(n)]
            if math.log2(n_heads).is_integer():
                return np.array(pow2_slopes(n_heads), dtype=np.float32)
            cp2 = 2 ** math.floor(math.log2(n_heads))
            extra = pow2_slopes(2 * cp2)[0::2][:n_heads - cp2]
            return np.array(pow2_slopes(cp2) + extra, dtype=np.float32)
        ALIBI_SLOPES = jnp.asarray(get_alibi_slopes(NUM_HEADS))
        key = jax.random.key(seed)
        ks = jax.random.split(key, 6)
        B, T, C = (32, 128, 64)
        s = 1.0 / math.sqrt(C)
        return {'x': jax.random.normal(ks[0], (B, T, C), dtype=jnp.float32), 'Wq': jax.random.normal(ks[1], (C, NUM_HEADS * HEAD_SIZE), dtype=jnp.float32) * s, 'Wk': jax.random.normal(ks[2], (C, NUM_HEADS * HEAD_SIZE), dtype=jnp.float32) * s, 'Wv': jax.random.normal(ks[3], (C, NUM_HEADS * HEAD_SIZE), dtype=jnp.float32) * s, 'Wo': jax.random.normal(ks[4], (NUM_HEADS * HEAD_SIZE, C), dtype=jnp.float32) * s, 'bo': jax.random.normal(ks[5], (C,), dtype=jnp.float32) * 0.01}
    _L0_attn_all = _L0_attn_setup()
    _L0_attn_in = {k: v for k, v in _L0_attn_all.items() if k in ('Wq', 'Wk', 'Wv', 'Wo', 'bo')}
    del _L0_attn_all

    def _L0_ffn_setup():
        import jax, jax.numpy as jnp
        import numpy as np
        B, S, H, F, E, K = (8, 1024, 64, 128, 16, 2)
        EPS = 1e-05
        key = jax.random.key(seed)
        ks = jax.random.split(key, 9)
        sc = 0.02
        return {'x': jax.random.normal(ks[0], (B, S, H), dtype=jnp.float32), 'gate_w': jax.random.normal(ks[1], (H, E), dtype=jnp.float32) * sc, 'gate_b': jnp.zeros((E,), dtype=jnp.float32), 'w1': jax.random.normal(ks[2], (E, H, F), dtype=jnp.float32) * sc, 'b1': jnp.zeros((E, F), dtype=jnp.float32), 'w2': jax.random.normal(ks[3], (E, F, H), dtype=jnp.float32) * sc, 'b2': jnp.zeros((E, H), dtype=jnp.float32), 'gamma': jnp.ones((H,), dtype=jnp.float32), 'beta': jnp.zeros((H,), dtype=jnp.float32)}
    _L0_ffn_all = _L0_ffn_setup()
    _L0_ffn_in = {k: v for k, v in _L0_ffn_all.items() if k in ('gate_w', 'gate_b', 'w1', 'b1', 'w2', 'b2', 'gamma', 'beta')}
    del _L0_ffn_all
    return {'x': x, 'L0_tok_item_emb': _L0_tok_in['item_emb'], 'L0_tok_pos_emb': _L0_tok_in['pos_emb'], 'L0_tok_ln0_w': _L0_tok_in['ln0_w'], 'L0_tok_ln0_b': _L0_tok_in['ln0_b'], 'L0_tok_cw': _L0_tok_in['cw'], 'L0_tok_fln_w': _L0_tok_in['fln_w'], 'L0_tok_fln_b': _L0_tok_in['fln_b'], 'L0_tok_d1_w': _L0_tok_in['d1_w'], 'L0_tok_d1_b': _L0_tok_in['d1_b'], 'L0_tok_d2_w': _L0_tok_in['d2_w'], 'L0_tok_d2_b': _L0_tok_in['d2_b'], 'L0_tok_iln_w': _L0_tok_in['iln_w'], 'L0_tok_iln_b': _L0_tok_in['iln_b'], 'L0_attn_Wq': _L0_attn_in['Wq'], 'L0_attn_Wk': _L0_attn_in['Wk'], 'L0_attn_Wv': _L0_attn_in['Wv'], 'L0_attn_Wo': _L0_attn_in['Wo'], 'L0_attn_bo': _L0_attn_in['bo'], 'L0_ffn_gate_w': _L0_ffn_in['gate_w'], 'L0_ffn_gate_b': _L0_ffn_in['gate_b'], 'L0_ffn_w1': _L0_ffn_in['w1'], 'L0_ffn_b1': _L0_ffn_in['b1'], 'L0_ffn_w2': _L0_ffn_in['w2'], 'L0_ffn_b2': _L0_ffn_in['b2'], 'L0_ffn_gamma': _L0_ffn_in['gamma'], 'L0_ffn_beta': _L0_ffn_in['beta']}

def reference(x, L0_tok_item_emb, L0_tok_pos_emb, L0_tok_ln0_w, L0_tok_ln0_b, L0_tok_cw, L0_tok_fln_w, L0_tok_fln_b, L0_tok_d1_w, L0_tok_d1_b, L0_tok_d2_w, L0_tok_d2_b, L0_tok_iln_w, L0_tok_iln_b, L0_attn_Wq, L0_attn_Wk, L0_attn_Wv, L0_attn_Wo, L0_attn_bo, L0_ffn_gate_w, L0_ffn_gate_b, L0_ffn_w1, L0_ffn_b1, L0_ffn_w2, L0_ffn_b2, L0_ffn_gamma, L0_ffn_beta):
    import jax
    import jax.numpy as jnp

    def _L0_tok_ref(input_ids, item_emb, pos_emb, ln0_w, ln0_b, cw, fln_w, fln_b, d1_w, d1_b, d2_w, d2_b, iln_w, iln_b):
        import jax, jax.numpy as jnp
        import numpy as np
        L = 2
        MAXLEN = 200
        HID = 64
        DFF = 4 * HID
        NITEM = 50001
        EPS = 1e-12

        def _ln(x, w, b):
            u = jnp.mean(x, axis=-1, keepdims=True)
            s = jnp.mean((x - u) ** 2, axis=-1, keepdims=True)
            return w * (x - u) / jnp.sqrt(s + EPS) + b
        seq_len = input_ids.shape[1]
        x = item_emb[input_ids] + pos_emb[None, :, :]
        x = _ln(x, ln0_w, ln0_b)
        for l in range(L):
            f = jnp.fft.rfft(x, axis=1, norm='ortho')
            w = (cw[l, :, :, 0] + 1j * cw[l, :, :, 1])[None]
            y = jnp.fft.irfft(f * w, n=seq_len, axis=1, norm='ortho')
            x = _ln(y + x, fln_w[l], fln_b[l])
            h = jax.nn.gelu(jnp.einsum('bsh,hf->bsf', x, d1_w[l]) + d1_b[l], approximate=False)
            h = jnp.einsum('bsf,fh->bsh', h, d2_w[l]) + d2_b[l]
            x = _ln(h + x, iln_w[l], iln_b[l])
        return x

    def _L0_attn_ref(x, Wq, Wk, Wv, Wo, bo):
        import jax, jax.numpy as jnp
        import numpy as np
        import math
        NUM_HEADS = 8
        HEAD_SIZE = 32

        def get_alibi_slopes(n_heads):

            def pow2_slopes(n):
                start = 2.0 ** (-2.0 ** (-(math.log2(n) - 3)))
                ratio = start
                return [start * ratio ** i for i in range(n)]
            if math.log2(n_heads).is_integer():
                return np.array(pow2_slopes(n_heads), dtype=np.float32)
            cp2 = 2 ** math.floor(math.log2(n_heads))
            extra = pow2_slopes(2 * cp2)[0::2][:n_heads - cp2]
            return np.array(pow2_slopes(cp2) + extra, dtype=np.float32)
        ALIBI_SLOPES = jnp.asarray(get_alibi_slopes(NUM_HEADS))
        B, T, C = x.shape
        H, D = (NUM_HEADS, HEAD_SIZE)
        q = (x @ Wq).reshape(B, T, H, D).transpose(0, 2, 1, 3)
        k = (x @ Wk).reshape(B, T, H, D).transpose(0, 2, 1, 3)
        v = (x @ Wv).reshape(B, T, H, D).transpose(0, 2, 1, 3)
        scale = 1.0 / math.sqrt(D)
        wei = jnp.einsum('bhtd,bhsd->bhts', q, k) * scale
        pos = jnp.arange(T)
        rel = (pos[None, :] - pos[:, None]).astype(jnp.float32)
        bias = ALIBI_SLOPES[:, None, None] * rel[None, :, :]
        wei = wei + bias[None]
        causal = pos[None, :] <= pos[:, None]
        wei = jnp.where(causal[None, None], wei, -jnp.inf)
        wei = jax.nn.softmax(wei, axis=-1)
        out = jnp.einsum('bhts,bhsd->bhtd', wei, v)
        out = out.transpose(0, 2, 1, 3).reshape(B, T, H * D)
        return out @ Wo + bo

    def _L0_ffn_ref(x, gate_w, gate_b, w1, b1, w2, b2, gamma, beta):
        import jax, jax.numpy as jnp
        import numpy as np
        B, S, H, F, E, K = (8, 1024, 64, 128, 16, 2)
        EPS = 1e-05
        gate_logits = x @ gate_w + gate_b
        topk_vals, topk_idx = jax.lax.top_k(gate_logits, K)
        topk_w = jax.nn.softmax(topk_vals, axis=-1)
        h = jax.nn.relu(jnp.einsum('bsh,ehf->bsef', x, w1) + b1)
        expert_out = jnp.einsum('bsef,efh->bseh', h, w2) + b2
        sel = jnp.take_along_axis(expert_out, topk_idx[:, :, :, None], axis=2)
        moe = jnp.sum(topk_w[..., None] * sel, axis=2)
        y = x + moe
        mu = jnp.mean(y, axis=-1, keepdims=True)
        var = jnp.var(y, axis=-1, keepdims=True)
        return (y - mu) / jnp.sqrt(var + EPS) * gamma + beta
    h = _L0_tok_ref(x, L0_tok_item_emb, L0_tok_pos_emb, L0_tok_ln0_w, L0_tok_ln0_b, L0_tok_cw, L0_tok_fln_w, L0_tok_fln_b, L0_tok_d1_w, L0_tok_d1_b, L0_tok_d2_w, L0_tok_d2_b, L0_tok_iln_w, L0_tok_iln_b)
    h = h + _L0_attn_ref(_layernorm(h, axis=-1), L0_attn_Wq, L0_attn_Wk, L0_attn_Wv, L0_attn_Wo, L0_attn_bo)
    h = h + _L0_ffn_ref(_layernorm(h, axis=-1), L0_ffn_gate_w, L0_ffn_gate_b, L0_ffn_w1, L0_ffn_b1, L0_ffn_w2, L0_ffn_b2, L0_ffn_gamma, L0_ffn_beta)
    return h

_drawn_inputs = setup_inputs


def setup_inputs(seed=0):
    import zlib

    import numpy as np

    out = dict(_drawn_inputs(seed))
    spreads = {'L0_tok_ln0_w': (1.0, 0.2),
     'L0_tok_ln0_b': (0.0, 0.1),
     'L0_tok_fln_w': (1.0, 0.2),
     'L0_tok_fln_b': (0.0, 0.1),
     'L0_tok_d1_b': (0.0, 0.1),
     'L0_tok_d2_b': (0.0, 0.1),
     'L0_tok_iln_w': (1.0, 0.2),
     'L0_tok_iln_b': (0.0, 0.1),
     'L0_ffn_gate_b': (0.0, 0.271),
     'L0_ffn_b1': (0.0, 0.8),
     'L0_ffn_b2': (0.0, 0.284),
     'L0_ffn_gamma': (1.0, 0.2),
     'L0_ffn_beta': (0.0, 0.1)}
    factors = {'L0_attn_bo': 6.644, 'L0_ffn_w1': 8.0, 'L0_ffn_w2': 6.702}
    for name, (base, spread) in spreads.items():
        noise = np.random.default_rng([zlib.crc32(name.encode()), seed]).standard_normal(out[name].shape)
        drawn = base * np.exp(spread * noise) if base else spread * noise
        out[name] = jnp.asarray(drawn.astype(out[name].dtype))
    for name, factor in factors.items():
        out[name] = (out[name] * factor).astype(out[name].dtype)
    return out
```

```python
from contextlib import ExitStack

import numpy as np

import concourse.bass as bass
from concourse import mybir

F32, F16, BF16 = mybir.dt.float32, mybir.dt.float16, mybir.dt.bfloat16
I32, U32 = mybir.dt.int32, mybir.dt.uint32
ALU = mybir.AluOpType
ACT = mybir.ActivationFunctionType
AX = mybir.AxisListType

B, S, C = 128, 200, 64
T = 100
NT = B * S // T
DFF = 256
NH, DH = 8, 32
NE, FE = 16, 128
K = S // 2 + 1
WS = 64.0
QUAD = 8
PAIR = 4
PT = PAIR * T
CH = 4
NEG = -1.0e30


class Unit:

    def __init__(self, r, c):
        self.half, self.parity = r + c // 2, c % 2
        self.n = r * 2 + c

    def __add__(self, k):
        return self.n + k

    def __sub__(self, k):
        return self.n - k


def run_steps(eng, steps, first, last, body, start=0):
    def straight(t):
        body(lambda lag: Unit((start + t - lag) // 2, (start + t - lag) % 2), lambda lag, units: 0 <= t - lag < units,
             lambda lag, n: t - lag >= n)

    for t in range(first):
        straight(t)
    with eng.Fori((start + first) // 2, (start + last) // 2) as r:
        for c in range(2):
            body(lambda lag: Unit(r, c - lag), lambda lag, units: True, lambda lag, n: True)
    for t in range(last, steps):
        straight(t)


def bcast(ap, shape):
    return ap.to_broadcast(shape)


def turn_twice(pe, out, tile, g):
    for half in range(2):
        mm = pe.matmul(out[half * C:(half + 1) * C], tile, g.ident[0:T, 0:T], start=True, stop=True)
    return mm


class LayerNorm:

    def __init__(self, nc, ctx, name, tiles, eps, sem=None):
        def sb(n, shape):
            return ctx.enter_context(nc.sbuf_tensor(f"{name}_{n}", shape, F32))

        def own(n):
            return ctx.enter_context(nc.semaphore(f"{name}_{n}"))

        sem = sem or own
        self.tiles, self.eps = tiles, eps
        self.shape = [T, tiles, C]
        self.sums = sb("sums", [T, 2, tiles])
        self.squares = sb("squares", [T, 2, tiles])
        self.shifted = sb("shifted", [T, 2, tiles])
        self.power, self.shift = sb("power", [T, tiles]), sb("shift", [T, tiles])
        self.rstd = sb("rstd", [T, 2, tiles])
        self.centered = sb("centered", [T, 2, tiles, C])
        self.squared = sb("squared", [T, 2, tiles, C])
        self.summed, self.centred, self.square_done = sem("summed"), sem("centred"), sem("square_done")
        self.squares_summed, self.shift_done, self.rstd_done = sem("squares_summed"), sem("shift_done"), sem("rstd_done")
        self.done = sem("done")

    def setup(self, pool, signal):
        pool.memset(self.power[:], -0.5).then_inc(signal, 1)
        pool.memset(self.shift[:], C * self.eps).then_inc(signal, 1)

    def per_token(self, t):
        return bcast(t.unsqueeze(2), self.shape)

    def center(self, dve, u, x, free):
        if free:
            dve.wait_ge(self.done, u - 1)
        dve.tensor_reduce(self.sums[:, u.parity], x, AX.X, ALU.add).then_inc(self.summed, 1)
        dve.wait_ge(self.summed, u + 1)
        dve.scalar_tensor_tensor(out=self.centered[:, u.parity], in0=self.per_token(self.sums[:, u.parity]),
                                 scalar=-1.0 / C, in1=x, op0=ALU.mult, op1=ALU.add).then_inc(self.centred, 1)

    def square(self, act, u):
        act.wait_ge(self.centred, u + 1)
        act.activation(self.squared[:, u.parity], self.centered[:, u.parity], ACT.Square)\
           .then_inc(self.square_done, 1)

    def sum_squares(self, dve, u):
        dve.wait_ge(self.square_done, u + 1)
        dve.tensor_reduce(self.squares[:, u.parity], self.squared[:, u.parity], AX.X, ALU.add)\
           .then_inc(self.squares_summed, 1)

    def root(self, pool, u):
        pool.wait_ge(self.squares_summed, u + 1)
        pool.tensor_tensor(self.shifted[:, u.parity], self.squares[:, u.parity], self.shift[:], ALU.add)\
            .then_inc(self.shift_done, 1)
        pool.wait_ge(self.shift_done, u + 1)
        pool.tensor_tensor(self.rstd[:, u.parity], self.shifted[:, u.parity], self.power[:], ALU.pow)\
            .then_inc(self.rstd_done, 1)

    def scale(self, dve, u, out):
        dve.wait_ge(self.rstd_done, u + 1)
        dve.scalar_tensor_tensor(out=out, in0=self.centered[:, u.parity], scalar=float(C) ** 0.5,
                                 in1=self.per_token(self.rstd[:, u.parity]), op0=ALU.mult, op1=ALU.mult)\
           .then_inc(self.done, 1)


def per_channel(row, tiles, n=C):
    return bcast(row.unsqueeze(1), [T, tiles, n])


def of_tiles(x, u, tiles, start=0):
    return x[:, bass.ds((u - start) * tiles, tiles), :]


def width(ap):
    return int(np.prod(ap.shape[1:]))


def prepare(nc, g, d):
    with ExitStack() as ctx:
        def sb(n, shape, dt=F32):
            return ctx.enter_context(nc.sbuf_tensor(n, shape, dt))

        def ps(n, shape):
            return ctx.enter_context(nc.psum_tensor(n, shape, F32))

        def sem(n):
            return ctx.enter_context(nc.semaphore(n))

        splits = [(g.ffn_w1[:, l, :], d.d1_w[l]) for l in range(2)]
        splits += [(g.w_v[:], d.Wv), (g.w_gate[:], d.gate_w),
                   (g.moe_w1[:].rearrange("p e f -> p (e f)"), d.w1)]
        staged = [sb(f"stage{n}", [2 * C, width(s)]) for n, (s, _) in enumerate(splits)]
        wq, wk = sb("wq", [C, NH * DH]), sb("wk", [C, NH * DH])
        wqT, wkT = sb("wqT", [DH, NH, 2, C]), sb("wkT", [DH, NH, 2, C])
        b2, b2_high, b2_low, b2_even = (sb("b2", [C, C]), sb("b2_high", [C, C], F16), sb("b2_low", [C, C]),
                                        sb("b2_even", [C, C]))
        freq = sb("freq", [K, 2, 2, C])
        dft = sb("dft", [K, 3, 2 * S])
        kernel2 = sb("kernel2", [C, 2, 2 * S])
        tp = ps("tp", [C, 2, 512])
        ap = ps("ap", [2 * C, 2, 512])
        kp = ps("kp", [C, 2, 512])

        staged_in, heads_in, freq_in = sem("staged_in"), sem("heads_in"), sem("freq_in")
        tables_in, ident_in, b2_in, parity_in = sem("tables_in"), sem("ident_in"), sem("b2_in"), sem("parity_in")
        set_up, high_done, low_done = sem("set_up"), sem("high_done"), sem("low_done")
        turned, turned_copied, folded = sem("turned"), sem("turned_copied"), sem("folded")
        fold_high, fold_low = sem("fold_high"), sem("fold_low")
        kernel_done, kernel_copied, kernel_out = sem("kernel_done"), sem("kernel_copied"), sem("kernel_out")
        impulse_added = sem("impulse_added")
        b2_split, b2_parts = sem("b2_split"), sem("b2_parts")

        sp_loads = [(g.ids[:], d.ids)]
        sp_loads += [(g.ffn_w2[:, l], d.d2_w[l].rearrange("(f p) h -> p f h", p=128)) for l in range(2)]
        sp_loads += [(g.ffn_b1[:], d.d1_b)]
        sp_loads += [(g.w_o[:], d.Wo.rearrange("(f p) h -> p f h", p=128)),
                     (g.moe_w2[:], d.w2.rearrange("e f h -> f e h")),
                     (g.moe_b1[:], d.b1)]
        act_loads = [(g.y_bias[0:C, n:n + 1], src.unsqueeze(1)) for n, src in enumerate((d.d2_b[0], d.d2_b[1], d.bo))]
        act_loads += [(g.pos[:], d.pos_emb.rearrange("(k p) c -> p k c", p=T)),
                      (g.table_rows[:], d.table_rows), (g.selector[:], d.selector), (g.ident_ones[:], d.ident_ones),
                      (g.iota[:], d.iota), (g.gate_b[:], bcast(d.gate_b.unsqueeze(0), [T, NE]))]
        act_loads += [(g.rows[:, n, :], bcast(src.unsqueeze(0), [T, C])) for n, src in enumerate(
            (d.ln0_w, d.ln0_b, d.fln_w[0], d.fln_w[1], d.fln_b[0], d.fln_b[1],
             d.iln_w[0], d.iln_w[1], d.iln_b[0], d.iln_b[1], d.gamma, d.beta))]
        act_loads += [(g.table_cols[0:T, par, b], d.table_cols) for par in range(2) for b in range(2)]

        with nc.Block() as block:
            @block.sync
            def _(sp):
                sp.dma_start(g.ident[:], d.ident).then_inc(ident_in, 16)
                sp.dma_start(wq[:], d.Wq).then_inc(heads_in, 16)
                sp.dma_start(wk[:], d.Wk).then_inc(heads_in, 16)
                sp.dma_start(freq[:], d.cw).then_inc(freq_in, 16)
                sp.dma_start(dft[:], d.dft).then_inc(freq_in, 16)
                for stage, (_, source) in zip(staged, splits):
                    for half in range(2):
                        part = stage[half * C:(half + 1) * C, :]
                        if len(source.shape) == 3:
                            part, source_ = part.rearrange("p (e f) -> p e f", e=NE), source.rearrange("e h f -> h e f")
                        else:
                            source_ = source
                        sp.dma_start(part, source_).then_inc(staged_in, 16)
                for dst, src in sp_loads:
                    sp.dma_start(dst, src).then_inc(tables_in, 16)
                sp.wait_ge(impulse_added, 1)
                sp.dma_start(d.filters.rearrange("l c j -> c l j"), kernel2[:]).then_inc(kernel_out, 16)
                sp.wait_ge(kernel_out, 16)
                sp.wait_ge(tables_in, 16 * (len(sp_loads) + len(act_loads)))

            @block.scalar
            def _(act):
                act.dma_start(g.parity[:], d.parity).then_inc(parity_in, 16)
                for q in range(4):
                    act.dma_start(b2[NE * q:NE * q + NE, :], d.b2).then_inc(b2_in, 16)
                act.wait_ge(set_up, 3)
                for dst, src in act_loads:
                    act.dma_start(dst, src).then_inc(tables_in, 16)
                act.wait_ge(staged_in, 16 * 2 * len(splits))
                for stage, (dst, _) in zip(staged, splits):
                    act.activation(dst, stage[:], ACT.Copy, scale=WS).then_inc(high_done, 1)
                act.wait_ge(folded, NH)
                for n in range(2):
                    act.activation(g.w_a[:, 4 * n:4 * n + 4, :], ap[:, n, :].rearrange("p (h c) -> p h c", h=4),
                                   ACT.Copy, scale=WS * DH ** -0.5).then_inc(fold_high, 1)
                act.wait_ge(kernel_done, 2)
                for l in range(2):
                    act.activation(kernel2[:, l, :], kp[:, l, 0:2 * S], ACT.Copy).then_inc(kernel_copied, 1)
                act.wait_ge(b2_in, 64)
                act.activation(b2_high[:], b2[:], ACT.Copy).then_inc(b2_split, 1)

            @block.vector
            def _(dve):
                for n, (stage, (dst, _)) in enumerate(zip(staged, splits)):
                    dve.wait_ge(high_done, n + 1)
                    dve.scalar_tensor_tensor(out=dst[C:2 * C], in0=stage[C:2 * C, :], scalar=WS, in1=dst[C:2 * C],
                                             op0=ALU.mult, op1=ALU.subtract).then_inc(low_done, 1)
                for n in range(2):
                    dve.wait_ge(turned, NH * (n + 1))
                    dst, src = (wqT, wkT)[n], tp[0:DH, n, 0:NH * C].rearrange("p (h c) -> p h c", h=NH)
                    for twice in range(2):
                        dve.tensor_copy(dst[:, :, twice, :], src).then_inc(turned_copied, 1)
                for n in range(2):
                    dve.wait_ge(fold_high, n + 1)
                    half = g.w_a[C:2 * C, 4 * n:4 * n + 4, :]
                    dve.scalar_tensor_tensor(out=half, in0=ap[C:2 * C, n, :].rearrange("p (h c) -> p h c", h=4),
                                             scalar=WS * DH ** -0.5, in1=half,
                                             op0=ALU.mult, op1=ALU.subtract).then_inc(fold_low, 1)
                dve.wait_ge(kernel_copied, 2)
                dve.tensor_scalar(kernel2[:, :, 0:2 * S:S], kernel2[:, :, 0:2 * S:S], 1.0, None, ALU.add)\
                   .then_inc(impulse_added, 1)
                dve.wait_ge(b2_split, 1)
                dve.wait_ge(parity_in, 16)
                dve.wait_ge(set_up, 3)
                dve.tensor_tensor(b2_low[:], b2[:], b2_high[:], ALU.subtract).then_inc(b2_parts, 1)
                dve.tensor_scalar(b2_even[:], b2_high[:], g.parity[:, 0:1], None, ALU.mult).then_inc(b2_parts, 1)
                dve.wait_ge(b2_parts, 2)
                dve.scalar_tensor_tensor(out=g.moe_b2[0:C, :], in0=b2_low[:], scalar=g.parity[:, 1:2], in1=b2_even[:],
                                         op0=ALU.mult, op1=ALU.add).then_inc(b2_parts, 1)

            @block.gpsimd
            def _(pool):
                pool.memset(g.y_bias[:], 0.0).then_inc(set_up, 1)
                pool.memset(g.ones[:], 1.0).then_inc(set_up, 1)
                pool.memset(g.moe_b2[:], 0.0).then_inc(set_up, 1)

            @block.tensor
            def _(pe):
                pe.wait_ge(heads_in, 32)
                pe.wait_ge(ident_in, 16)
                for n, w in enumerate((wq, wk)):
                    for h in range(NH):
                        pe.transpose(tp[0:DH, n, h * C:(h + 1) * C], w[:, h * DH:(h + 1) * DH], g.ident[0:C, 0:C])\
                          .then_inc(turned, 1)
                pe.wait_ge(turned_copied, 4)
                for h in range(NH):
                    pe.matmul(ap[:, h // 4, (h % 4) * 2 * C:(h % 4 + 1) * 2 * C],
                              wqT[:, h, :, :].rearrange("p a c -> p (a c)"),
                              wkT[:, h, :, :].rearrange("p a c -> p (a c)"), start=True, stop=True).then_inc(folded, 1)
                pe.wait_ge(freq_in, 32)
                for l in range(2):
                    for part in range(2):
                        mm = pe.matmul(kp[:, l, 0:2 * S], freq[:, l, part, :], dft[:, part and part + l, :],
                                       start=(part == 0), stop=(part == 1))
                    mm.then_inc(kernel_done, 1)


def embed(nc, g, d):
    units = NT // QUAD
    with ExitStack() as ctx:
        def sb(n, shape, dt=F32):
            return ctx.enter_context(nc.sbuf_tensor(n, shape, dt))

        def sem(n):
            return ctx.enter_context(nc.semaphore(n))

        index = sb("index", [T, 2, QUAD], I32)
        found = sb("found", [T, 2, QUAD, C])
        placed = sb("placed", [T, 2, QUAD, C])
        scaled = sb("scaled", [T, 2, QUAD, C])
        weighted = sb("weighted", [T, 2, QUAD, C])
        ln = LayerNorm(nc, ctx, "ln0", QUAD, 1e-12)
        set_up, index_ready = sem("emb_set_up"), sem("index_ready")
        found_in = [sem("found_in0"), sem("found_in1")]
        placed_done, weighted_done, stored = sem("placed_done"), sem("weighted_done"), sem("emb_stored")

        with nc.Block() as block:
            @block.gpsimd
            def _(pool):
                ln.setup(pool, set_up)
                pool.wait_ge(set_up, 2)

                def step(unit, has, later):
                    if has(0, units):
                        u = unit(0)
                        if later(0, 2):
                            pool.wait_ge(placed_done, u - 1)
                        pool.tensor_copy(index[:, u.parity], g.ids[:, bass.ds(u.n * QUAD, QUAD)]).then_inc(index_ready, 1)
                        pool.wait_ge(index_ready, u + 1)
                    if has(2, units):
                        ln.root(pool, unit(2))
                    if has(0, units):
                        for j in range(QUAD):
                            pool.indirect_dma_start(
                                out=found[:, u.parity, j, :], out_offset=None, in_=d.item_emb,
                                in_offset=bass.IndirectOffsetOnAxis(ap=index[:, u.parity, j:j + 1], axis=0),
                            ).then_inc(found_in[u.parity], 16)

                run_steps(pool, units + 2, 4, units, step)

            @block.vector
            def _(dve):
                def step(unit, has, later):
                    if has(2, units):
                        u = unit(2)
                        ln.scale(dve, u, scaled[:, u.parity])
                        dve.wait_ge(ln.done, u + 1)
                        dve.tensor_tensor(weighted[:, u.parity], scaled[:, u.parity], per_channel(g.rows[:, 0, :], QUAD),
                                          ALU.mult).then_inc(weighted_done, 1)
                        dve.wait_ge(weighted_done, u + 1)
                        dve.tensor_tensor(of_tiles(g.x, u, QUAD), weighted[:, u.parity],
                                          per_channel(g.rows[:, 1, :], QUAD), ALU.add).then_inc(stored, 1)
                    if has(0, units):
                        u = unit(0)
                        dve.wait_ge(found_in[u.parity], 16 * QUAD * u.half + 16 * QUAD)
                        if later(0, 2):
                            dve.wait_ge(ln.centred, u - 1)
                        pos = g.pos[:].unsqueeze(1).to_broadcast([T, QUAD // 2, 2, C])
                        dve.tensor_tensor(placed[:, u.parity].rearrange("p (b k) c -> p b k c", k=2),
                                          found[:, u.parity].rearrange("p (b k) c -> p b k c", k=2), pos,
                                          ALU.add).then_inc(placed_done, 1)
                        dve.wait_ge(placed_done, u + 1)
                        ln.center(dve, u, placed[:, u.parity], later(0, 2))
                        ln.sum_squares(dve, u)

                run_steps(dve, units + 2, 4, units, step)

            @block.scalar
            def _(act):
                def step(unit, has, later):
                    if has(0, units):
                        if later(0, 2):
                            act.wait_ge(ln.squares_summed, unit(0) - 1)
                        ln.square(act, unit(0))

                run_steps(act, units, 4, units, step)


def spectral_filter(nc, g, d, l):
    units = C // CH
    with ExitStack() as ctx:
        def sem(n):
            return ctx.enter_context(nc.semaphore(f"{n}_{l}"))

        circulant = ctx.enter_context(nc.sbuf_tensor(f"circulant{l}", [T, 2, CH, S], F32))
        conv = ctx.enter_context(nc.psum_tensor(f"conv{l}", [T, 2, 2, CH, B], F32))
        loaded = [sem("circulant_in0"), sem("circulant_in1")]
        convolved = sem("convolved")
        stored = [sem("filtered_first"), sem("filtered_second")]
        rows = d.filters[l]
        rows = bass.AP(tensor=rows.tensor, offset=rows.offset + 1, ap=[[1, T], [2 * S, C], [1, S]])
        x = g.x[:].rearrange("p (b k) c -> p k b c", k=2)

        with nc.Block() as block:
            @block.sync
            def _(sp):
                def step(unit, has, later):
                    u = unit(0)
                    if later(0, 2):
                        sp.wait_ge(convolved, u - 1)
                    sp.dma_start(circulant[:, u.parity], rows[:, bass.ds(u.n * CH, CH), :])\
                      .then_inc(loaded[u.parity], 16)

                run_steps(sp, units, 4, units, step)

            @block.tensor
            def _(pe):
                def step(unit, has, later):
                    u = unit(0)
                    pe.wait_ge(loaded[u.parity], 16 * u.half + 16)
                    if later(0, 2):
                        pe.wait_ge(stored[0], u - 1)
                        pe.wait_ge(stored[1], u - 1)
                    for c in range(CH):
                        for k in range(2):
                            for stay in range(2):
                                source = x[:, k if stay else 1 - k, :, bass.ds(u.n * CH + c, 1)]
                                mm = pe.matmul(conv[:, u.parity, k, c, :],
                                               circulant[:, u.parity, c, stay * T:(stay + 1) * T],
                                               source.rearrange("p b c -> p (b c)"),
                                               start=(stay == 0), stop=(stay == 1))
                    mm.then_inc(convolved, 1)

                run_steps(pe, units, 4, units, step)

            def result(u, k):
                return conv[:, u.parity, k].rearrange("p c b -> p b c")

            @block.vector
            def _(dve):
                def step(unit, has, later):
                    u = unit(0)
                    dve.wait_ge(convolved, u + 1)
                    dve.tensor_copy(x[:, 0, :, bass.ds(u.n * CH, CH)], result(u, 0)).then_inc(stored[0], 1)

                run_steps(dve, units, 4, units, step)

            @block.scalar
            def _(act):
                def step(unit, has, later):
                    u = unit(0)
                    act.wait_ge(convolved, u + 1)
                    act.activation(x[:, 1, :, bass.ds(u.n * CH, CH)], result(u, 1), ACT.Copy).then_inc(stored[1], 1)

                run_steps(act, units, 4, units, step)


def feed_forward(nc, g, d, l):
    units = NT // QUAD
    start = l * units
    with ExitStack() as ctx:
        def sb(n, shape, dt=F32):
            return ctx.enter_context(nc.sbuf_tensor(f"{n}_{l}", shape, dt))

        def ps(n, shape):
            return ctx.enter_context(nc.psum_tensor(f"{n}_{l}", shape, F32))

        def sem(n):
            if n not in g.ffn_sems:
                g.ffn_sems[n] = g.ctx.enter_context(nc.semaphore(n))
            return g.ffn_sems[n]

        scaled, weighted = sb("f_scaled", [T, 2, QUAD, C]), sb("f_weighted", [T, 2, QUAD, C])
        base = sb("f_base", [T, 2, QUAD, C])
        x1, x2 = sb("f_x1", [2 * C, 2, 2, PT], F16), sb("f_x2", [2 * C, 2, 2, PT], F16)
        hidden = sb("f_hidden", [128, 2, 2, PT])
        y = sb("f_y", [128, 2, PT])
        top, both = sb("f_top", [T, 2, QUAD, C]), sb("f_both", [T, 2, QUAD, C])
        scaled2, weighted2 = sb("f_scaled2", [T, 2, QUAD, C]), sb("f_weighted2", [T, 2, QUAD, C])
        xt_ps = ps("f_xt", [128, 2, 512])
        h_ps = ps("f_h", [128, 4, 512])
        y_ps = ps("f_yps", [128, 512])
        back_ps = ps("f_back", [T, PAIR, 2 * C])
        backs = [back_ps, xt_ps[0:T, 1, :].rearrange("p (j c) -> p j c", j=PAIR)]
        ln1 = LayerNorm(nc, ctx, f"fln{l}", QUAD, 1e-12, lambda n: sem(f"f_ln_{n}"))
        ln2 = LayerNorm(nc, ctx, f"iln{l}", QUAD, 1e-12, lambda n: sem(f"f_ln2_{n}"))
        set_up, weighted_done, base_done = sem("f_set_up"), sem("f_weighted_done"), sem("f_base_done")
        turned, x1_done, x2_done = sem("f_turned"), sem("f_x1_done"), sem("f_x2_done")
        up_done, gelu_done, down_done, y_done = sem("f_up_done"), sem("f_gelu_done"), sem("f_down_done"), sem("f_y_done")
        back_done, top_done, both_done = sem("f_back_done"), sem("f_top_done"), sem("f_both_done")
        weighted2_done, stored = sem("f_weighted2_done"), sem("f_stored")

        with nc.Block() as block:
            @block.gpsimd
            def _(pool):
                ln1.setup(pool, set_up)
                ln2.setup(pool, set_up)
                pool.wait_ge(set_up, 4 * (l + 1))

                def step(unit, has, later):
                    if has(0, units):
                        ln1.root(pool, unit(0))
                    if has(2, units):
                        ln2.root(pool, unit(2))
                    if has(0, units):
                        u = unit(0)
                        pool.wait_ge(ln1.done, u + 1)
                        if later(0, 2):
                            pool.wait_ge(both_done, 2 * (u - 1))
                        pool.tensor_tensor(weighted[:, u.parity], scaled[:, u.parity],
                                           per_channel(g.rows[:, 2 + l, :], QUAD), ALU.mult).then_inc(weighted_done, 1)
                    if has(2, units):
                        u = unit(2)
                        pool.wait_ge(ln2.done, u + 1)
                        pool.tensor_tensor(weighted2[:, u.parity], scaled2[:, u.parity],
                                           per_channel(g.rows[:, 6 + l, :], QUAD), ALU.mult).then_inc(weighted2_done, 1)
                    if has(0, units):
                        u = unit(0)
                        pool.wait_ge(weighted_done, u + 1)
                        pool.tensor_tensor(base[:, u.parity], weighted[:, u.parity],
                                           per_channel(g.rows[:, 4 + l, :], QUAD), ALU.add).then_inc(base_done, 1)
                    if has(2, units):
                        u = unit(2)
                        pool.wait_ge(weighted2_done, u + 1)
                        pool.tensor_tensor(of_tiles(g.x, u, QUAD, start), weighted2[:, u.parity],
                                           per_channel(g.rows[:, 8 + l, :], QUAD), ALU.add).then_inc(stored, 1)

                run_steps(pool, units + 2, 4, units, step, start)

            @block.vector
            def _(dve):
                def step(unit, has, later):
                    if has(2, units):
                        u = unit(2)
                        if later(2, 2):
                            dve.wait_ge(ln2.centred, u - 1)
                        for q in range(2):
                            tiles = slice(q * PAIR, q * PAIR + PAIR)
                            dve.wait_ge(back_done, 2 * u.n + q + 1)
                            dve.tensor_tensor(top[:, u.parity, tiles], backs[q][:, :, 0:C], base[:, u.parity, tiles],
                                              ALU.add).then_inc(top_done, 1)
                            dve.wait_ge(top_done, 2 * u.n + q + 1)
                            dve.tensor_tensor(both[:, u.parity, tiles], backs[q][:, :, C:2 * C], top[:, u.parity, tiles],
                                              ALU.add).then_inc(both_done, 1)
                    if has(1, units):
                        u = unit(1)
                        for q in range(2):
                            dve.wait_ge(x1_done, 2 * u.n + q + 1)
                            dve.tensor_tensor(x2[:, u.parity, q], xt_ps[:, q, 0:PT], x1[:, u.parity, q],
                                              ALU.subtract).then_inc(x2_done, 1)
                    if has(0, units):
                        u = unit(0)
                        ln1.center(dve, u, of_tiles(g.x, u, QUAD, start), later(0, 2))
                    if has(2, units):
                        u = unit(2)
                        dve.wait_ge(both_done, 2 * u.n + 2)
                        ln2.center(dve, u, both[:, u.parity], later(2, 2))
                    if has(0, units):
                        ln1.sum_squares(dve, unit(0))
                    if has(2, units):
                        ln2.sum_squares(dve, unit(2))
                    if has(0, units):
                        u = unit(0)
                        if later(0, 2):
                            dve.wait_ge(weighted_done, u - 1)
                        ln1.scale(dve, u, scaled[:, u.parity])
                    if has(2, units):
                        u = unit(2)
                        if later(2, 2):
                            dve.wait_ge(weighted2_done, u - 1)
                        ln2.scale(dve, u, scaled2[:, u.parity])

                run_steps(dve, units + 2, 4, units, step, start)

            @block.scalar
            def _(act):
                def step(unit, has, later):
                    if has(1, units):
                        u = unit(1)
                        for q in range(2):
                            act.wait_ge(turned, 2 * u.n + q + 1)
                            if q == 0 and later(1, 2):
                                act.wait_ge(up_done, 4 * (u - 1))
                            act.activation(x1[:, u.parity, q], xt_ps[:, q, 0:PT], ACT.Copy).then_inc(x1_done, 1)
                    if has(0, units):
                        u = unit(0)
                        if later(0, 2):
                            act.wait_ge(ln1.squares_summed, u - 1)
                        ln1.square(act, u)
                    if has(2, units):
                        u = unit(2)
                        if later(2, 2):
                            act.wait_ge(ln2.squares_summed, u - 1)
                        ln2.square(act, u)
                    if has(1, units):
                        u = unit(1)
                        for q in range(2):
                            for f in range(2):
                                act.wait_ge(up_done, 4 * u.n + 2 * q + f + 1)
                                if later(1, 1):
                                    act.wait_ge(down_done, 2 * u.n + q - 1)
                                act.activation(hidden[:, q, f], h_ps[:, 2 * q + f, 0:PT], ACT.Gelu,
                                               bias=g.ffn_b1[:, l, f:f + 1], scale=1.0 / WS).then_inc(gelu_done, 1)
                            if q == 1:
                                out_y(act, u, 0, later)
                        out_y(act, u, 1, later)

                def out_y(act, u, q, later):
                    act.wait_ge(down_done, 2 * u.n + q + 1)
                    if later(1, 1):
                        act.wait_ge(back_done, 2 * u.n + q - 1)
                    act.activation(y[:, q], y_ps[:, 0:PT], ACT.Identity, bias=g.y_bias[:, l:l + 1]).then_inc(y_done, 1)

                run_steps(act, units + 2, 4, units, step, start)

            @block.tensor
            def _(pe):
                def step(unit, has, later):
                    if not has(1, units):
                        return
                    u = unit(1)
                    pe.wait_ge(base_done, u + 1)
                    for q in range(2):
                        if later(1, 1):
                            pe.wait_ge(*((x2_done, 2 * u.n - 1), (both_done, 2 * u.n))[q])
                        for j in range(PAIR):
                            mm = turn_twice(pe, xt_ps[:, q, j * T:(j + 1) * T], base[:, u.parity, q * PAIR + j, :], g)
                        mm.then_inc(turned, 1)

                    def up(q):
                        pe.wait_ge(x2_done, 2 * u.n + q + 1)
                        if later(1, 1):
                            pe.wait_ge(gelu_done, 4 * u.n + 2 * q - 2)
                        for f in range(2):
                            w = g.ffn_w1[:, l, f * 128:(f + 1) * 128]
                            out = h_ps[:, 2 * q + f, 0:PT]
                            pe.matmul(out, w, x1[:, u.parity, q], start=True, stop=False)
                            pe.matmul(out, w, x2[:, u.parity, q], start=False, stop=True).then_inc(up_done, 1)

                    def down(q):
                        pe.wait_ge(gelu_done, 4 * u.n + 2 * q + 2)
                        if q == 1:
                            pe.wait_ge(y_done, 2 * u.n + 1)
                        elif later(1, 1):
                            pe.wait_ge(y_done, 2 * u.n)
                        for f in range(2):
                            mm = pe.matmul(y_ps[f * C:(f + 1) * C, 0:PT], g.ffn_w2[:, l, f, :], hidden[:, q, f],
                                           start=True, stop=True)
                        mm.then_inc(down_done, 1)

                    def back(q):
                        pe.wait_ge(y_done, 2 * u.n + q + 1)
                        if q == 0 and later(1, 1):
                            pe.wait_ge(both_done, 2 * u.n - 1)
                        for j in range(PAIR):
                            mm = pe.transpose(backs[q][:, j, :], y[:, q, j * T:(j + 1) * T], g.ident[:])
                        mm.then_inc(back_done, 1)

                    up(0)
                    up(1)
                    down(0)
                    down(1)
                    back(0)
                    back(1)

                run_steps(pe, units + 2, 4, units, step, start)


def attention(nc, g, d):
    units = NT // PAIR
    with ExitStack() as ctx:
        def sb(n, shape, dt=F32):
            return ctx.enter_context(nc.sbuf_tensor(f"a_{n}", shape, dt))

        def ps(n, shape):
            return ctx.enter_context(nc.psum_tensor(f"a_{n}", shape, F32))

        def sem(n):
            return ctx.enter_context(nc.semaphore(f"a_{n}"))

        xn = sb("xn", [T, 2, PAIR, C])
        x1, x2 = sb("x1", [2 * C, 2, PT], F16), sb("x2", [2 * C, 2, PT], F16)
        gs = sb("gs", [2 * C, 2, NH, PT], F16)
        v = sb("v", [T, 2, PAIR, NH * DH])
        block_max = sb("block_max", [T, 2, NH, 3])
        row_max = sb("row_max", [T, 96])
        max_rows = sb("max_rows", [48, 2, T], BF16)
        probs = sb("probs", [T, 4, 3 * T])
        log_sum, inv_sum = sb("log_sum", [128, 2, S]), sb("inv_sum", [128, 2, S])
        heads_out = sb("heads_out", [128, 2, PT])
        y = sb("y", [128, PT])
        top = sb("top", [T, PAIR, C])
        proj = ps("proj", [128, 2, 512])
        max_ps = ps("max_ps", [T, 2, 512])
        score_ps = ps("score_ps", [T, 2, 512])
        pv_ps = ps("pv_ps", [128, 2, 512])
        back_ps = proj[0:T, 0, :].rearrange("p (j c) -> p j c", j=PAIR)
        ln = LayerNorm(nc, ctx, "a_ln", PAIR, 1e-5)
        set_up = sem("set_up")
        turned, x1_done, x2_done = sem("turned"), sem("x1_done"), sem("x2_done")
        g_full, g_high, g_low = sem("g_full"), sem("g_high"), sem("g_low")
        v_full, v_done = sem("v_full"), sem("v_done")
        max_full, max_done, row_max_done = sem("max_full"), sem("max_done"), sem("row_max_done")
        max_turned, max_rows_done = sem("max_turned"), sem("max_rows_done")
        max_in = [sem("max_in0"), sem("max_in1")]
        score_full, probs_done, pv_full = sem("score_full"), sem("probs_done"), sem("pv_full")
        log_done, inv_done, heads_done = sem("log_done"), sem("inv_done"), sem("heads_done")
        y_full, y_done, back_full, top_done, stored = (
            sem("y_full"), sem("y_done"), sem("back_full"), sem("top_done"), sem("stored"))
        slots = 27

        def of(b, k=0):
            return slice(b * S + k * T, b * S + (k + 1) * T)

        def both(b):
            return slice(b * S, (b + 1) * S)

        with nc.Block() as block:
            @block.gpsimd
            def _(pool):
                ln.setup(pool, set_up)
                pool.memset(row_max[:], 0.0).then_inc(set_up, 1)
                pool.wait_ge(set_up, 3)

                def step(unit, has, later):
                    if has(0, units):
                        ln.root(pool, unit(0))

                run_steps(pool, units + 2, 4, units, step)

            @block.sync
            def _(sp):
                def step(unit, has, later):
                    if not has(1, units):
                        return
                    a = unit(1)
                    sp.wait_ge(max_rows_done, a + 1)
                    if later(1, 2):
                        sp.wait_ge(score_full, 16 * (a - 1))
                    sp.dma_start(g.table_cols[T:T + 1, a.parity].rearrange("p b h (k t) -> p (b h k) t", t=T),
                                 max_rows[:, a.parity, :]).then_inc(max_in[a.parity], 16)

                run_steps(sp, units + 2, 4, units, step)

            @block.scalar
            def _(act):
                act.preload_act_table_set("natural_log_exp_and_others")

                def step(unit, has, later):
                    a, b = unit(1), unit(2)
                    for s in range(slots):
                        if s == 1 and has(1, units):
                            act.wait_ge(turned, a + 1)
                            if later(1, 2):
                                act.wait_ge(score_full, 16 * (a - 1))
                            act.activation(x1[:, a.parity], proj[:, 0, 0:PT], ACT.Copy).then_inc(x1_done, 1)
                        if s == 6 and has(0, units):
                            if later(0, 2):
                                act.wait_ge(ln.squares_summed, unit(0) - 1)
                            ln.square(act, unit(0))
                        if s % 2 == 0 and 2 <= s <= 16 and has(1, units):
                            h = (s - 2) // 2
                            act.wait_ge(g_full, 8 * a.n + h + 1)
                            act.activation(gs[:, a.parity, h], proj[:, h % 2, 0:PT], ACT.Copy, scale=1.0 / WS)\
                               .then_inc(g_high, 1)
                        if s in (5, 7) and has(1, units):
                            k = (s - 5) // 2
                            act.wait_ge(v_full, 2 * a.n + k + 1)
                            if k == 0 and later(1, 2):
                                act.wait_ge(pv_full, 16 * (a - 1))
                            act.activation(v[:, a.parity, 2 * k:2 * k + 2, :],
                                           proj[0:T, k, :].rearrange("p (j n) -> p j n", j=2),
                                           ACT.Copy, scale=1.0 / WS).then_inc(v_done, 1)
                        if 5 <= s <= 20 and has(2, units):
                            i = s - 5
                            act.wait_ge(score_full, 16 * b.n + i + 1)
                            if i >= 4 or later(2, 1):
                                act.wait_ge(pv_full, 16 * b.n + i - 3)
                            act.activation(probs[:, i % 4, :], score_ps[:, i % 2, 0:3 * T], ACT.Exp).then_inc(probs_done, 1)
                        if s in (11, 15, 19, 23) and has(2, units):
                            q = (s - 11) // 4
                            act.wait_ge(pv_full, 16 * b.n + 4 * q + 4)
                            if q or later(2, 1):
                                act.wait_ge(inv_done, 4 * b.n + q)
                            act.activation(log_sum[:, q % 2], pv_ps[:, q % 2, S:2 * S], ACT.Ln).then_inc(log_done, 1)
                            act.wait_ge(log_done, 4 * b.n + q + 1)
                            if q >= 2 or later(2, 1):
                                act.wait_ge(heads_done, 4 * b.n + q - 1)
                            act.activation(inv_sum[:, q % 2], log_sum[:, q % 2], ACT.Exp, scale=-1.0).then_inc(inv_done, 1)
                        if s == 22 and has(1, units):
                            act.wait_ge(max_turned, a + 1)
                            if later(1, 2):
                                act.wait_ge(max_in[a.parity], 16 * a.half)
                            act.activation(max_rows[:, a.parity, :], max_ps[0:48, 0, 0:T], ACT.Copy, scale=-1.0)\
                               .then_inc(max_rows_done, 1)
                        if s == 25 and has(2, units):
                            act.wait_ge(y_full, b + 1)
                            if later(2, 1):
                                act.wait_ge(back_full, b.n)
                            act.activation(y[:], proj[:, 1, 0:PT], ACT.Identity, bias=g.y_bias[:, 2:3]).then_inc(y_done, 1)

                run_steps(act, units + 2, 4, units, step)

            @block.vector
            def _(dve):
                def step(unit, has, later):
                    n, a, b = unit(0), unit(1), unit(2)
                    for s in range(slots):
                        if s == 1 and has(1, units):
                            dve.wait_ge(x1_done, a + 1)
                            dve.tensor_tensor(x2[:, a.parity], proj[:, 0, 0:PT], x1[:, a.parity], ALU.subtract)\
                               .then_inc(x2_done, 1)
                        if s == 1 and has(0, units):
                            ln.center(dve, n, of_tiles(g.x, n, PAIR), later(0, 2))
                        if s == 8 and has(0, units):
                            ln.sum_squares(dve, n)
                        if s == 16 and has(0, units):
                            if later(0, 2):
                                dve.wait_ge(turned, n - 1)
                            ln.scale(dve, n, xn[:, n.parity])
                        if s % 2 == 0 and 2 <= s <= 16 and has(1, units):
                            h = (s - 2) // 2
                            dve.wait_ge(g_high, 8 * a.n + h + 1)
                            low = gs[C:2 * C, a.parity, h]
                            dve.scalar_tensor_tensor(out=low, in0=proj[C:2 * C, h % 2, 0:PT], scalar=1.0 / WS, in1=low,
                                                     op0=ALU.mult, op1=ALU.subtract).then_inc(g_low, 1)
                        if 4 <= s <= 19 and has(1, units):
                            m = s - 4
                            dve.wait_ge(max_full, 16 * a.n + m + 1)
                            if m == 0 and later(1, 1):
                                dve.wait_ge(row_max_done, 2 * a.n)
                            dve.tensor_reduce(block_max[:, m % 2, m // 2, :],
                                              max_ps[:, m % 2, 0:3 * T].rearrange("p (k t) -> p k t", k=3),
                                              AX.X, ALU.max).then_inc(max_done, 1)
                        if s == 20 and has(1, units):
                            dve.wait_ge(max_done, 16 * a.n + 16)
                            if later(1, 1):
                                dve.wait_ge(max_turned, a.n)
                            rows = row_max[:, 0:48].rearrange("p (b h k) -> p b h k", b=2, h=NH)
                            dve.tensor_copy(rows[:, :, :, 0], block_max[:, :, :, 0]).then_inc(row_max_done, 1)
                            dve.tensor_tensor(rows[:, :, :, 1:3], bcast(block_max[:, :, :, 1:2], [T, 2, NH, 2]),
                                              bcast(block_max[:, :, :, 2:3], [T, 2, NH, 2]), ALU.max)\
                               .then_inc(row_max_done, 1)
                        if s in (12, 16, 20, 24) and has(2, units):
                            q = (s - 12) // 4
                            dve.wait_ge(inv_done, 4 * b.n + q + 1)
                            if q == 0 and later(2, 1):
                                dve.wait_ge(y_full, b.n)
                            dve.tensor_tensor(heads_out[:, q % 2, both(q // 2)], pv_ps[:, q % 2, 0:S], inv_sum[:, q % 2],
                                              ALU.mult).then_inc(heads_done, 1)
                        if s == 26 and has(2, units):
                            dve.wait_ge(back_full, b + 1)
                            if later(2, 1):
                                dve.wait_ge(stored, b.n)
                            x = of_tiles(g.x, b, PAIR)
                            dve.tensor_tensor(top[:], back_ps[:, :, 0:C], x, ALU.add).then_inc(top_done, 1)
                            dve.wait_ge(top_done, b + 1)
                            dve.tensor_tensor(x, back_ps[:, :, C:2 * C], top[:], ALU.add).then_inc(stored, 1)

                run_steps(dve, units + 2, 4, units, step)

            @block.tensor
            def _(pe):
                def step(unit, has, later):
                    a, b = unit(1), unit(2)

                    def turn():
                        pe.wait_ge(ln.done, a + 1)
                        if later(1, 2):
                            pe.wait_ge(stored, a - 1)
                        for j in range(PAIR):
                            mm = turn_twice(pe, proj[:, 0, j * T:(j + 1) * T], xn[:, a.parity, j, :], g)
                        mm.then_inc(turned, 1)

                    def project(h):
                        if h == 0:
                            pe.wait_ge(x2_done, a + 1)
                        elif h == 1 and later(1, 2):
                            pe.wait_ge(y_done, a - 1)
                        elif h in (2, 3):
                            pe.wait_ge(v_done, 2 * a.n + h - 1)
                        elif h > 3:
                            pe.wait_ge(g_low, 8 * a.n + h - 1)
                        for part, x in enumerate((x1, x2)):
                            mm = pe.matmul(proj[:, h % 2, 0:PT], g.w_a[:, h, :], x[:, a.parity], start=(part == 0),
                                           stop=(part == 1))
                        mm.then_inc(g_full, 1)

                    def values(k):
                        pe.wait_ge(g_low, 8 * a.n + k + 1)
                        for j in range(2):
                            for part, x in enumerate((x1, x2)):
                                mm = pe.matmul(proj[0:T, k, j * 256:(j + 1) * 256], x[:, a.parity, of(k, j)], g.w_v[:],
                                               start=(part == 0), stop=(part == 1))
                        mm.then_inc(v_full, 1)

                    def query_rows(m):
                        h, q = m // 2, m % 2
                        pe.wait_ge(g_low, 8 * a.n + h + 1)
                        if m >= 2:
                            pe.wait_ge(max_done, 16 * a.n + m - 1)
                        elif later(1, 1):
                            if m == 0:
                                pe.wait_ge(max_rows_done, a.n)
                            else:
                                pe.wait_ge(max_done, 16 * a.n)
                        out = max_ps[:, m % 2, 0:3 * T]
                        pe.matmul(out, g.ident_ones[0:T, :], g.table_rows[:, h, :], start=True, stop=False)
                        pe.matmul(out[:, 0:T], gs[:, a.parity, h, of(q, 0)], x1[:, a.parity, of(q, 0)],
                                  start=False, stop=False)
                        pe.matmul(out[:, T:3 * T], gs[:, a.parity, h, of(q, 1)], x1[:, a.parity, both(q)],
                                  start=False, stop=True).then_inc(max_full, 1)

                    def turn_maxima():
                        pe.wait_ge(row_max_done, 2 * a.n + 2)
                        pe.transpose(max_ps[0:96, 0, 0:T], row_max[:], g.ident[0:T, 0:T]).then_inc(max_turned, 1)

                    def key_rows(i):
                        h, q = i % NH, i // NH
                        if i == 0:
                            pe.wait_ge(max_in[b.parity], 16 * b.half + 16)
                        if i >= 2 or later(2, 1):
                            pe.wait_ge(probs_done, 16 * b.n + i - 1)
                        out = score_ps[:, i % 2, 0:3 * T]
                        pe.matmul(out, g.ident_ones[:], g.table_cols[:, b.parity, q, h, :], start=True, stop=False)
                        for part, x in enumerate((x1, x2)):
                            pe.matmul(out[:, 0:S], x[:, b.parity, of(q, 0)], gs[:, b.parity, h, both(q)],
                                      start=False, stop=False)
                            mm = pe.matmul(out[:, S:3 * T], x[:, b.parity, of(q, 1)], gs[:, b.parity, h, of(q, 1)],
                                           start=False, stop=(part == 1))
                        mm.then_inc(score_full, 1)

                    def weigh(i):
                        h, q = i % NH, i // NH
                        group, j = i // 4, i % 4
                        pe.wait_ge(probs_done, 16 * b.n + i + 1)
                        if j == 0 and (group >= 2 or later(2, 1)):
                            pe.wait_ge(heads_done, 4 * b.n + group - 1)
                        out = pv_ps[32 * j:32 * j + 32, group % 2, :]
                        for k in range(2):
                            p = probs[:, i % 4, 0:S] if k == 0 else probs[:, i % 4, S:3 * T]
                            for first, w in enumerate((v[:, b.parity, 2 * q + k, h * DH:(h + 1) * DH], g.ones[:])):
                                mm = pe.matmul(out[:, first * S + k * T:(first + 1) * S], w, p,
                                               start=(k == 0 and first == 0), stop=(k == 1), skip_group_check=True)
                        mm.then_inc(pv_full, 1)

                    def out_project():
                        pe.wait_ge(heads_done, 4 * b.n + 4)
                        if has(1, units):
                            pe.wait_ge(g_low, 8 * a.n + 8)
                        for half in range(2):
                            mm = pe.matmul(proj[half * C:(half + 1) * C, 1, 0:PT], g.w_o[:, half, :], heads_out[:, half, :],
                                           start=True, stop=True)
                        mm.then_inc(y_full, 1)

                    def turn_back():
                        pe.wait_ge(y_done, b + 1)
                        for j in range(PAIR):
                            mm = pe.transpose(back_ps[:, j, :], y[:, j * T:(j + 1) * T], g.ident[:])
                        mm.then_inc(back_full, 1)

                    for s in range(slots):
                        if has(1, units):
                            if s == 0:
                                turn()
                            if s % 2 == 0 and 2 <= s <= 16:
                                project((s - 2) // 2)
                            if s in (5, 7):
                                values((s - 5) // 2)
                            if 4 <= s <= 19:
                                query_rows(s - 4)
                        if has(2, units):
                            if 5 <= s <= 20:
                                key_rows(s - 5)
                            if 7 <= s <= 22:
                                weigh(s - 7)
                        if s == 22 and has(1, units):
                            turn_maxima()
                        if has(2, units):
                            if s == 25:
                                out_project()
                                turn_back()

                run_steps(pe, units + 2, 4, units, step)


def experts(nc, g, d, out):
    units = NT // PAIR
    with ExitStack() as ctx:
        def sb(n, shape, dt=F32):
            return ctx.enter_context(nc.sbuf_tensor(f"m_{n}", shape, dt))

        def ps(n, shape):
            return ctx.enter_context(nc.psum_tensor(f"m_{n}", shape, F32))

        def sem(n):
            return ctx.enter_context(nc.semaphore(f"m_{n}"))

        xn = sb("xn", [T, 2, PAIR, C])
        x1, x2 = sb("x1", [2 * C, 2, PT], F16), sb("x2", [2 * C, 2, PT], F16)
        logits = sb("logits", [T, PAIR, NE])
        best, best_at = sb("best", [T, PAIR, 8]), sb("best_at", [T, PAIR, 8], U32)
        at = sb("at", [T, PAIR, 2])
        behind, odds, total = sb("behind", [T, PAIR]), sb("odds", [T, PAIR]), sb("total", [T, PAIR])
        share = sb("share", [T, PAIR, 2])
        chosen = sb("chosen", [T, 2, PAIR, NE])
        part = sb("part", [T, 2, PAIR, NE])
        gates = sb("gates", [T, PAIR, 6, NE])
        gate_rows = sb("gate_rows", [96, 2, PT], F16)
        hidden, weighted = sb("hidden", [FE, 2, PT]), sb("weighted", [FE, 4, PT])
        y = sb("y", [128, PT])
        top, both = sb("top", [T, PAIR, C]), sb("both", [T, 2, PAIR, C])
        scaled, by_gamma, plus_beta = sb("scaled", [T, PAIR, C]), sb("by_gamma", [T, PAIR, C]), sb("plus_beta", [T, PAIR, C])
        result = sb("result", [T, 2, PAIR, C])
        h_ps, gate_bc = ps("h", [128, 2, 512]), ps("gate_bc", [128, 2, 512])
        y_ps, xt_ps = ps("y_ps", [128, 512]), ps("xt_ps", [128, 512])
        gate_ps, back_ps = ps("gate_ps", [128, 512]), ps("back_ps", [T, PAIR, 2 * C])
        ln1, ln2 = LayerNorm(nc, ctx, "m_ln", PAIR, 1e-5), LayerNorm(nc, ctx, "m_out_ln", PAIR, 1e-5)
        set_up = sem("set_up")
        turned, x1_done, x2_done = sem("turned"), sem("x1_done"), sem("x2_done")
        logits_full, logits_done, best_done, best_at_done = (
            sem("logits_full"), sem("logits_done"), sem("best_done"), sem("best_at_done"))
        at_done, behind_done, odds_done, total_done, share_done = (
            sem("at_done"), sem("behind_done"), sem("odds_done"), sem("total_done"), sem("share_done"))
        chosen_done, part_done, gates_done = sem("chosen_done"), sem("part_done"), sem("gates_done")
        gates_turned, gates_high, gates_low = sem("gates_turned"), sem("gates_high"), sem("gates_low")
        up_full, relu_done, weighted_done, down_done = (
            sem("up_full"), sem("relu_done"), sem("weighted_done"), sem("down_done"))
        y_done, back_full, top_done, both_done = sem("y_done"), sem("back_full"), sem("top_done"), sem("both_done")
        by_gamma_done, plus_beta_done, result_done = sem("by_gamma_done"), sem("plus_beta_done"), sem("result_done")
        stored = [sem("stored0"), sem("stored1")]
        slots = 22
        out_rows = out.rearrange("b (k p) c -> p (b k) c", p=T)

        with nc.Block() as block:
            @block.gpsimd
            def _(pool):
                ln1.setup(pool, set_up)
                ln2.setup(pool, set_up)
                pool.wait_ge(set_up, 4)

                def step(unit, has, later):
                    if has(3, units):
                        c = unit(3)
                        ln2.root(pool, c)
                        pool.wait_ge(ln2.done, c + 1)
                        if later(3, 1):
                            pool.wait_ge(plus_beta_done, c.n)
                        pool.tensor_tensor(by_gamma[:], scaled[:], per_channel(g.rows[:, 10, :], PAIR), ALU.mult)\
                            .then_inc(by_gamma_done, 1)
                        pool.wait_ge(by_gamma_done, c + 1)
                        if later(3, 1):
                            pool.wait_ge(result_done, c.n)
                        pool.tensor_tensor(plus_beta[:], by_gamma[:], per_channel(g.rows[:, 11, :], PAIR), ALU.add)\
                            .then_inc(plus_beta_done, 1)
                        pool.wait_ge(plus_beta_done, c + 1)
                        if later(3, 2):
                            pool.wait_ge(stored[c.parity], 16 * c.half)
                        pool.tensor_tensor(result[:, c.parity], plus_beta[:], of_tiles(g.x, c, PAIR), ALU.add)\
                            .then_inc(result_done, 1)
                    if has(0, units):
                        ln1.root(pool, unit(0))

                run_steps(pool, units + 3, 6, units, step)

            @block.sync
            def _(sp):
                def step(unit, has, later):
                    if has(3, units):
                        c = unit(3)
                        sp.wait_ge(result_done, c + 1)
                        sp.dma_start(out_rows[:, bass.ds(c.n * PAIR, PAIR), :], result[:, c.parity])\
                          .then_inc(stored[c.parity], 16)

                run_steps(sp, units + 3, 6, units, step)
                for s in stored:
                    sp.wait_ge(s, 16 * (units // 2))

            @block.scalar
            def _(act):
                def step(unit, has, later):
                    n, a, b, c = unit(0), unit(1), unit(2), unit(3)
                    for s in range(slots):
                        if s < NE and has(2, units):
                            act.wait_ge(up_full, NE * b.n + s + 1)
                            if s >= 2 or later(2, 1):
                                act.wait_ge(weighted_done, NE * b.n + s - 1)
                            act.activation(hidden[:, s % 2], h_ps[:, s % 2, 0:PT], ACT.Relu, bias=g.moe_b1[:, s:s + 1],
                                           scale=1.0 / WS).then_inc(relu_done, 1)
                        if s == 2 and has(1, units):
                            act.wait_ge(turned, a + 1)
                            if later(1, 2):
                                act.wait_ge(down_done, NE * (a - 1))
                            act.activation(x1[:, a.parity], xt_ps[:, 0:PT], ACT.Copy).then_inc(x1_done, 1)
                        if s == 5 and has(0, units):
                            if later(0, 2):
                                act.wait_ge(ln1.squares_summed, n - 1)
                            ln1.square(act, n)
                        if s == 4 and has(3, units):
                            if later(3, 2):
                                act.wait_ge(ln2.squares_summed, c - 1)
                            ln2.square(act, c)
                        if s == 9 and has(1, units):
                            act.wait_ge(behind_done, a + 1)
                            if later(1, 1):
                                act.wait_ge(share_done, 2 * a.n)
                            act.activation(odds[:], behind[:], ACT.Exp).then_inc(odds_done, 1)
                        if s == 18 and has(1, units):
                            act.wait_ge(gates_turned, a + 1)
                            act.activation(gate_rows[:, a.parity], gate_ps[0:96, 0:PT], ACT.Copy).then_inc(gates_high, 1)
                        if s == 19 and has(2, units):
                            act.wait_ge(down_done, NE * b.n + NE)
                            if later(2, 1):
                                act.wait_ge(back_full, b.n)
                            act.activation(y[:], y_ps[:, 0:PT], ACT.Copy).then_inc(y_done, 1)

                run_steps(act, units + 3, 6, units, step)

            @block.vector
            def _(dve):
                def step(unit, has, later):
                    n, a, b, c = unit(0), unit(1), unit(2), unit(3)
                    for s in range(slots):
                        if s == 0 and has(3, units):
                            dve.wait_ge(both_done, c + 1)
                            ln2.center(dve, c, both[:, c.parity], later(3, 2))
                        if s == 1 and has(0, units):
                            ln1.center(dve, n, of_tiles(g.x, n, PAIR), later(0, 2))
                        if 1 <= s <= NE and has(2, units):
                            e = s - 1
                            dve.wait_ge(relu_done, NE * b.n + e + 1)
                            if e >= 4 or later(2, 1):
                                dve.wait_ge(down_done, NE * b.n + e - 3)
                            dve.tensor_tensor(weighted[:, e % 4], gate_bc[:, e % 2, 0:PT], hidden[:, e % 2], ALU.mult)\
                               .then_inc(weighted_done, 1)
                        if s == 3 and has(1, units):
                            dve.wait_ge(x1_done, a + 1)
                            dve.tensor_tensor(x2[:, a.parity], xt_ps[:, 0:PT], x1[:, a.parity], ALU.subtract)\
                               .then_inc(x2_done, 1)
                        if s == 5 and has(3, units):
                            ln2.sum_squares(dve, c)
                        if s == 6 and has(1, units):
                            dve.wait_ge(logits_full, a + 1)
                            if later(1, 1):
                                dve.wait_ge(best_at_done, 4 * a.n)
                            dve.scalar_tensor_tensor(
                                out=logits[:], in0=gate_ps[0:T, 0:PAIR * NE].rearrange("p (j e) -> p j e", j=PAIR),
                                scalar=1.0 / WS, in1=per_channel(g.gate_b[:], PAIR, NE), op0=ALU.mult, op1=ALU.add)\
                               .then_inc(logits_done, 1)
                        if s == 8:
                            if has(1, units):
                                dve.wait_ge(logits_done, a + 1)
                            if has(0, units):
                                ln1.sum_squares(dve, n)
                            if has(1, units):
                                for j in range(PAIR):
                                    dve.max(best[:, j, :], logits[:, j, :]).then_inc(best_done, 1)
                        if s == 9:
                            if has(1, units):
                                dve.wait_ge(best_done, 4 * a.n + 4)
                            if has(3, units):
                                if later(3, 1):
                                    dve.wait_ge(by_gamma_done, c.n)
                                ln2.scale(dve, c, scaled[:])
                            if has(1, units):
                                for j in range(PAIR):
                                    dve.max_index(best_at[:, j, :], best[:, j, :], logits[:, j, :])\
                                       .then_inc(best_at_done, 1)
                                dve.tensor_tensor(behind[:], best[:, :, 1], best[:, :, 0], ALU.subtract)\
                                   .then_inc(behind_done, 1)
                        if s == 11 and has(1, units):
                            dve.wait_ge(best_at_done, 4 * a.n + 4)
                            dve.tensor_copy(at[:], best_at[:, :, 0:2]).then_inc(at_done, 1)
                            dve.wait_ge(odds_done, a + 1)
                            dve.tensor_scalar(total[:], odds[:], 1.0, None, ALU.add).then_inc(total_done, 1)
                            dve.wait_ge(at_done, a + 1)
                            for k in range(2):
                                dve.tensor_tensor(chosen[:, k], per_channel(g.iota[:], PAIR, NE),
                                                  bcast(at[:, :, k:k + 1], [T, PAIR, NE]), ALU.is_equal)\
                                   .then_inc(chosen_done, 1)
                        if s == 12 and has(1, units):
                            dve.wait_ge(total_done, a + 1)
                            dve.reciprocal(share[:, :, 0], total[:]).then_inc(share_done, 1)
                            dve.wait_ge(share_done, 2 * a.n + 1)
                            dve.tensor_tensor(share[:, :, 1], share[:, :, 0], odds[:], ALU.mult).then_inc(share_done, 1)
                        if s == 13 and has(1, units):
                            dve.wait_ge(share_done, 2 * a.n + 2)
                            dve.wait_ge(chosen_done, 2 * a.n + 2)
                            for k in range(2):
                                dve.tensor_tensor(part[:, k], chosen[:, k], bcast(share[:, :, k:k + 1], [T, PAIR, NE]),
                                                  ALU.mult).then_inc(part_done, 1)
                        if s == 14 and has(1, units):
                            dve.wait_ge(part_done, 2 * a.n + 2)
                            if later(1, 1):
                                dve.wait_ge(gates_turned, a.n)
                            six = [T, PAIR, 6, NE]
                            dve.tensor_tensor(gates[:], bcast(part[:, 0].unsqueeze(2), six),
                                              bcast(part[:, 1].unsqueeze(2), six), ALU.add).then_inc(gates_done, 1)
                        if s == 18 and has(1, units):
                            dve.wait_ge(gates_high, a + 1)
                            low = gate_rows[32:64, a.parity]
                            dve.tensor_tensor(low, gate_ps[32:64, 0:PT], low, ALU.subtract).then_inc(gates_low, 1)
                        if s == 20 and has(2, units):
                            dve.wait_ge(back_full, b + 1)
                            if later(2, 1):
                                dve.wait_ge(both_done, b.n)
                            if later(2, 2):
                                dve.wait_ge(ln2.centred, b - 1)
                            dve.tensor_tensor(top[:], back_ps[:, :, 0:C], xn[:, b.parity], ALU.add).then_inc(top_done, 1)
                            dve.wait_ge(top_done, b + 1)
                            dve.tensor_tensor(both[:, b.parity], back_ps[:, :, C:2 * C], top[:], ALU.add)\
                               .then_inc(both_done, 1)
                        if s == 21 and has(0, units):
                            if later(0, 2):
                                dve.wait_ge(top_done, n - 1)
                            ln1.scale(dve, n, xn[:, n.parity])

                run_steps(dve, units + 3, 6, units, step)

            @block.tensor
            def _(pe):
                def step(unit, has, later):
                    a, b = unit(1), unit(2)

                    def turn():
                        pe.wait_ge(ln1.done, a + 1)
                        if later(1, 1):
                            pe.wait_ge(x2_done, a.n)
                        for j in range(PAIR):
                            mm = turn_twice(pe, xt_ps[:, j * T:(j + 1) * T], xn[:, a.parity, j, :], g)
                        mm.then_inc(turned, 1)

                    def gate():
                        pe.wait_ge(x2_done, a + 1)
                        if later(1, 1):
                            pe.wait_ge(gates_low, a.n)
                        for j in range(PAIR):
                            for k, x in enumerate((x1, x2)):
                                mm = pe.matmul(gate_ps[0:T, j * NE:(j + 1) * NE], x[:, a.parity, j * T:(j + 1) * T],
                                               g.w_gate[:], start=(k == 0), stop=(k == 1))
                        mm.then_inc(logits_full, 1)

                    def turn_gates():
                        pe.wait_ge(gates_done, a + 1)
                        for j in range(PAIR):
                            mm = pe.transpose(gate_ps[0:96, j * T:(j + 1) * T],
                                              gates[:, j].rearrange("p k e -> p (k e)"), g.ident[0:T, 0:T])
                        mm.then_inc(gates_turned, 1)

                    def up(e):
                        if e == 0:
                            pe.wait_ge(gates_low, b + 1)
                        if e >= 2 or later(2, 1):
                            pe.wait_ge(weighted_done, NE * b.n + e - 1)
                        for k, x in enumerate((x1, x2)):
                            pe.matmul(h_ps[:, e % 2, 0:PT], g.moe_w1[:, e, :], x[:, b.parity], start=(k == 0), stop=(k == 1))
                        pe.matmul(gate_bc[:, e % 2, 0:PT], g.selector[:, e, :], gate_rows[:, b.parity],
                                  start=True, stop=True).then_inc(up_full, 1)

                    def down(e):
                        half = e % 2
                        out = y_ps[half * C:(half + 1) * C, 0:PT]
                        if e == 0:
                            if later(2, 1):
                                pe.wait_ge(y_done, b.n)
                            pe.matmul(out, g.moe_b2[:], gate_rows[:, b.parity], start=True, stop=False)
                        pe.wait_ge(weighted_done, NE * b.n + e + 1)
                        pe.matmul(out, g.moe_w2[:, e, :], weighted[:, e % 4], start=(e == 1), stop=(e >= NE - 2))\
                          .then_inc(down_done, 1)

                    def turn_back():
                        pe.wait_ge(y_done, b + 1)
                        if later(2, 1):
                            pe.wait_ge(both_done, b.n)
                        for j in range(PAIR):
                            mm = pe.transpose(back_ps[:, j, :], y[:, j * T:(j + 1) * T], g.ident[:])
                        mm.then_inc(back_full, 1)

                    for s in range(slots):
                        if s < NE and has(2, units):
                            up(s)
                        if s == 1 and has(1, units):
                            turn()
                        if s == 5 and has(1, units):
                            gate()
                        if 2 <= s < NE + 2 and has(2, units):
                            down(s - 2)
                        if s == 17 and has(1, units):
                            turn_gates()
                        if s == 20 and has(2, units):
                            turn_back()

                run_steps(pe, units + 3, 6, units, step)


_LOADS = {
    "item_emb": "L0_tok_item_emb", "pos_emb": "L0_tok_pos_emb", "ln0_w": "L0_tok_ln0_w", "ln0_b": "L0_tok_ln0_b",
    "fln_w": "L0_tok_fln_w", "fln_b": "L0_tok_fln_b", "d1_w": "L0_tok_d1_w",
    "d1_b": "L0_tok_d1_b", "d2_w": "L0_tok_d2_w", "d2_b": "L0_tok_d2_b", "iln_w": "L0_tok_iln_w",
    "iln_b": "L0_tok_iln_b", "Wq": "L0_attn_Wq", "Wk": "L0_attn_Wk", "Wv": "L0_attn_Wv", "Wo": "L0_attn_Wo",
    "bo": "L0_attn_bo", "gate_w": "L0_ffn_gate_w", "gate_b": "L0_ffn_gate_b", "w1": "L0_ffn_w1", "b1": "L0_ffn_b1",
    "w2": "L0_ffn_w2", "b2": "L0_ffn_b2", "gamma": "L0_ffn_gamma", "beta": "L0_ffn_beta",
}


class Names:
    pass


def build(nc, d, out):
    with ExitStack() as ctx:
        def sb(n, shape, dt=F32):
            return ctx.enter_context(nc.sbuf_tensor(n, shape, dt))

        g = Names()
        g.ctx, g.ffn_sems = ctx, {}
        g.x = sb("x_stream", [T, NT, C])
        g.ids = sb("ids_sb", [T, NT], I32)
        g.ident = sb("ident_sb", [128, 128])
        g.ident_ones = sb("ident_ones_sb", [T + 1, T], BF16)
        g.ones = sb("ones_sb", [T, DH])
        g.pos = sb("pos_sb", [T, 2, C])
        g.rows = sb("rows_sb", [T, 12, C])
        g.iota = sb("iota_sb", [T, NE])
        g.parity = sb("parity_sb", [C, 2])
        g.gate_b = sb("gate_b_sb", [T, NE])
        g.table_rows = sb("table_rows_sb", [T, NH, 3 * T], BF16)
        g.table_cols = sb("table_cols_sb", [T + 1, 2, 2, NH, 3 * T], BF16)
        g.selector = sb("selector_sb", [96, NE, 128], F16)
        g.ffn_w1 = sb("ffn_w1_sb", [2 * C, 2, DFF], F16)
        g.ffn_b1 = sb("ffn_b1_sb", [128, 2, 2])
        g.ffn_w2 = sb("ffn_w2_sb", [128, 2, 2, C])
        g.y_bias = sb("y_bias_sb", [128, 3])
        g.w_a = sb("w_a_sb", [2 * C, NH, 2 * C], F16)
        g.w_v = sb("w_v_sb", [2 * C, NH * DH], F16)
        g.w_o = sb("w_o_sb", [128, 2, C])
        g.w_gate = sb("w_gate_sb", [2 * C, NE], F16)
        g.moe_w1 = sb("moe_w1_sb", [2 * C, NE, FE], F16)
        g.moe_b1 = sb("moe_b1_sb", [128, NE])
        g.moe_w2 = sb("moe_w2_sb", [128, NE, C])
        g.moe_b2 = sb("moe_b2_sb", [96, C], F16)
        d.filters = nc.dram_tensor("kernels", [2, C, 2 * S], F32, kind="Internal").ap()
        prepare(nc, g, d)
        embed(nc, g, d)
        for l in range(2):
            spectral_filter(nc, g, d, l)
            feed_forward(nc, g, d, l)
        attention(nc, g, d)
        experts(nc, g, d, out)


def shape_constants():
    bf = mybir.dt.np(BF16)
    j, k = np.arange(2 * S)[None, :], np.arange(K)[:, None]
    weight = np.where((k == 0) | (k == S // 2), 1.0, 2.0) / S
    angle = 2 * np.pi * ((k * j) % S) / S
    sine = weight * np.where((k == 0) | (k == S // 2), 0.0, -np.sin(angle))
    dft = np.stack([weight * np.cos(angle), -sine, sine], 1).astype(np.float32)
    slopes = 2.0 ** -(np.arange(NH) + 1.0)
    q, s = np.arange(S)[:, None], np.arange(S)[None, :]
    bias = np.where(s <= q, slopes[:, None, None] * (s - q), NEG)
    table_rows = np.concatenate([bias[:, 0:T, 0:T], bias[:, T:S, 0:T], bias[:, T:S, T:S]], 2).transpose(1, 0, 2)
    keys = bias.transpose(2, 0, 1)
    table_cols = np.concatenate([keys[0:T], keys[T:S, :, T:S]], 2)
    selector = np.zeros((96, NE, 128), np.float16)
    for e in range(NE):
        selector[e, e] = 1
        selector[32 + e, e] = 1
    even = (np.arange(C) // NE) % 2 == 0
    return {
        "dft": dft, "table_rows": table_rows.astype(bf), "table_cols": table_cols.astype(bf), "selector": selector,
        "ident": np.eye(128, dtype=np.float32),
        "ident_ones": np.concatenate([np.eye(T), np.ones((1, T))]).astype(bf),
        "iota": np.tile(np.arange(NE, dtype=np.float32), (T, 1)),
        "parity": np.stack([even, ~even], 1).astype(np.float32),
    }


def kernel(**inputs):
    import concourse.bacc as bacc
    from concourse.bass_utils import run_bass_kernel_spmd

    nc = bacc.Bacc("TRN2", target_bir_lowering=False, num_devices=1)
    arrays = {name: np.ascontiguousarray(inputs[source]) for name, source in _LOADS.items()}
    arrays["ids"] = np.ascontiguousarray(np.asarray(inputs["x"]).reshape(B, 2, T).transpose(2, 0, 1).reshape(T, NT))
    arrays["cw"] = np.ascontiguousarray(np.asarray(inputs["L0_tok_cw"]).transpose(1, 0, 3, 2))
    arrays["d1_b"] = np.ascontiguousarray(arrays["d1_b"].reshape(2, 2, 128).transpose(2, 0, 1))
    arrays["b1"] = np.ascontiguousarray(arrays["b1"].T)
    arrays.update(shape_constants())
    d = Names()
    for name, a in arrays.items():
        d.__dict__[name] = nc.dram_tensor(f"in_{name}", a.shape, mybir.dt.from_np(a.dtype), kind="ExternalInput").ap()
    out = nc.dram_tensor("out", (B, S, C), F32, kind="ExternalOutput").ap()
    build(nc, d, out)
    result = run_bass_kernel_spmd(nc, [{f"in_{name}": a for name, a in arrays.items()}], core_ids=[0])
    return result.results[0]["out"]
```

```python
from contextlib import ExitStack

import numpy as np

import concourse.bass as bass
from concourse import mybir

F32, F16, BF16 = mybir.dt.float32, mybir.dt.float16, mybir.dt.bfloat16
I32, U32 = mybir.dt.int32, mybir.dt.uint32
ALU = mybir.AluOpType
ACT = mybir.ActivationFunctionType
AX = mybir.AxisListType

B, S, C = 128, 200, 64
T = 100
NT = B * S // T
DFF = 256
NH, DH = 8, 32
NE, FE = 16, 128
K = S // 2 + 1
WS = 64.0
QUAD = 8
PAIR = 4
PT = PAIR * T
CH = 4
NEG = -1.0e30
KEY_LAG, PV_LAG = 4, 6
DOWN_LAG = 3


class Unit:

    def __init__(self, r, c, ways=2):
        self.half, self.parity = r * (ways // 2) + c // 2, c % 2
        self.way = c % ways
        self.n = r * ways + c

    def __add__(self, k):
        return self.n + k

    def __sub__(self, k):
        return self.n - k


def run_steps(eng, steps, first, last, body, start=0, ways=2):
    def straight(t):
        body(lambda lag: Unit((start + t - lag) // ways, (start + t - lag) % ways, ways),
             lambda lag, units: 0 <= t - lag < units, lambda lag, n: t - lag >= n)

    for t in range(first):
        straight(t)
    with eng.Fori((start + first) // ways, (start + last) // ways) as r:
        for c in range(ways):
            body(lambda lag: Unit(r, c - lag, ways), lambda lag, units: True, lambda lag, n: True)
    for t in range(last, steps):
        straight(t)


def bcast(ap, shape):
    return ap.to_broadcast(shape)


def turn_twice(pe, out, tile, g):
    for half in range(2):
        mm = pe.matmul(out[half * C:(half + 1) * C], tile, g.ident[0:T, 0:T], start=True, stop=True)
    return mm


class LayerNorm:

    def __init__(self, nc, ctx, name, tiles, eps, sem=None):
        def sb(n, shape):
            return ctx.enter_context(nc.sbuf_tensor(f"{name}_{n}", shape, F32))

        def own(n):
            return ctx.enter_context(nc.semaphore(f"{name}_{n}"))

        sem = sem or own
        self.tiles, self.eps = tiles, eps
        self.shape = [T, tiles, C]
        self.sums = sb("sums", [T, 2, tiles])
        self.squares = sb("squares", [T, 2, tiles])
        self.shifted = sb("shifted", [T, 2, tiles])
        self.power, self.shift = sb("power", [T, tiles]), sb("shift", [T, tiles])
        self.rstd = sb("rstd", [T, 2, tiles])
        self.centered = sb("centered", [T, 2, tiles, C])
        self.squared = sb("squared", [T, 2, tiles, C])
        self.summed, self.centred, self.square_done = sem("summed"), sem("centred"), sem("square_done")
        self.squares_summed, self.shift_done, self.rstd_done = sem("squares_summed"), sem("shift_done"), sem("rstd_done")
        self.done = sem("done")

    def setup(self, pool, signal):
        pool.memset(self.power[:], -0.5).then_inc(signal, 1)
        pool.memset(self.shift[:], C * self.eps).then_inc(signal, 1)

    def per_token(self, t):
        return bcast(t.unsqueeze(2), self.shape)

    def center(self, dve, u, x, free):
        if free:
            dve.wait_ge(self.done, u - 1)
        dve.tensor_reduce(self.sums[:, u.parity], x, AX.X, ALU.add).then_inc(self.summed, 1)
        dve.wait_ge(self.summed, u + 1)
        dve.scalar_tensor_tensor(out=self.centered[:, u.parity], in0=self.per_token(self.sums[:, u.parity]),
                                 scalar=-1.0 / C, in1=x, op0=ALU.mult, op1=ALU.add).then_inc(self.centred, 1)

    def square(self, act, u):
        act.wait_ge(self.centred, u + 1)
        act.activation(self.squared[:, u.parity], self.centered[:, u.parity], ACT.Square)\
           .then_inc(self.square_done, 1)

    def sum_squares(self, dve, u):
        dve.wait_ge(self.square_done, u + 1)
        dve.tensor_reduce(self.squares[:, u.parity], self.squared[:, u.parity], AX.X, ALU.add)\
           .then_inc(self.squares_summed, 1)

    def root(self, pool, u):
        pool.wait_ge(self.squares_summed, u + 1)
        pool.tensor_tensor(self.shifted[:, u.parity], self.squares[:, u.parity], self.shift[:], ALU.add)\
            .then_inc(self.shift_done, 1)
        pool.wait_ge(self.shift_done, u + 1)
        pool.tensor_tensor(self.rstd[:, u.parity], self.shifted[:, u.parity], self.power[:], ALU.pow)\
            .then_inc(self.rstd_done, 1)

    def scale(self, dve, u, out):
        dve.wait_ge(self.rstd_done, u + 1)
        dve.scalar_tensor_tensor(out=out, in0=self.centered[:, u.parity], scalar=float(C) ** 0.5,
                                 in1=self.per_token(self.rstd[:, u.parity]), op0=ALU.mult, op1=ALU.mult)\
           .then_inc(self.done, 1)


def per_channel(row, tiles, n=C):
    return bcast(row.unsqueeze(1), [T, tiles, n])


def of_tiles(x, u, tiles, start=0):
    return x[:, bass.ds((u - start) * tiles, tiles), :]


def width(ap):
    return int(np.prod(ap.shape[1:]))


def prepare(nc, g, d):
    with ExitStack() as ctx:
        def sb(n, shape, dt=F32):
            return ctx.enter_context(nc.sbuf_tensor(n, shape, dt))

        def ps(n, shape):
            return ctx.enter_context(nc.psum_tensor(n, shape, F32))

        def sem(n):
            return ctx.enter_context(nc.semaphore(n))

        splits = [(g.ffn_w1[:, l, :], d.d1_w[l]) for l in range(2)]
        splits += [(g.w_v[:], d.Wv), (g.w_gate[:], d.gate_w),
                   (g.moe_w1[:].rearrange("p e f -> p (e f)"), d.w1)]
        staged = [sb(f"stage{n}", [2 * C, width(s)]) for n, (s, _) in enumerate(splits)]
        wq, wk = sb("wq", [C, NH * DH]), sb("wk", [C, NH * DH])
        wqT, wkT = sb("wqT", [DH, NH, 2, C]), sb("wkT", [DH, NH, 2, C])
        b2, b2_high, b2_low, b2_even = (sb("b2", [C, C]), sb("b2_high", [C, C], F16), sb("b2_low", [C, C]),
                                        sb("b2_even", [C, C]))
        freq = sb("freq", [K, 2, 2, C])
        dft = sb("dft", [K, 3, 2 * S])
        kernel2 = sb("kernel2", [C, 2, 2 * S])
        tp = ps("tp", [C, 2, 512])
        ap = ps("ap", [2 * C, 2, 512])
        kp = ps("kp", [C, 2, 512])

        staged_in, heads_in, freq_in = sem("staged_in"), sem("heads_in"), sem("freq_in")
        tables_in, ident_in, b2_in, parity_in = sem("tables_in"), sem("ident_in"), sem("b2_in"), sem("parity_in")
        set_up, high_done, low_done = sem("set_up"), sem("high_done"), sem("low_done")
        turned, turned_copied, folded = sem("turned"), sem("turned_copied"), sem("folded")
        fold_high, fold_low = sem("fold_high"), sem("fold_low")
        kernel_done, kernel_copied, kernel_out = sem("kernel_done"), sem("kernel_copied"), sem("kernel_out")
        impulse_added = sem("impulse_added")
        b2_split, b2_parts = sem("b2_split"), sem("b2_parts")

        sp_loads = [(g.ids[:], d.ids)]
        sp_loads += [(g.ffn_w2[:, l], d.d2_w[l].rearrange("(f p) h -> p f h", p=128)) for l in range(2)]
        sp_loads += [(g.ffn_b1[:], d.d1_b)]
        sp_loads += [(g.w_o[:], d.Wo.rearrange("(f p) h -> p f h", p=128)),
                     (g.moe_w2[:], d.w2.rearrange("e f h -> f e h")),
                     (g.moe_b1[:], d.b1)]
        act_loads = [(g.y_bias[0:C, n:n + 1], src.unsqueeze(1)) for n, src in enumerate((d.d2_b[0], d.d2_b[1], d.bo))]
        act_loads += [(g.pos[:], d.pos_emb.rearrange("(k p) c -> p k c", p=T)),
                      (g.table_rows[:], d.table_rows), (g.selector[:], d.selector), (g.ident_ones[:], d.ident_ones),
                      (g.iota[:], d.iota), (g.gate_b[:], bcast(d.gate_b.unsqueeze(0), [T, NE]))]
        act_loads += [(g.rows[:, n, :], bcast(src.unsqueeze(0), [T, C])) for n, src in enumerate(
            (d.ln0_w, d.ln0_b, d.fln_w[0], d.fln_w[1], d.fln_b[0], d.fln_b[1],
             d.iln_w[0], d.iln_w[1], d.iln_b[0], d.iln_b[1], d.gamma, d.beta))]
        act_loads += [(g.table_cols[0:T, par, b], d.table_cols) for par in range(2) for b in range(2)]

        with nc.Block() as block:
            @block.sync
            def _(sp):
                sp.dma_start(g.ident[:], d.ident).then_inc(ident_in, 16)
                sp.dma_start(wq[:], d.Wq).then_inc(heads_in, 16)
                sp.dma_start(wk[:], d.Wk).then_inc(heads_in, 16)
                sp.dma_start(freq[:], d.cw).then_inc(freq_in, 16)
                sp.dma_start(dft[:], d.dft).then_inc(freq_in, 16)
                for stage, (_, source) in zip(staged, splits):
                    for half in range(2):
                        part = stage[half * C:(half + 1) * C, :]
                        if len(source.shape) == 3:
                            part, source_ = part.rearrange("p (e f) -> p e f", e=NE), source.rearrange("e h f -> h e f")
                        else:
                            source_ = source
                        sp.dma_start(part, source_).then_inc(staged_in, 16)
                for dst, src in sp_loads:
                    sp.dma_start(dst, src).then_inc(tables_in, 16)
                sp.wait_ge(impulse_added, 1)
                sp.dma_start(d.filters.rearrange("l c j -> c l j"), kernel2[:]).then_inc(kernel_out, 16)
                sp.wait_ge(kernel_out, 16)
                sp.wait_ge(tables_in, 16 * (len(sp_loads) + len(act_loads)))

            @block.scalar
            def _(act):
                act.dma_start(g.parity[:], d.parity).then_inc(parity_in, 16)
                for q in range(4):
                    act.dma_start(b2[NE * q:NE * q + NE, :], d.b2).then_inc(b2_in, 16)
                act.wait_ge(set_up, 3)
                for dst, src in act_loads:
                    act.dma_start(dst, src).then_inc(tables_in, 16)
                act.wait_ge(staged_in, 16 * 2 * len(splits))
                for stage, (dst, _) in zip(staged, splits):
                    act.activation(dst, stage[:], ACT.Copy, scale=WS).then_inc(high_done, 1)
                act.wait_ge(folded, NH)
                for n in range(2):
                    act.activation(g.w_a[:, 4 * n:4 * n + 4, :], ap[:, n, :].rearrange("p (h c) -> p h c", h=4),
                                   ACT.Copy, scale=WS * DH ** -0.5).then_inc(fold_high, 1)
                act.wait_ge(kernel_done, 2)
                for l in range(2):
                    act.activation(kernel2[:, l, :], kp[:, l, 0:2 * S], ACT.Copy).then_inc(kernel_copied, 1)
                act.wait_ge(b2_in, 64)
                act.activation(b2_high[:], b2[:], ACT.Copy).then_inc(b2_split, 1)

            @block.vector
            def _(dve):
                for n, (stage, (dst, _)) in enumerate(zip(staged, splits)):
                    dve.wait_ge(high_done, n + 1)
                    dve.scalar_tensor_tensor(out=dst[C:2 * C], in0=stage[C:2 * C, :], scalar=WS, in1=dst[C:2 * C],
                                             op0=ALU.mult, op1=ALU.subtract).then_inc(low_done, 1)
                for n in range(2):
                    dve.wait_ge(turned, NH * (n + 1))
                    dst, src = (wqT, wkT)[n], tp[0:DH, n, 0:NH * C].rearrange("p (h c) -> p h c", h=NH)
                    for twice in range(2):
                        dve.tensor_copy(dst[:, :, twice, :], src).then_inc(turned_copied, 1)
                for n in range(2):
                    dve.wait_ge(fold_high, n + 1)
                    half = g.w_a[C:2 * C, 4 * n:4 * n + 4, :]
                    dve.scalar_tensor_tensor(out=half, in0=ap[C:2 * C, n, :].rearrange("p (h c) -> p h c", h=4),
                                             scalar=WS * DH ** -0.5, in1=half,
                                             op0=ALU.mult, op1=ALU.subtract).then_inc(fold_low, 1)
                dve.wait_ge(kernel_copied, 2)
                dve.tensor_scalar(kernel2[:, :, 0:2 * S:S], kernel2[:, :, 0:2 * S:S], 1.0, None, ALU.add)\
                   .then_inc(impulse_added, 1)
                dve.wait_ge(b2_split, 1)
                dve.wait_ge(parity_in, 16)
                dve.wait_ge(set_up, 3)
                dve.tensor_tensor(b2_low[:], b2[:], b2_high[:], ALU.subtract).then_inc(b2_parts, 1)
                dve.tensor_scalar(b2_even[:], b2_high[:], g.parity[:, 0:1], None, ALU.mult).then_inc(b2_parts, 1)
                dve.wait_ge(b2_parts, 2)
                dve.scalar_tensor_tensor(out=g.moe_b2[0:C, :], in0=b2_low[:], scalar=g.parity[:, 1:2], in1=b2_even[:],
                                         op0=ALU.mult, op1=ALU.add).then_inc(b2_parts, 1)

            @block.gpsimd
            def _(pool):
                pool.memset(g.y_bias[:], 0.0).then_inc(set_up, 1)
                pool.memset(g.ones[:], 1.0).then_inc(set_up, 1)
                pool.memset(g.moe_b2[:], 0.0).then_inc(set_up, 1)

            @block.tensor
            def _(pe):
                pe.wait_ge(heads_in, 32)
                pe.wait_ge(ident_in, 16)
                for n, w in enumerate((wq, wk)):
                    for h in range(NH):
                        pe.transpose(tp[0:DH, n, h * C:(h + 1) * C], w[:, h * DH:(h + 1) * DH], g.ident[0:C, 0:C])\
                          .then_inc(turned, 1)
                pe.wait_ge(turned_copied, 4)
                for h in range(NH):
                    pe.matmul(ap[:, h // 4, (h % 4) * 2 * C:(h % 4 + 1) * 2 * C],
                              wqT[:, h, :, :].rearrange("p a c -> p (a c)"),
                              wkT[:, h, :, :].rearrange("p a c -> p (a c)"), start=True, stop=True).then_inc(folded, 1)
                pe.wait_ge(freq_in, 32)
                for l in range(2):
                    for part in range(2):
                        mm = pe.matmul(kp[:, l, 0:2 * S], freq[:, l, part, :], dft[:, part and part + l, :],
                                       start=(part == 0), stop=(part == 1))
                    mm.then_inc(kernel_done, 1)


def embed(nc, g, d):
    units = NT // QUAD
    with ExitStack() as ctx:
        def sb(n, shape, dt=F32):
            return ctx.enter_context(nc.sbuf_tensor(n, shape, dt))

        def sem(n):
            return ctx.enter_context(nc.semaphore(n))

        index = sb("index", [T, 2, QUAD], I32)
        found = sb("found", [T, 2, QUAD, C])
        placed = sb("placed", [T, 2, QUAD, C])
        scaled = sb("scaled", [T, 2, QUAD, C])
        weighted = sb("weighted", [T, 2, QUAD, C])
        ln = LayerNorm(nc, ctx, "ln0", QUAD, 1e-12)
        set_up, index_ready = sem("emb_set_up"), sem("index_ready")
        found_in = [sem("found_in0"), sem("found_in1")]
        placed_done, weighted_done, stored = sem("placed_done"), sem("weighted_done"), sem("emb_stored")

        with nc.Block() as block:
            @block.gpsimd
            def _(pool):
                ln.setup(pool, set_up)
                pool.wait_ge(set_up, 2)

                def step(unit, has, later):
                    if has(0, units):
                        u = unit(0)
                        if later(0, 2):
                            pool.wait_ge(placed_done, u - 1)
                        pool.tensor_copy(index[:, u.parity], g.ids[:, bass.ds(u.n * QUAD, QUAD)]).then_inc(index_ready, 1)
                        pool.wait_ge(index_ready, u + 1)
                    if has(2, units):
                        ln.root(pool, unit(2))
                    if has(0, units):
                        for j in range(QUAD):
                            pool.indirect_dma_start(
                                out=found[:, u.parity, j, :], out_offset=None, in_=d.item_emb,
                                in_offset=bass.IndirectOffsetOnAxis(ap=index[:, u.parity, j:j + 1], axis=0),
                            ).then_inc(found_in[u.parity], 16)

                run_steps(pool, units + 2, 4, units, step)

            @block.vector
            def _(dve):
                def step(unit, has, later):
                    if has(2, units):
                        u = unit(2)
                        ln.scale(dve, u, scaled[:, u.parity])
                        dve.wait_ge(ln.done, u + 1)
                        dve.tensor_tensor(weighted[:, u.parity], scaled[:, u.parity], per_channel(g.rows[:, 0, :], QUAD),
                                          ALU.mult).then_inc(weighted_done, 1)
                        dve.wait_ge(weighted_done, u + 1)
                        dve.tensor_tensor(of_tiles(g.x, u, QUAD), weighted[:, u.parity],
                                          per_channel(g.rows[:, 1, :], QUAD), ALU.add).then_inc(stored, 1)
                    if has(0, units):
                        u = unit(0)
                        dve.wait_ge(found_in[u.parity], 16 * QUAD * u.half + 16 * QUAD)
                        if later(0, 2):
                            dve.wait_ge(ln.centred, u - 1)
                        pos = g.pos[:].unsqueeze(1).to_broadcast([T, QUAD // 2, 2, C])
                        dve.tensor_tensor(placed[:, u.parity].rearrange("p (b k) c -> p b k c", k=2),
                                          found[:, u.parity].rearrange("p (b k) c -> p b k c", k=2), pos,
                                          ALU.add).then_inc(placed_done, 1)
                        dve.wait_ge(placed_done, u + 1)
                        ln.center(dve, u, placed[:, u.parity], later(0, 2))
                        ln.sum_squares(dve, u)

                run_steps(dve, units + 2, 4, units, step)

            @block.scalar
            def _(act):
                def step(unit, has, later):
                    if has(0, units):
                        if later(0, 2):
                            act.wait_ge(ln.squares_summed, unit(0) - 1)
                        ln.square(act, unit(0))

                run_steps(act, units, 4, units, step)


def spectral_filter(nc, g, d, l):
    units = C // CH
    with ExitStack() as ctx:
        def sem(n):
            return ctx.enter_context(nc.semaphore(f"{n}_{l}"))

        circulant = ctx.enter_context(nc.sbuf_tensor(f"circulant{l}", [T, 2, CH, S], F32))
        conv = ctx.enter_context(nc.psum_tensor(f"conv{l}", [T, 2, 2, CH, B], F32))
        loaded = [sem("circulant_in0"), sem("circulant_in1")]
        convolved = sem("convolved")
        stored = [sem("filtered_first"), sem("filtered_second")]
        rows = d.filters[l]
        rows = bass.AP(tensor=rows.tensor, offset=rows.offset + 1, ap=[[1, T], [2 * S, C], [1, S]])
        x = g.x[:].rearrange("p (b k) c -> p k b c", k=2)

        with nc.Block() as block:
            @block.sync
            def _(sp):
                def step(unit, has, later):
                    u = unit(0)
                    if later(0, 2):
                        sp.wait_ge(convolved, u - 1)
                    sp.dma_start(circulant[:, u.parity], rows[:, bass.ds(u.n * CH, CH), :])\
                      .then_inc(loaded[u.parity], 16)

                run_steps(sp, units, 4, units, step)

            @block.tensor
            def _(pe):
                def step(unit, has, later):
                    u = unit(0)
                    pe.wait_ge(loaded[u.parity], 16 * u.half + 16)
                    if later(0, 2):
                        pe.wait_ge(stored[0], u - 1)
                        pe.wait_ge(stored[1], u - 1)
                    for c in range(CH):
                        for k in range(2):
                            for stay in range(2):
                                source = x[:, k if stay else 1 - k, :, bass.ds(u.n * CH + c, 1)]
                                mm = pe.matmul(conv[:, u.parity, k, c, :],
                                               circulant[:, u.parity, c, stay * T:(stay + 1) * T],
                                               source.rearrange("p b c -> p (b c)"),
                                               start=(stay == 0), stop=(stay == 1))
                    mm.then_inc(convolved, 1)

                run_steps(pe, units, 4, units, step)

            def result(u, k):
                return conv[:, u.parity, k].rearrange("p c b -> p b c")

            @block.vector
            def _(dve):
                def step(unit, has, later):
                    u = unit(0)
                    dve.wait_ge(convolved, u + 1)
                    dve.tensor_copy(x[:, 0, :, bass.ds(u.n * CH, CH)], result(u, 0)).then_inc(stored[0], 1)

                run_steps(dve, units, 4, units, step)

            @block.scalar
            def _(act):
                def step(unit, has, later):
                    u = unit(0)
                    act.wait_ge(convolved, u + 1)
                    act.activation(x[:, 1, :, bass.ds(u.n * CH, CH)], result(u, 1), ACT.Copy).then_inc(stored[1], 1)

                run_steps(act, units, 4, units, step)


def feed_forward(nc, g, d, l):
    units = NT // QUAD
    start = l * units
    with ExitStack() as ctx:
        def sb(n, shape, dt=F32):
            return ctx.enter_context(nc.sbuf_tensor(f"{n}_{l}", shape, dt))

        def ps(n, shape):
            return ctx.enter_context(nc.psum_tensor(f"{n}_{l}", shape, F32))

        def sem(n):
            if n not in g.ffn_sems:
                g.ffn_sems[n] = g.ctx.enter_context(nc.semaphore(n))
            return g.ffn_sems[n]

        scaled, weighted = sb("f_scaled", [T, 2, QUAD, C]), sb("f_weighted", [T, 2, QUAD, C])
        base = sb("f_base", [T, 2, QUAD, C])
        x1, x2 = sb("f_x1", [2 * C, 2, 2, PT], F16), sb("f_x2", [2 * C, 2, 2, PT], F16)
        hidden = sb("f_hidden", [128, 2, 2, PT])
        y = sb("f_y", [128, 2, PT])
        top, both = sb("f_top", [T, 2, QUAD, C]), sb("f_both", [T, 2, QUAD, C])
        scaled2, weighted2 = sb("f_scaled2", [T, 2, QUAD, C]), sb("f_weighted2", [T, 2, QUAD, C])
        xt_ps = ps("f_xt", [128, 2, 512])
        h_ps = ps("f_h", [128, 4, 512])
        y_ps = ps("f_yps", [128, 512])
        back_ps = ps("f_back", [T, PAIR, 2 * C])
        backs = [back_ps, xt_ps[0:T, 1, :].rearrange("p (j c) -> p j c", j=PAIR)]
        ln1 = LayerNorm(nc, ctx, f"fln{l}", QUAD, 1e-12, lambda n: sem(f"f_ln_{n}"))
        ln2 = LayerNorm(nc, ctx, f"iln{l}", QUAD, 1e-12, lambda n: sem(f"f_ln2_{n}"))
        set_up, weighted_done, base_done = sem("f_set_up"), sem("f_weighted_done"), sem("f_base_done")
        turned, x1_done, x2_done = sem("f_turned"), sem("f_x1_done"), sem("f_x2_done")
        up_done, gelu_done, down_done, y_done = sem("f_up_done"), sem("f_gelu_done"), sem("f_down_done"), sem("f_y_done")
        back_done, top_done, both_done = sem("f_back_done"), sem("f_top_done"), sem("f_both_done")
        weighted2_done, stored = sem("f_weighted2_done"), sem("f_stored")

        with nc.Block() as block:
            @block.gpsimd
            def _(pool):
                ln1.setup(pool, set_up)
                ln2.setup(pool, set_up)
                pool.wait_ge(set_up, 4 * (l + 1))

                def step(unit, has, later):
                    if has(0, units):
                        ln1.root(pool, unit(0))
                    if has(2, units):
                        ln2.root(pool, unit(2))
                    if has(0, units):
                        u = unit(0)
                        pool.wait_ge(ln1.done, u + 1)
                        if later(0, 2):
                            pool.wait_ge(both_done, 2 * (u - 1))
                        pool.tensor_tensor(weighted[:, u.parity], scaled[:, u.parity],
                                           per_channel(g.rows[:, 2 + l, :], QUAD), ALU.mult).then_inc(weighted_done, 1)
                    if has(2, units):
                        u = unit(2)
                        pool.wait_ge(ln2.done, u + 1)
                        pool.tensor_tensor(weighted2[:, u.parity], scaled2[:, u.parity],
                                           per_channel(g.rows[:, 6 + l, :], QUAD), ALU.mult).then_inc(weighted2_done, 1)
                    if has(0, units):
                        u = unit(0)
                        pool.wait_ge(weighted_done, u + 1)
                        pool.tensor_tensor(base[:, u.parity], weighted[:, u.parity],
                                           per_channel(g.rows[:, 4 + l, :], QUAD), ALU.add).then_inc(base_done, 1)
                    if has(2, units):
                        u = unit(2)
                        pool.wait_ge(weighted2_done, u + 1)
                        pool.tensor_tensor(of_tiles(g.x, u, QUAD, start), weighted2[:, u.parity],
                                           per_channel(g.rows[:, 8 + l, :], QUAD), ALU.add).then_inc(stored, 1)

                run_steps(pool, units + 2, 4, units, step, start)

            @block.vector
            def _(dve):
                def step(unit, has, later):
                    if has(2, units):
                        u = unit(2)
                        if later(2, 2):
                            dve.wait_ge(ln2.centred, u - 1)
                        for q in range(2):
                            tiles = slice(q * PAIR, q * PAIR + PAIR)
                            dve.wait_ge(back_done, 2 * u.n + q + 1)
                            dve.tensor_tensor(top[:, u.parity, tiles], backs[q][:, :, 0:C], base[:, u.parity, tiles],
                                              ALU.add).then_inc(top_done, 1)
                            dve.wait_ge(top_done, 2 * u.n + q + 1)
                            dve.tensor_tensor(both[:, u.parity, tiles], backs[q][:, :, C:2 * C], top[:, u.parity, tiles],
                                              ALU.add).then_inc(both_done, 1)
                    if has(1, units):
                        u = unit(1)
                        for q in range(2):
                            dve.wait_ge(x1_done, 2 * u.n + q + 1)
                            dve.tensor_tensor(x2[:, u.parity, q], xt_ps[:, q, 0:PT], x1[:, u.parity, q],
                                              ALU.subtract).then_inc(x2_done, 1)
                    if has(0, units):
                        u = unit(0)
                        ln1.center(dve, u, of_tiles(g.x, u, QUAD, start), later(0, 2))
                    if has(2, units):
                        u = unit(2)
                        dve.wait_ge(both_done, 2 * u.n + 2)
                        ln2.center(dve, u, both[:, u.parity], later(2, 2))
                    if has(0, units):
                        ln1.sum_squares(dve, unit(0))
                    if has(2, units):
                        ln2.sum_squares(dve, unit(2))
                    if has(0, units):
                        u = unit(0)
                        if later(0, 2):
                            dve.wait_ge(weighted_done, u - 1)
                        ln1.scale(dve, u, scaled[:, u.parity])
                    if has(2, units):
                        u = unit(2)
                        if later(2, 2):
                            dve.wait_ge(weighted2_done, u - 1)
                        ln2.scale(dve, u, scaled2[:, u.parity])

                run_steps(dve, units + 2, 4, units, step, start)

            @block.scalar
            def _(act):
                def step(unit, has, later):
                    if has(1, units):
                        u = unit(1)
                        for q in range(2):
                            act.wait_ge(turned, 2 * u.n + q + 1)
                            if q == 0 and later(1, 2):
                                act.wait_ge(up_done, 4 * (u - 1))
                            act.activation(x1[:, u.parity, q], xt_ps[:, q, 0:PT], ACT.Copy).then_inc(x1_done, 1)
                    if has(0, units):
                        u = unit(0)
                        if later(0, 2):
                            act.wait_ge(ln1.squares_summed, u - 1)
                        ln1.square(act, u)
                    if has(2, units):
                        u = unit(2)
                        if later(2, 2):
                            act.wait_ge(ln2.squares_summed, u - 1)
                        ln2.square(act, u)
                    if has(1, units):
                        u = unit(1)
                        for q in range(2):
                            for f in range(2):
                                act.wait_ge(up_done, 4 * u.n + 2 * q + f + 1)
                                if later(1, 1):
                                    act.wait_ge(down_done, 2 * u.n + q - 1)
                                act.activation(hidden[:, q, f], h_ps[:, 2 * q + f, 0:PT], ACT.Gelu,
                                               bias=g.ffn_b1[:, l, f:f + 1], scale=1.0 / WS).then_inc(gelu_done, 1)
                            if q == 1:
                                out_y(act, u, 0, later)
                        out_y(act, u, 1, later)

                def out_y(act, u, q, later):
                    act.wait_ge(down_done, 2 * u.n + q + 1)
                    if later(1, 1):
                        act.wait_ge(back_done, 2 * u.n + q - 1)
                    act.activation(y[:, q], y_ps[:, 0:PT], ACT.Identity, bias=g.y_bias[:, l:l + 1]).then_inc(y_done, 1)

                run_steps(act, units + 2, 4, units, step, start)

            @block.tensor
            def _(pe):
                def step(unit, has, later):
                    if not has(1, units):
                        return
                    u = unit(1)
                    pe.wait_ge(base_done, u + 1)
                    for q in range(2):
                        if later(1, 1):
                            pe.wait_ge(*((x2_done, 2 * u.n - 1), (both_done, 2 * u.n))[q])
                        for j in range(PAIR):
                            mm = turn_twice(pe, xt_ps[:, q, j * T:(j + 1) * T], base[:, u.parity, q * PAIR + j, :], g)
                        mm.then_inc(turned, 1)

                    def up(q):
                        pe.wait_ge(x2_done, 2 * u.n + q + 1)
                        if later(1, 1):
                            pe.wait_ge(gelu_done, 4 * u.n + 2 * q - 2)
                        for f in range(2):
                            w = g.ffn_w1[:, l, f * 128:(f + 1) * 128]
                            out = h_ps[:, 2 * q + f, 0:PT]
                            pe.matmul(out, w, x1[:, u.parity, q], start=True, stop=False)
                            pe.matmul(out, w, x2[:, u.parity, q], start=False, stop=True).then_inc(up_done, 1)

                    def down(q):
                        pe.wait_ge(gelu_done, 4 * u.n + 2 * q + 2)
                        if q == 1:
                            pe.wait_ge(y_done, 2 * u.n + 1)
                        elif later(1, 1):
                            pe.wait_ge(y_done, 2 * u.n)
                        for f in range(2):
                            mm = pe.matmul(y_ps[f * C:(f + 1) * C, 0:PT], g.ffn_w2[:, l, f, :], hidden[:, q, f],
                                           start=True, stop=True)
                        mm.then_inc(down_done, 1)

                    def back(q):
                        pe.wait_ge(y_done, 2 * u.n + q + 1)
                        if q == 0 and later(1, 1):
                            pe.wait_ge(both_done, 2 * u.n - 1)
                        for j in range(PAIR):
                            mm = pe.transpose(backs[q][:, j, :], y[:, q, j * T:(j + 1) * T], g.ident[:])
                        mm.then_inc(back_done, 1)

                    up(0)
                    up(1)
                    down(0)
                    down(1)
                    back(0)
                    back(1)

                run_steps(pe, units + 2, 4, units, step, start)


def attention(nc, g, d):
    units = NT // PAIR
    with ExitStack() as ctx:
        def sb(n, shape, dt=F32):
            return ctx.enter_context(nc.sbuf_tensor(f"a_{n}", shape, dt))

        def ps(n, shape):
            return ctx.enter_context(nc.psum_tensor(f"a_{n}", shape, F32))

        def sem(n):
            return ctx.enter_context(nc.semaphore(f"a_{n}"))

        xn = sb("xn", [T, 2, PAIR, C])
        x1, x2 = sb("x1", [2 * C, 4, PT], F16), sb("x2", [2 * C, 4, PT], F16)
        gs = sb("gs", [2 * C, 2, NH, PT], F16)
        v = sb("v", [T, 2, PAIR, NH * DH])
        block_max = sb("block_max", [T, 2, NH, 3])
        row_max = sb("row_max", [T, 96])
        max_rows = sb("max_rows", [48, 2, T], BF16)
        probs = sb("probs", [T, 4, 3 * T])
        log_sum, inv_sum = sb("log_sum", [128, 2, S]), sb("inv_sum", [128, 2, S])
        heads_out = sb("heads_out", [128, 2, PT])
        y = sb("y", [128, PT])
        top = sb("top", [T, PAIR, C])
        proj = ps("proj", [128, 2, 512])
        max_ps = ps("max_ps", [T, 2, 512])
        score_ps = ps("score_ps", [T, 2, 512])
        pv_ps = ps("pv_ps", [128, 2, 512])
        back_ps = proj[0:T, 1, :].rearrange("p (j c) -> p j c", j=PAIR)
        ln = LayerNorm(nc, ctx, "a_ln", PAIR, 1e-5)
        set_up = sem("set_up")
        turned, x1_done, x2_done = sem("turned"), sem("x1_done"), sem("x2_done")
        g_full, g_high, g_low = sem("g_full"), sem("g_high"), sem("g_low")
        v_full, v_done = sem("v_full"), sem("v_done")
        max_full, max_done, row_max_done = sem("max_full"), sem("max_done"), sem("row_max_done")
        max_turned, max_rows_done = sem("max_turned"), sem("max_rows_done")
        max_in = [sem("max_in0"), sem("max_in1")]
        score_full, probs_done, pv_full = sem("score_full"), sem("probs_done"), sem("pv_full")
        log_done, inv_done, heads_done = sem("log_done"), sem("inv_done"), sem("heads_done")
        y_full, y_done, back_full, top_done, stored = (
            sem("y_full"), sem("y_done"), sem("back_full"), sem("top_done"), sem("stored"))
        slots = 2 * NH

        def of(b, k=0):
            return slice(b * S + k * T, b * S + (k + 1) * T)

        def both(b):
            return slice(b * S, (b + 1) * S)

        def late(s, by, has):
            stage, i = (3, s - by) if s >= by else (4, s - by + slots)
            return (stage, i) if has(stage, units) else None

        def projection(s, has):
            if s % 2 == 0:
                return None
            stage, h = (2, (s + 3) // 2) if s <= 11 else (1, (s - 13) // 2)
            return (stage, h) if has(stage, units) else None

        whole = [(10, 3, 0), (14, 3, 1), (2, 4, 2), (6, 4, 3)]

        with nc.Block() as block:
            @block.gpsimd
            def _(pool):
                ln.setup(pool, set_up)
                pool.memset(row_max[:], 0.0).then_inc(set_up, 1)
                pool.wait_ge(set_up, 3)

                def step(unit, has, later):
                    if has(0, units):
                        ln.root(pool, unit(0))

                run_steps(pool, units + 4, 8, units, step, ways=4)

            @block.sync
            def _(sp):
                def step(unit, has, later):
                    if not has(3, units):
                        return
                    b = unit(3)
                    sp.wait_ge(max_rows_done, b + 1)
                    sp.dma_start(g.table_cols[T:T + 1, b.parity].rearrange("p b h (k t) -> p (b h k) t", t=T),
                                 max_rows[:, b.parity, :]).then_inc(max_in[b.parity], 16)

                run_steps(sp, units + 4, 8, units, step, ways=4)

            @block.scalar
            def _(act):
                act.preload_act_table_set("natural_log_exp_and_others")

                def step(unit, has, later):
                    f, n, a, b, c = (unit(k) for k in range(5))
                    for s in range(slots):
                        if late(s, KEY_LAG, has):
                            stage, i = late(s, KEY_LAG, has)
                            u = unit(stage)
                            act.wait_ge(score_full, 16 * u.n + i + 1)
                            if i >= 4 or later(stage, 1):
                                act.wait_ge(pv_full, 16 * u.n + i - 3)
                            act.activation(probs[:, i % 4, :], score_ps[:, i % 2, 0:3 * T], ACT.Exp).then_inc(probs_done, 1)
                        if projection(s, has):
                            stage, h = projection(s, has)
                            u = unit(stage)
                            act.wait_ge(g_full, 8 * u.n + h + 1)
                            if later(stage, 2):
                                act.wait_ge(score_full, 16 * u.n - 23 + h)
                            act.activation(gs[:, u.parity, h], proj[:, 0, 0:PT], ACT.Copy, scale=1.0 / WS)\
                               .then_inc(g_high, 1)
                        if s == 3 and has(1, units):
                            act.wait_ge(turned, n + 1)
                            if later(1, 4):
                                act.wait_ge(score_full, 16 * (n - 3))
                            act.activation(x1[:, n.way], proj[:, 1, 0:PT], ACT.Copy).then_inc(x1_done, 1)
                        if s in (7, 9) and has(2, units):
                            k = (s - 7) // 2
                            act.wait_ge(v_full, 2 * a.n + k + 1)
                            if k == 0 and later(2, 2):
                                act.wait_ge(pv_full, 16 * (a - 1))
                            act.activation(v[:, a.parity, 2 * k:2 * k + 2, :],
                                           proj[0:T, 1, :].rearrange("p (j n) -> p j n", j=2),
                                           ACT.Copy, scale=1.0 / WS).then_inc(v_done, 1)
                        if s == 1 and has(3, units):
                            act.wait_ge(max_turned, b + 1)
                            if later(3, 2):
                                act.wait_ge(max_in[b.parity], 16 * b.half)
                            act.activation(max_rows[:, b.parity, :], proj[0:48, 1, 0:T], ACT.Copy, scale=-1.0)\
                               .then_inc(max_rows_done, 1)
                        for at, stage, q in whole:
                            if s == at and has(stage, units):
                                u = unit(stage)
                                act.wait_ge(pv_full, 16 * u.n + 4 * q + 4)
                                if q or later(stage, 1):
                                    act.wait_ge(inv_done, 4 * u.n + q)
                                act.activation(log_sum[:, q % 2], pv_ps[:, q % 2, S:2 * S], ACT.Ln).then_inc(log_done, 1)
                                act.wait_ge(log_done, 4 * u.n + q + 1)
                                if q >= 2 or later(stage, 1):
                                    act.wait_ge(heads_done, 4 * u.n + q - 1)
                                act.activation(inv_sum[:, q % 2], log_sum[:, q % 2], ACT.Exp, scale=-1.0)\
                                   .then_inc(inv_done, 1)
                        if s == 7 and has(0, units):
                            if later(0, 2):
                                act.wait_ge(ln.squares_summed, f - 1)
                            ln.square(act, f)
                        if s == 12 and has(4, units):
                            act.wait_ge(y_full, c + 1)
                            if later(4, 1):
                                act.wait_ge(back_full, c.n)
                            act.activation(y[:], proj[:, 1, 0:PT], ACT.Identity, bias=g.y_bias[:, 2:3]).then_inc(y_done, 1)

                run_steps(act, units + 4, 8, units, step, ways=4)

            @block.vector
            def _(dve):
                def step(unit, has, later):
                    f, n, a, b, c = (unit(k) for k in range(5))
                    for s in range(slots):
                        if s == 0 and has(3, units):
                            dve.wait_ge(max_done, 16 * b.n + 16)
                            if later(3, 1):
                                dve.wait_ge(max_turned, b.n)
                            rows = row_max[:, 0:48].rearrange("p (b h k) -> p b h k", b=2, h=NH)
                            dve.tensor_copy(rows[:, :, :, 0], block_max[:, :, :, 0]).then_inc(row_max_done, 1)
                            dve.tensor_tensor(rows[:, :, :, 1:3], bcast(block_max[:, :, :, 1:2], [T, 2, NH, 2]),
                                              bcast(block_max[:, :, :, 2:3], [T, 2, NH, 2]), ALU.max)\
                               .then_inc(row_max_done, 1)
                        if has(2, units):
                            dve.wait_ge(max_full, 16 * a.n + s + 1)
                            if s == 0 and later(2, 1):
                                dve.wait_ge(row_max_done, 2 * a.n)
                            dve.tensor_reduce(block_max[:, s % 2, s // 2, :],
                                              max_ps[:, s % 2, 0:3 * T].rearrange("p (k t) -> p k t", k=3),
                                              AX.X, ALU.max).then_inc(max_done, 1)
                        if projection(s, has):
                            stage, h = projection(s, has)
                            u = unit(stage)
                            dve.wait_ge(g_high, 8 * u.n + h + 1)
                            low = gs[C:2 * C, u.parity, h]
                            dve.scalar_tensor_tensor(out=low, in0=proj[C:2 * C, 0, 0:PT], scalar=1.0 / WS, in1=low,
                                                     op0=ALU.mult, op1=ALU.subtract).then_inc(g_low, 1)
                        if s == 4 and has(1, units):
                            dve.wait_ge(x1_done, n + 1)
                            dve.tensor_tensor(x2[:, n.way], proj[:, 1, 0:PT], x1[:, n.way], ALU.subtract)\
                               .then_inc(x2_done, 1)
                        if s == 5 and has(0, units):
                            ln.center(dve, f, of_tiles(g.x, f, PAIR), later(0, 2))
                        if s == 9 and has(0, units):
                            ln.sum_squares(dve, f)
                        if s == 15 and has(0, units):
                            if later(0, 2):
                                dve.wait_ge(turned, f - 1)
                            ln.scale(dve, f, xn[:, f.parity])
                        for at, stage, q in whole:
                            if s == (at + 1) % slots and has(stage, units):
                                u = unit(stage)
                                dve.wait_ge(inv_done, 4 * u.n + q + 1)
                                if q == 0 and later(3, 1):
                                    dve.wait_ge(y_full, u.n)
                                dve.tensor_tensor(heads_out[:, q % 2, both(q // 2)], pv_ps[:, q % 2, 0:S],
                                                  inv_sum[:, q % 2], ALU.mult).then_inc(heads_done, 1)
                        if s == 14 and has(4, units):
                            dve.wait_ge(back_full, c + 1)
                            if later(4, 1):
                                dve.wait_ge(stored, c.n)
                            x = of_tiles(g.x, c, PAIR)
                            dve.tensor_tensor(top[:], back_ps[:, :, 0:C], x, ALU.add).then_inc(top_done, 1)
                            dve.wait_ge(top_done, c + 1)
                            dve.tensor_tensor(x, back_ps[:, :, C:2 * C], top[:], ALU.add).then_inc(stored, 1)

                run_steps(dve, units + 4, 8, units, step, ways=4)

            @block.tensor
            def _(pe):
                def step(unit, has, later):
                    n, a, b, c = (unit(k) for k in range(1, 5))

                    def turn():
                        pe.wait_ge(ln.done, n + 1)
                        if later(1, 2):
                            pe.wait_ge(max_rows_done, n - 1)
                        elif later(1, 1):
                            pe.wait_ge(x2_done, n.n)
                        for j in range(PAIR):
                            mm = turn_twice(pe, proj[:, 1, j * T:(j + 1) * T], xn[:, n.parity, j, :], g)
                        mm.then_inc(turned, 1)

                    def project(stage, h):
                        u = unit(stage)
                        if h == 0:
                            pe.wait_ge(x2_done, u + 1)
                        if h or later(stage, 1):
                            pe.wait_ge(g_low, 8 * u.n + h)
                        for part, x in enumerate((x1, x2)):
                            mm = pe.matmul(proj[:, 0, 0:PT], g.w_a[:, h, :], x[:, u.way], start=(part == 0),
                                           stop=(part == 1))
                        mm.then_inc(g_full, 1)

                    def values(k):
                        if k == 1:
                            pe.wait_ge(v_done, 2 * a.n + 1)
                        elif has(1, units):
                            pe.wait_ge(x2_done, a + 2)
                        else:
                            pe.wait_ge(max_rows_done, a.n)
                        for j in range(2):
                            for part, x in enumerate((x1, x2)):
                                mm = pe.matmul(proj[0:T, 1, j * 256:(j + 1) * 256], x[:, a.way, of(k, j)], g.w_v[:],
                                               start=(part == 0), stop=(part == 1))
                        mm.then_inc(v_full, 1)

                    def query_rows(m):
                        h, q = m // 2, m % 2
                        if q == 0:
                            pe.wait_ge(g_low, 8 * a.n + h + 1)
                        if m >= 2 or later(2, 1):
                            pe.wait_ge(max_done, 16 * a.n + m - 1)
                        out = max_ps[:, m % 2, 0:3 * T]
                        pe.matmul(out, g.ident_ones[0:T, :], g.table_rows[:, h, :], start=True, stop=False)
                        pe.matmul(out[:, 0:T], gs[:, a.parity, h, of(q, 0)], x1[:, a.way, of(q, 0)],
                                  start=False, stop=False)
                        pe.matmul(out[:, T:3 * T], gs[:, a.parity, h, of(q, 1)], x1[:, a.way, both(q)],
                                  start=False, stop=True).then_inc(max_full, 1)

                    def turn_maxima():
                        pe.wait_ge(row_max_done, 2 * b.n + 2)
                        if later(3, 2):
                            pe.wait_ge(stored, b - 1)
                        else:
                            pe.wait_ge(v_done, 2 * b.n + 2)
                        pe.transpose(proj[0:96, 1, 0:T], row_max[:], g.ident[0:T, 0:T]).then_inc(max_turned, 1)

                    def key_rows(stage, i):
                        u, h, q = unit(stage), i % NH, i // NH
                        if i == 0:
                            pe.wait_ge(max_in[u.parity], 16 * u.half + 16)
                        if i >= 2 or later(stage, 1):
                            pe.wait_ge(probs_done, 16 * u.n + i - 1)
                        out = score_ps[:, i % 2, 0:3 * T]
                        pe.matmul(out, g.ident_ones[:], g.table_cols[:, u.parity, q, h, :], start=True, stop=False)
                        for part, x in enumerate((x1, x2)):
                            pe.matmul(out[:, 0:S], x[:, u.way, of(q, 0)], gs[:, u.parity, h, both(q)],
                                      start=False, stop=False)
                            mm = pe.matmul(out[:, S:3 * T], x[:, u.way, of(q, 1)], gs[:, u.parity, h, of(q, 1)],
                                           start=False, stop=(part == 1))
                        mm.then_inc(score_full, 1)

                    def weigh(s, stage, i):
                        u, h, q = unit(stage), i % NH, i // NH
                        group, j = i // 4, i % 4
                        if not late(s, KEY_LAG, has):
                            pe.wait_ge(probs_done, 16 * u.n + i + 1)
                        if j == 0 and (group >= 2 or later(stage, 1)):
                            pe.wait_ge(heads_done, 4 * u.n + group - 1)
                        out = pv_ps[32 * j:32 * j + 32, group % 2, :]
                        for k in range(2):
                            p = probs[:, i % 4, 0:S] if k == 0 else probs[:, i % 4, S:3 * T]
                            for first, w in enumerate((v[:, u.parity, 2 * q + k, h * DH:(h + 1) * DH], g.ones[:])):
                                mm = pe.matmul(out[:, first * S + k * T:(first + 1) * S], w, p,
                                               start=(k == 0 and first == 0), stop=(k == 1), skip_group_check=True)
                        mm.then_inc(pv_full, 1)

                    def out_project():
                        pe.wait_ge(heads_done, 4 * c.n + 4)
                        if has(2, units):
                            pe.wait_ge(v_done, 2 * a.n + 2)
                        elif has(3, units):
                            pe.wait_ge(max_rows_done, b + 1)
                        else:
                            pe.wait_ge(stored, c.n)
                        for half in range(2):
                            mm = pe.matmul(proj[half * C:(half + 1) * C, 1, 0:PT], g.w_o[:, half, :], heads_out[:, half, :],
                                           start=True, stop=True)
                        mm.then_inc(y_full, 1)

                    def turn_back():
                        pe.wait_ge(y_done, c + 1)
                        for j in range(PAIR):
                            mm = pe.transpose(back_ps[:, j, :], y[:, j * T:(j + 1) * T], g.ident[:])
                        mm.then_inc(back_full, 1)

                    for s in range(slots):
                        if s == 3 and has(1, units):
                            turn()
                        if projection(s, has):
                            project(*projection(s, has))
                        if has(2, units):
                            query_rows(s)
                        if s == 1 and has(3, units):
                            turn_maxima()
                        if s in (7, 9) and has(2, units):
                            values((s - 7) // 2)
                        if late(s, KEY_LAG, has):
                            key_rows(*late(s, KEY_LAG, has))
                        if late(s, PV_LAG, has):
                            weigh(s, *late(s, PV_LAG, has))
                        if s == 11 and has(4, units):
                            out_project()
                        if s == 13 and has(4, units):
                            turn_back()

                run_steps(pe, units + 4, 8, units, step, ways=4)


def experts(nc, g, d, out):
    units = NT // PAIR
    with ExitStack() as ctx:
        def sb(n, shape, dt=F32):
            return ctx.enter_context(nc.sbuf_tensor(f"m_{n}", shape, dt))

        def ps(n, shape):
            return ctx.enter_context(nc.psum_tensor(f"m_{n}", shape, F32))

        def sem(n):
            return ctx.enter_context(nc.semaphore(f"m_{n}"))

        xn = sb("xn", [T, 4, PAIR, C])
        x1, x2 = sb("x1", [2 * C, 4, PT], F16), sb("x2", [2 * C, 4, PT], F16)
        logits = sb("logits", [T, PAIR, NE])
        best, best_at = sb("best", [T, PAIR, 8]), sb("best_at", [T, PAIR, 8], U32)
        at = sb("at", [T, PAIR, 2])
        behind, odds, total = sb("behind", [T, PAIR]), sb("odds", [T, PAIR]), sb("total", [T, PAIR])
        share = sb("share", [T, PAIR, 2])
        chosen = sb("chosen", [T, 2, PAIR, NE])
        part = sb("part", [T, 2, PAIR, NE])
        gates = sb("gates", [T, PAIR, 6, NE])
        gate_rows = sb("gate_rows", [96, 2, PT], F16)
        hidden, weighted = sb("hidden", [FE, 4, PT]), sb("weighted", [FE, 4, PT])
        y = sb("y", [128, PT])
        top, both = sb("top", [T, PAIR, C]), sb("both", [T, 2, PAIR, C])
        scaled, by_gamma, plus_beta = sb("scaled", [T, PAIR, C]), sb("by_gamma", [T, PAIR, C]), sb("plus_beta", [T, PAIR, C])
        result = sb("result", [T, 2, PAIR, C])
        h_ps, gate_bc = ps("h", [128, 2, 512]), ps("gate_bc", [128, 2, 512])
        y_ps, xt_ps, gate_ps = ps("y_ps", [128, 2, 512]), ps("xt_ps", [128, 512]), ps("gate_ps", [128, 512])
        back_ps = xt_ps[0:T, :].rearrange("p (j c) -> p j c", j=PAIR)
        ln1, ln2 = LayerNorm(nc, ctx, "m_ln", PAIR, 1e-5), LayerNorm(nc, ctx, "m_out_ln", PAIR, 1e-5)
        set_up = sem("set_up")
        turned, x1_done, x2_done = sem("turned"), sem("x1_done"), sem("x2_done")
        logits_full, logits_done, best_done, best_at_done = (
            sem("logits_full"), sem("logits_done"), sem("best_done"), sem("best_at_done"))
        at_done, behind_done, odds_done, total_done, share_done = (
            sem("at_done"), sem("behind_done"), sem("odds_done"), sem("total_done"), sem("share_done"))
        chosen_done, part_done, gates_done = sem("chosen_done"), sem("part_done"), sem("gates_done")
        gates_turned, gates_high, gates_low = sem("gates_turned"), sem("gates_high"), sem("gates_low")
        gate_full = sem("gate_full")
        up_full, relu_done, weighted_done, down_done = (
            sem("up_full"), sem("relu_done"), sem("weighted_done"), sem("down_done"))
        y_done, back_full, top_done, both_done = sem("y_done"), sem("back_full"), sem("top_done"), sem("both_done")
        by_gamma_done, plus_beta_done, result_done = sem("by_gamma_done"), sem("plus_beta_done"), sem("result_done")
        stored = [sem("stored0"), sem("stored1")]
        slots = NE
        out_rows = out.rearrange("b (k p) c -> p (b k) c", p=T)

        def weighing(s, has, lag):
            stage, e = (2, s - lag) if s >= lag else (3, s - lag + NE)
            return (stage, e) if has(stage, units) else None

        with nc.Block() as block:
            @block.gpsimd
            def _(pool):
                ln1.setup(pool, set_up)
                ln2.setup(pool, set_up)
                pool.wait_ge(set_up, 4)

                def step(unit, has, later):
                    if has(0, units):
                        ln1.root(pool, unit(0))
                    if has(4, units):
                        ln2.root(pool, unit(4))
                    if has(4, units):
                        d = unit(4)
                        pool.wait_ge(ln2.done, d + 1)
                        if later(4, 1):
                            pool.wait_ge(plus_beta_done, d.n)
                        pool.tensor_tensor(by_gamma[:], scaled[:], per_channel(g.rows[:, 10, :], PAIR), ALU.mult)\
                            .then_inc(by_gamma_done, 1)
                        pool.wait_ge(by_gamma_done, d + 1)
                        if later(4, 1):
                            pool.wait_ge(result_done, d.n)
                        pool.tensor_tensor(plus_beta[:], by_gamma[:], per_channel(g.rows[:, 11, :], PAIR), ALU.add)\
                            .then_inc(plus_beta_done, 1)
                        pool.wait_ge(plus_beta_done, d + 1)
                        if later(4, 2):
                            pool.wait_ge(stored[d.parity], 16 * d.half)
                        pool.tensor_tensor(result[:, d.parity], plus_beta[:], of_tiles(g.x, d, PAIR), ALU.add)\
                            .then_inc(result_done, 1)

                run_steps(pool, units + 4, 8, units, step, ways=4)

            @block.sync
            def _(sp):
                def step(unit, has, later):
                    if has(4, units):
                        d = unit(4)
                        sp.wait_ge(result_done, d + 1)
                        sp.dma_start(out_rows[:, bass.ds(d.n * PAIR, PAIR), :], result[:, d.parity])\
                          .then_inc(stored[d.parity], 16)

                run_steps(sp, units + 4, 8, units, step, ways=4)
                for s in stored:
                    sp.wait_ge(s, 16 * (units // 2))

            @block.scalar
            def _(act):
                def step(unit, has, later):
                    f, n, b, c, d = (unit(k) for k in range(5))
                    for s in range(slots):
                        if has(2, units):
                            act.wait_ge(up_full, NE * b.n + s + 1)
                            if s >= 4 or later(2, 1):
                                act.wait_ge(weighted_done, NE * b.n + s - 3)
                            act.activation(hidden[:, s % 4], h_ps[:, s % 2, 0:PT], ACT.Relu, bias=g.moe_b1[:, s:s + 1],
                                           scale=1.0 / WS).then_inc(relu_done, 1)
                        if s == 13 and has(0, units):
                            act.wait_ge(turned, f + 1)
                            if later(0, 4):
                                act.wait_ge(up_full, NE * (f - 3))
                            act.activation(x1[:, f.way], xt_ps[:, 0:PT], ACT.Copy).then_inc(x1_done, 1)
                        if s == 3 and has(3, units):
                            act.wait_ge(down_done, NE * c.n + NE)
                            if later(3, 1):
                                act.wait_ge(back_full, c.n)
                            act.activation(y[:], y_ps[:, c.parity, 0:PT], ACT.Copy).then_inc(y_done, 1)
                        if s == 1 and has(0, units):
                            if later(0, 2):
                                act.wait_ge(ln1.squares_summed, f - 1)
                            ln1.square(act, f)
                        if s == 2 and has(4, units):
                            if later(4, 2):
                                act.wait_ge(ln2.squares_summed, d - 1)
                            ln2.square(act, d)
                        if s == 5 and has(1, units):
                            act.wait_ge(behind_done, n + 1)
                            if later(1, 1):
                                act.wait_ge(share_done, 2 * n.n)
                            act.activation(odds[:], behind[:], ACT.Exp).then_inc(odds_done, 1)
                        if s == 12 and has(1, units):
                            act.wait_ge(gates_turned, n + 1)
                            act.activation(gate_rows[:, n.parity], gate_ps[0:96, 0:PT], ACT.Copy).then_inc(gates_high, 1)

                run_steps(act, units + 4, 8, units, step, ways=4)

            @block.vector
            def _(dve):
                def step(unit, has, later):
                    f, n, b, c, d = (unit(k) for k in range(5))
                    for s in range(slots):
                        if has(2, units):
                            dve.wait_ge(relu_done, NE * b.n + s + 1)
                            dve.wait_ge(gate_full, NE * b.n + s + 1)
                            if s >= 4 or later(2, 1):
                                dve.wait_ge(down_done, NE * b.n + s - 3)
                            dve.tensor_tensor(weighted[:, s % 4], gate_bc[:, s % 2, 0:PT], hidden[:, s % 4], ALU.mult)\
                               .then_inc(weighted_done, 1)
                        if s == 1 and has(4, units):
                            dve.wait_ge(both_done, d + 1)
                            ln2.center(dve, d, both[:, d.parity], later(4, 2))
                        if s == 13 and has(0, units):
                            dve.wait_ge(x1_done, f + 1)
                            dve.tensor_tensor(x2[:, f.way], xt_ps[:, 0:PT], x1[:, f.way], ALU.subtract)\
                               .then_inc(x2_done, 1)
                        if s == 0 and has(0, units):
                            ln1.center(dve, f, of_tiles(g.x, f, PAIR), later(0, 2))
                        if s == 1 and has(1, units):
                            dve.wait_ge(logits_full, n + 1)
                            if later(1, 1):
                                dve.wait_ge(best_at_done, 4 * n.n)
                            dve.scalar_tensor_tensor(
                                out=logits[:], in0=gate_ps[0:T, 0:PAIR * NE].rearrange("p (j e) -> p j e", j=PAIR),
                                scalar=1.0 / WS, in1=per_channel(g.gate_b[:], PAIR, NE), op0=ALU.mult, op1=ALU.add)\
                               .then_inc(logits_done, 1)
                        if s == 3:
                            if has(1, units):
                                dve.wait_ge(logits_done, n + 1)
                            if has(0, units):
                                ln1.sum_squares(dve, f)
                            if has(1, units):
                                for j in range(PAIR):
                                    dve.max(best[:, j, :], logits[:, j, :]).then_inc(best_done, 1)
                        if s == 4:
                            if has(1, units):
                                dve.wait_ge(best_done, 4 * n.n + 4)
                            if has(4, units):
                                ln2.sum_squares(dve, d)
                            if has(1, units):
                                for j in range(PAIR):
                                    dve.max_index(best_at[:, j, :], best[:, j, :], logits[:, j, :])\
                                       .then_inc(best_at_done, 1)
                                dve.tensor_tensor(behind[:], best[:, :, 1], best[:, :, 0], ALU.subtract)\
                                   .then_inc(behind_done, 1)
                        if s == 5 and has(1, units):
                            dve.wait_ge(best_at_done, 4 * n.n + 4)
                            dve.tensor_copy(at[:], best_at[:, :, 0:2]).then_inc(at_done, 1)
                        if s == 6 and has(1, units):
                            dve.wait_ge(odds_done, n + 1)
                            dve.tensor_scalar(total[:], odds[:], 1.0, None, ALU.add).then_inc(total_done, 1)
                            dve.wait_ge(at_done, n + 1)
                            for k in range(2):
                                dve.tensor_tensor(chosen[:, k], per_channel(g.iota[:], PAIR, NE),
                                                  bcast(at[:, :, k:k + 1], [T, PAIR, NE]), ALU.is_equal)\
                                   .then_inc(chosen_done, 1)
                            dve.wait_ge(total_done, n + 1)
                            dve.reciprocal(share[:, :, 0], total[:]).then_inc(share_done, 1)
                        if s == 7 and has(1, units):
                            dve.wait_ge(share_done, 2 * n.n + 1)
                            dve.tensor_tensor(share[:, :, 1], share[:, :, 0], odds[:], ALU.mult).then_inc(share_done, 1)
                        if s == 8 and has(1, units):
                            dve.wait_ge(share_done, 2 * n.n + 2)
                            dve.wait_ge(chosen_done, 2 * n.n + 2)
                            for k in range(2):
                                dve.tensor_tensor(part[:, k], chosen[:, k], bcast(share[:, :, k:k + 1], [T, PAIR, NE]),
                                                  ALU.mult).then_inc(part_done, 1)
                        if s == 9 and has(1, units):
                            dve.wait_ge(part_done, 2 * n.n + 2)
                            if later(1, 1):
                                dve.wait_ge(gates_turned, n.n)
                            six = [T, PAIR, 6, NE]
                            dve.tensor_tensor(gates[:], bcast(part[:, 0].unsqueeze(2), six),
                                              bcast(part[:, 1].unsqueeze(2), six), ALU.add).then_inc(gates_done, 1)
                        if s == 11 and has(4, units):
                            if later(4, 1):
                                dve.wait_ge(by_gamma_done, d.n)
                            ln2.scale(dve, d, scaled[:])
                        if s == 13 and has(1, units):
                            dve.wait_ge(gates_high, n + 1)
                            low = gate_rows[32:64, n.parity]
                            dve.tensor_tensor(low, gate_ps[32:64, 0:PT], low, ALU.subtract).then_inc(gates_low, 1)
                        if s == 7 and has(3, units):
                            dve.wait_ge(back_full, c + 1)
                            if later(3, 1):
                                dve.wait_ge(both_done, c.n)
                            if later(3, 2):
                                dve.wait_ge(ln2.centred, c - 1)
                            dve.tensor_tensor(top[:], back_ps[:, :, 0:C], xn[:, c.way], ALU.add).then_inc(top_done, 1)
                        if s == 8 and has(3, units):
                            dve.wait_ge(top_done, c + 1)
                            dve.tensor_tensor(both[:, c.parity], back_ps[:, :, C:2 * C], top[:], ALU.add)\
                               .then_inc(both_done, 1)
                        if s == 10 and has(0, units):
                            if later(0, 4):
                                dve.wait_ge(top_done, f - 3)
                            ln1.scale(dve, f, xn[:, f.way])

                run_steps(dve, units + 4, 8, units, step, ways=4)

            @block.tensor
            def _(pe):
                def step(unit, has, later):
                    f, n, b, c = (unit(k) for k in range(4))

                    def turn():
                        pe.wait_ge(ln1.done, f + 1)
                        if has(3, units):
                            pe.wait_ge(both_done, c + 1)
                        elif later(0, 1):
                            pe.wait_ge(x2_done, f.n)
                        for j in range(PAIR):
                            mm = turn_twice(pe, xt_ps[:, j * T:(j + 1) * T], xn[:, f.way, j, :], g)
                        mm.then_inc(turned, 1)

                    def gate():
                        pe.wait_ge(x2_done, n + 1)
                        if later(1, 1):
                            pe.wait_ge(gates_low, n.n)
                        for j in range(PAIR):
                            for k, x in enumerate((x1, x2)):
                                mm = pe.matmul(gate_ps[0:T, j * NE:(j + 1) * NE], x[:, n.way, j * T:(j + 1) * T],
                                               g.w_gate[:], start=(k == 0), stop=(k == 1))
                        mm.then_inc(logits_full, 1)

                    def turn_gates():
                        pe.wait_ge(gates_done, n + 1)
                        for j in range(PAIR):
                            mm = pe.transpose(gate_ps[0:96, j * T:(j + 1) * T],
                                              gates[:, j].rearrange("p k e -> p (k e)"), g.ident[0:T, 0:T])
                        mm.then_inc(gates_turned, 1)

                    def up(e):
                        if e >= 2 or later(2, 1):
                            pe.wait_ge(relu_done, NE * b.n + e - 1)
                        for k, x in enumerate((x1, x2)):
                            mm = pe.matmul(h_ps[:, e % 2, 0:PT], g.moe_w1[:, e, :], x[:, b.way], start=(k == 0), stop=(k == 1))
                        mm.then_inc(up_full, 1)

                    def spread_gate(e):
                        if e == 0:
                            pe.wait_ge(gates_low, b + 1)
                        if e >= 2 or later(2, 1):
                            pe.wait_ge(weighted_done, NE * b.n + e - 1)
                        pe.matmul(gate_bc[:, e % 2, 0:PT], g.selector[:, e, :], gate_rows[:, b.parity],
                                  start=True, stop=True).then_inc(gate_full, 1)

                    def down(s, stage, e):
                        u, half = unit(stage), e % 2
                        out = y_ps[half * C:(half + 1) * C, u.parity, 0:PT]
                        if e == 0:
                            if later(stage, 2):
                                pe.wait_ge(y_done, u - 1)
                            pe.matmul(out, g.moe_b2[:], gate_rows[:, u.parity], start=True, stop=False)
                        pe.wait_ge(weighted_done, NE * u.n + e + 1)
                        pe.matmul(out, g.moe_w2[:, e, :], weighted[:, e % 4], start=(e == 1), stop=(e >= NE - 2))\
                          .then_inc(down_done, 1)

                    def turn_back():
                        pe.wait_ge(y_done, c + 1)
                        if has(1, units):
                            pe.wait_ge(x2_done, n + 1)
                        elif later(3, 1):
                            pe.wait_ge(both_done, c.n)
                        for j in range(PAIR):
                            mm = pe.transpose(back_ps[:, j, :], y[:, j * T:(j + 1) * T], g.ident[:])
                        mm.then_inc(back_full, 1)

                    for s in range(slots):
                        if s == 12 and has(0, units):
                            turn()
                        if has(2, units):
                            up(s)
                        if weighing(s, has, DOWN_LAG):
                            down(s, *weighing(s, has, DOWN_LAG))
                        if has(2, units):
                            spread_gate(s)
                        if s == 0 and has(1, units):
                            gate()
                        if s == 5 and has(3, units):
                            turn_back()
                        if s == 11 and has(1, units):
                            turn_gates()

                run_steps(pe, units + 4, 8, units, step, ways=4)


_LOADS = {
    "item_emb": "L0_tok_item_emb", "pos_emb": "L0_tok_pos_emb", "ln0_w": "L0_tok_ln0_w", "ln0_b": "L0_tok_ln0_b",
    "fln_w": "L0_tok_fln_w", "fln_b": "L0_tok_fln_b", "d1_w": "L0_tok_d1_w",
    "d1_b": "L0_tok_d1_b", "d2_w": "L0_tok_d2_w", "d2_b": "L0_tok_d2_b", "iln_w": "L0_tok_iln_w",
    "iln_b": "L0_tok_iln_b", "Wq": "L0_attn_Wq", "Wk": "L0_attn_Wk", "Wv": "L0_attn_Wv", "Wo": "L0_attn_Wo",
    "bo": "L0_attn_bo", "gate_w": "L0_ffn_gate_w", "gate_b": "L0_ffn_gate_b", "w1": "L0_ffn_w1", "b1": "L0_ffn_b1",
    "w2": "L0_ffn_w2", "b2": "L0_ffn_b2", "gamma": "L0_ffn_gamma", "beta": "L0_ffn_beta",
}


class Names:
    pass


def build(nc, d, out):
    with ExitStack() as ctx:
        def sb(n, shape, dt=F32):
            return ctx.enter_context(nc.sbuf_tensor(n, shape, dt))

        g = Names()
        g.ctx, g.ffn_sems = ctx, {}
        g.x = sb("x_stream", [T, NT, C])
        g.ids = sb("ids_sb", [T, NT], I32)
        g.ident = sb("ident_sb", [128, 128])
        g.ident_ones = sb("ident_ones_sb", [T + 1, T], BF16)
        g.ones = sb("ones_sb", [T, DH])
        g.pos = sb("pos_sb", [T, 2, C])
        g.rows = sb("rows_sb", [T, 12, C])
        g.iota = sb("iota_sb", [T, NE])
        g.parity = sb("parity_sb", [C, 2])
        g.gate_b = sb("gate_b_sb", [T, NE])
        g.table_rows = sb("table_rows_sb", [T, NH, 3 * T], BF16)
        g.table_cols = sb("table_cols_sb", [T + 1, 2, 2, NH, 3 * T], BF16)
        g.selector = sb("selector_sb", [96, NE, 128], F16)
        g.ffn_w1 = sb("ffn_w1_sb", [2 * C, 2, DFF], F16)
        g.ffn_b1 = sb("ffn_b1_sb", [128, 2, 2])
        g.ffn_w2 = sb("ffn_w2_sb", [128, 2, 2, C])
        g.y_bias = sb("y_bias_sb", [128, 3])
        g.w_a = sb("w_a_sb", [2 * C, NH, 2 * C], F16)
        g.w_v = sb("w_v_sb", [2 * C, NH * DH], F16)
        g.w_o = sb("w_o_sb", [128, 2, C])
        g.w_gate = sb("w_gate_sb", [2 * C, NE], F16)
        g.moe_w1 = sb("moe_w1_sb", [2 * C, NE, FE], F16)
        g.moe_b1 = sb("moe_b1_sb", [128, NE])
        g.moe_w2 = sb("moe_w2_sb", [128, NE, C])
        g.moe_b2 = sb("moe_b2_sb", [96, C], F16)
        d.filters = nc.dram_tensor("kernels", [2, C, 2 * S], F32, kind="Internal").ap()
        prepare(nc, g, d)
        embed(nc, g, d)
        for l in range(2):
            spectral_filter(nc, g, d, l)
            feed_forward(nc, g, d, l)
        attention(nc, g, d)
        experts(nc, g, d, out)


def shape_constants():
    bf = mybir.dt.np(BF16)
    j, k = np.arange(2 * S)[None, :], np.arange(K)[:, None]
    weight = np.where((k == 0) | (k == S // 2), 1.0, 2.0) / S
    angle = 2 * np.pi * ((k * j) % S) / S
    sine = weight * np.where((k == 0) | (k == S // 2), 0.0, -np.sin(angle))
    dft = np.stack([weight * np.cos(angle), -sine, sine], 1).astype(np.float32)
    slopes = 2.0 ** -(np.arange(NH) + 1.0)
    q, s = np.arange(S)[:, None], np.arange(S)[None, :]
    bias = np.where(s <= q, slopes[:, None, None] * (s - q), NEG)
    table_rows = np.concatenate([bias[:, 0:T, 0:T], bias[:, T:S, 0:T], bias[:, T:S, T:S]], 2).transpose(1, 0, 2)
    keys = bias.transpose(2, 0, 1)
    table_cols = np.concatenate([keys[0:T], keys[T:S, :, T:S]], 2)
    selector = np.zeros((96, NE, 128), np.float16)
    for e in range(NE):
        selector[e, e] = 1
        selector[32 + e, e] = 1
    even = (np.arange(C) // NE) % 2 == 0
    return {
        "dft": dft, "table_rows": table_rows.astype(bf), "table_cols": table_cols.astype(bf), "selector": selector,
        "ident": np.eye(128, dtype=np.float32),
        "ident_ones": np.concatenate([np.eye(T), np.ones((1, T))]).astype(bf),
        "iota": np.tile(np.arange(NE, dtype=np.float32), (T, 1)),
        "parity": np.stack([even, ~even], 1).astype(np.float32),
    }


def kernel(**inputs):
    import concourse.bacc as bacc
    from concourse.bass_utils import run_bass_kernel_spmd

    nc = bacc.Bacc("TRN2", target_bir_lowering=False, num_devices=1)
    arrays = {name: np.ascontiguousarray(inputs[source]) for name, source in _LOADS.items()}
    arrays["ids"] = np.ascontiguousarray(np.asarray(inputs["x"]).reshape(B, 2, T).transpose(2, 0, 1).reshape(T, NT))
    arrays["cw"] = np.ascontiguousarray(np.asarray(inputs["L0_tok_cw"]).transpose(1, 0, 3, 2))
    arrays["d1_b"] = np.ascontiguousarray(arrays["d1_b"].reshape(2, 2, 128).transpose(2, 0, 1))
    arrays["b1"] = np.ascontiguousarray(arrays["b1"].T)
    arrays.update(shape_constants())
    d = Names()
    for name, a in arrays.items():
        d.__dict__[name] = nc.dram_tensor(f"in_{name}", a.shape, mybir.dt.from_np(a.dtype), kind="ExternalInput").ap()
    out = nc.dram_tensor("out", (B, S, C), F32, kind="ExternalOutput").ap()
    build(nc, d, out)
    result = run_bass_kernel_spmd(nc, [{f"in_{name}": a for name, a in arrays.items()}], core_ids=[0])
    return result.results[0]["out"]
```

```python
from contextlib import ExitStack

import numpy as np

import concourse.bass as bass
from concourse import mybir

F32, F16, BF16 = mybir.dt.float32, mybir.dt.float16, mybir.dt.bfloat16
I32, U32 = mybir.dt.int32, mybir.dt.uint32
ALU = mybir.AluOpType
ACT = mybir.ActivationFunctionType
AX = mybir.AxisListType

B, S, C = 128, 200, 64
T = 100
NT = B * S // T
DFF = 256
NH, DH = 8, 32
NE, FE = 16, 128
K = S // 2 + 1
WS = 64.0
QUAD = 8
PAIR = 4
PT = PAIR * T
CH = 4
NEG = -1.0e30
KEY_LAG = 5
WHOLE = 10
DOWN_LAG = 4


class Unit:

    def __init__(self, r, c, ways=2):
        self.half, self.parity = r * (ways // 2) + c // 2, c % 2
        self.lap, self.way = r + c // ways, c % ways
        self.n = r * ways + c

    def __add__(self, k):
        return self.n + k

    def __sub__(self, k):
        return self.n - k


def run_steps(eng, steps, first, last, body, start=0, ways=2):
    def straight(t):
        body(lambda lag: Unit((start + t - lag) // ways, (start + t - lag) % ways, ways),
             lambda lag, units: 0 <= t - lag < units, lambda lag, n: t - lag >= n)

    for t in range(first):
        straight(t)
    with eng.Fori((start + first) // ways, (start + last) // ways) as r:
        for c in range(ways):
            body(lambda lag: Unit(r, c - lag, ways), lambda lag, units: True, lambda lag, n: True)
    for t in range(last, steps):
        straight(t)


def bcast(ap, shape):
    return ap.to_broadcast(shape)


def turn_twice(pe, out, tile, g):
    for half in range(2):
        mm = pe.matmul(out[half * C:(half + 1) * C], tile, g.ident[0:T, 0:T], start=True, stop=True)
    return mm


class LayerNorm:

    def __init__(self, nc, ctx, name, tiles, eps, sem=None):
        def sb(n, shape):
            return ctx.enter_context(nc.sbuf_tensor(f"{name}_{n}", shape, F32))

        def own(n):
            return ctx.enter_context(nc.semaphore(f"{name}_{n}"))

        sem = sem or own
        self.tiles, self.eps = tiles, eps
        self.shape = [T, tiles, C]
        self.sums = sb("sums", [T, 2, tiles])
        self.squares = sb("squares", [T, 2, tiles])
        self.shifted = sb("shifted", [T, 2, tiles])
        self.power, self.shift = sb("power", [T, tiles]), sb("shift", [T, tiles])
        self.rstd = sb("rstd", [T, 2, tiles])
        self.centered = sb("centered", [T, 2, tiles, C])
        self.squared = sb("squared", [T, 2, tiles, C])
        self.summed, self.centred, self.square_done = sem("summed"), sem("centred"), sem("square_done")
        self.squares_summed, self.shift_done, self.rstd_done = sem("squares_summed"), sem("shift_done"), sem("rstd_done")
        self.done = sem("done")

    def setup(self, pool, signal):
        pool.memset(self.power[:], -0.5).then_inc(signal, 1)
        pool.memset(self.shift[:], self.eps).then_inc(signal, 1)

    def per_token(self, t):
        return bcast(t.unsqueeze(2), self.shape)

    def center(self, dve, u, x, free):
        if free:
            dve.wait_ge(self.done, u - 1)
        dve.tensor_reduce(self.sums[:, u.parity], x, AX.X, ALU.add).then_inc(self.summed, 1)
        dve.wait_ge(self.summed, u + 1)
        dve.scalar_tensor_tensor(out=self.centered[:, u.parity], in0=self.per_token(self.sums[:, u.parity]),
                                 scalar=-1.0 / C, in1=x, op0=ALU.mult, op1=ALU.add).then_inc(self.centred, 1)

    def square(self, act, u):
        act.wait_ge(self.centred, u + 1)
        act.activation(self.squared[:, u.parity], self.centered[:, u.parity], ACT.Square, scale=float(C) ** -0.5)\
           .then_inc(self.square_done, 1)

    def sum_squares(self, dve, u):
        dve.wait_ge(self.square_done, u + 1)
        dve.tensor_reduce(self.squares[:, u.parity], self.squared[:, u.parity], AX.X, ALU.add)\
           .then_inc(self.squares_summed, 1)

    def add_eps(self, eng, u):
        eng.wait_ge(self.squares_summed, u + 1)
        eng.tensor_tensor(self.shifted[:, u.parity], self.squares[:, u.parity], self.shift[:], ALU.add)\
           .then_inc(self.shift_done, 1)

    def root(self, pool, u):
        pool.wait_ge(self.shift_done, u + 1)
        pool.tensor_tensor(self.rstd[:, u.parity], self.shifted[:, u.parity], self.power[:], ALU.pow)\
            .then_inc(self.rstd_done, 1)

    def scale(self, eng, u, out):
        eng.wait_ge(self.rstd_done, u + 1)
        eng.tensor_tensor(out, self.centered[:, u.parity], self.per_token(self.rstd[:, u.parity]), ALU.mult)\
           .then_inc(self.done, 1)


def per_channel(row, tiles, n=C):
    return bcast(row.unsqueeze(1), [T, tiles, n])


def of_tiles(x, u, tiles, start=0):
    return x[:, bass.ds((u - start) * tiles, tiles), :]


def width(ap):
    return int(np.prod(ap.shape[1:]))


def prepare_and_embed(nc, g, d):
    units = NT // QUAD
    with ExitStack() as ctx:
        def sb(n, shape, dt=F32):
            return ctx.enter_context(nc.sbuf_tensor(n, shape, dt))

        def ps(n, shape):
            return ctx.enter_context(nc.psum_tensor(n, shape, F32))

        def sem(n):
            return ctx.enter_context(nc.semaphore(n))

        splits = [(g.ffn_w1[:, l, :], d.d1_w[l]) for l in range(2)]
        splits += [(g.w_v[:], d.Wv), (g.w_gate[:], d.gate_w),
                   (g.moe_w1[:].rearrange("p e f -> p (e f)"), d.w1)]
        staged = [sb(f"stage{n}", [2 * C, width(s)]) for n, (s, _) in enumerate(splits)]
        wq, wk = sb("wq", [C, NH * DH]), sb("wk", [C, NH * DH])
        wqT, wkT = sb("wqT", [DH, NH, 2, C]), sb("wkT", [DH, NH, 2, C])
        b2, b2_high, b2_low, b2_even = (sb("b2", [C, C]), sb("b2_high", [C, C], F16), sb("b2_low", [C, C]),
                                        sb("b2_even", [C, C]))
        freq = sb("freq", [K, 2, 2, C])
        dft = sb("dft", [K, 3, 2 * S])
        kernel2 = sb("kernel2", [C, 2, 2 * S])
        tp = ps("tp", [C, 2, 512])
        ap = ps("ap", [2 * C, 2, 512])
        kp = ps("kp", [C, 2, 512])

        index = sb("index", [T, 4, QUAD], I32)
        found = sb("found", [T, 4, QUAD, C])
        placed = sb("placed", [T, 2, QUAD, C])
        root = sb("root", [T, 2, QUAD])
        scaled = sb("scaled", [T, 2, QUAD, C])
        weighted = sb("weighted", [T, 2, QUAD, C])
        ln = LayerNorm(nc, ctx, "ln0", QUAD, 1e-12)
        ids_in, index_ready, found_in = sem("ids_in"), sem("index_ready"), [sem(f"found_in{n}") for n in range(4)]
        placed_done, root_done, weighted_done, embedded = (
            sem("placed_done"), sem("root_done"), sem("weighted_done"), sem("embedded"))

        staged_in, heads_in, freq_in = sem("staged_in"), sem("heads_in"), sem("freq_in")
        tables_in, b2_in = sem("tables_in"), sem("b2_in")
        set_up, high_done, splits_done = sem("set_up"), sem("high_done"), sem("splits_done")
        turned, turned_copied, folded, fold_high = sem("turned"), sem("turned_copied"), sem("folded"), sem("fold_high")
        kernel_done, kernel_copied, kernel_out = sem("kernel_done"), sem("kernel_copied"), sem("kernel_out")
        impulse_added = sem("impulse_added")
        b2_split, b2_parts = sem("b2_split"), sem("b2_parts")

        sp_loads = [(g.ffn_w2[:, l], d.d2_w[l].rearrange("(f p) h -> p f h", p=128)) for l in range(2)]
        sp_loads += [(g.ffn_b1[:], d.d1_b)]
        sp_loads += [(g.w_o[:], d.Wo.rearrange("(f p) h -> p f h", p=128)),
                     (g.moe_w2[:], d.w2.rearrange("e f h -> f e h")),
                     (g.moe_b1[:], d.b1)]
        act_loads = [(g.y_bias[0:C, n:n + 1], src.unsqueeze(1)) for n, src in enumerate((d.d2_b[0], d.d2_b[1], d.bo))]
        act_loads += [(g.pos[:], d.pos_emb.rearrange("(k p) c -> p k c", p=T)),
                      (g.table_rows[:], d.table_rows), (g.selector[:], d.selector), (g.fold[:], d.fold), (g.ident_ones[:], d.ident_ones),
                      (g.iota[:], d.iota), (g.gate_b[:], bcast(d.gate_b.unsqueeze(0), [T, NE]))]
        act_loads += [(g.rows[:, n, :], bcast(src.unsqueeze(0), [T, C])) for n, src in enumerate(
            (d.ln0_w, d.ln0_b, d.fln_w[0], d.fln_w[1], d.fln_b[0], d.fln_b[1],
             d.iln_w[0], d.iln_w[1], d.iln_b[0], d.iln_b[1], d.gamma, d.beta))]
        act_loads += [(g.table_cols[0:T, par, b], d.table_cols) for par in range(2) for b in range(2)]

        with nc.Block() as block:
            @block.sync
            def _(sp):
                sp.dma_start(g.ids[:], d.ids).then_inc(ids_in, 16)
                sp.dma_start(g.ident[:], d.ident).then_inc(heads_in, 16)
                sp.dma_start(wq[:], d.Wq).then_inc(heads_in, 16)
                sp.dma_start(wk[:], d.Wk).then_inc(heads_in, 16)
                sp.dma_start(freq[:], d.cw).then_inc(freq_in, 16)
                sp.dma_start(dft[:], d.dft).then_inc(freq_in, 16)
                for stage, (_, source) in zip(staged, splits):
                    for half in range(2):
                        part = stage[half * C:(half + 1) * C, :]
                        if len(source.shape) == 3:
                            part, source_ = part.rearrange("p (e f) -> p e f", e=NE), source.rearrange("e h f -> h e f")
                        else:
                            source_ = source
                        sp.dma_start(part, source_).then_inc(staged_in, 16)
                for dst, src in sp_loads:
                    sp.dma_start(dst, src).then_inc(tables_in, 16)
                sp.wait_ge(impulse_added, 1)
                sp.dma_start(d.filters.rearrange("l c j -> c l j"), kernel2[:]).then_inc(kernel_out, 16)
                sp.wait_ge(kernel_out, 16)
                for n in range(2):
                    load_circulant(sp, g, d, 0, n, n)
                sp.wait_ge(tables_in, 16 * (len(sp_loads) + len(act_loads)))

            @block.scalar
            def _(act):
                act.dma_start(g.parity[:], d.parity).then_inc(b2_in, 16)
                for q in range(4):
                    act.dma_start(b2[NE * q:NE * q + NE, :], d.b2).then_inc(b2_in, 16)
                act.wait_ge(set_up, 5)
                for dst, src in act_loads:
                    act.dma_start(dst, src).then_inc(tables_in, 16)
                act.wait_ge(staged_in, 16 * 2 * len(splits))
                for stage, (dst, _) in zip(staged, splits):
                    act.activation(dst, stage[:], ACT.Copy, scale=WS).then_inc(high_done, 1)
                act.wait_ge(folded, NH)
                for n in range(2):
                    act.activation(g.w_a[:, 4 * n:4 * n + 4, :], ap[:, n, :].rearrange("p (h c) -> p h c", h=4),
                                   ACT.Copy, scale=WS * DH ** -0.5).then_inc(fold_high, 1)
                act.wait_ge(kernel_done, 2)
                for l in range(2):
                    act.activation(kernel2[:, l, :], kp[:, l, 0:2 * S], ACT.Copy).then_inc(kernel_copied, 1)
                act.wait_ge(b2_in, 80)
                act.activation(b2_high[:], b2[:], ACT.Copy).then_inc(b2_split, 1)

                def step(unit, has, later):
                    if has(0, units):
                        u = unit(0)
                        if later(0, 2):
                            act.wait_ge(ln.squares_summed, u - 1)
                        ln.square(act, u)
                    if has(1, units):
                        u = unit(1)
                        act.wait_ge(ln.squares_summed, u + 1)
                        if later(1, 2):
                            act.wait_ge(ln.rstd_done, u - 1)
                        act.activation(root[:, u.parity], ln.squares[:, u.parity], ACT.Sqrt, bias=ln.shift[:, 0:1])\
                           .then_inc(root_done, 1)

                run_steps(act, units + 2, 4, units, step, ways=4)

            @block.vector
            def _(dve):
                for n, (stage, (dst, _)) in enumerate(zip(staged, splits)):
                    dve.wait_ge(high_done, n + 1)
                    dve.scalar_tensor_tensor(out=dst[C:2 * C], in0=stage[C:2 * C, :], scalar=WS, in1=dst[C:2 * C],
                                             op0=ALU.mult, op1=ALU.subtract).then_inc(splits_done, 1)
                for n in range(2):
                    dve.wait_ge(turned, NH * (n + 1))
                    dst, src = (wqT, wkT)[n], tp[0:DH, n, 0:NH * C].rearrange("p (h c) -> p h c", h=NH)
                    for twice in range(2):
                        dve.tensor_copy(dst[:, :, twice, :], src).then_inc(turned_copied, 1)
                for n in range(2):
                    dve.wait_ge(fold_high, n + 1)
                    half = g.w_a[C:2 * C, 4 * n:4 * n + 4, :]
                    dve.scalar_tensor_tensor(out=half, in0=ap[C:2 * C, n, :].rearrange("p (h c) -> p h c", h=4),
                                             scalar=WS * DH ** -0.5, in1=half,
                                             op0=ALU.mult, op1=ALU.subtract).then_inc(splits_done, 1)
                dve.wait_ge(kernel_copied, 2)
                dve.tensor_scalar(kernel2[:, :, 0:2 * S:S], kernel2[:, :, 0:2 * S:S], 1.0, None, ALU.add)\
                   .then_inc(impulse_added, 1)
                dve.wait_ge(b2_split, 1)
                dve.wait_ge(b2_in, 80)
                dve.wait_ge(set_up, 5)
                dve.tensor_tensor(b2_low[:], b2[:], b2_high[:], ALU.subtract).then_inc(b2_parts, 1)
                dve.tensor_scalar(b2_even[:], b2_high[:], g.parity[:, 0:1], None, ALU.mult).then_inc(b2_parts, 1)
                dve.wait_ge(b2_parts, 2)
                dve.scalar_tensor_tensor(out=g.moe_b2[0:C, :], in0=b2_low[:], scalar=g.parity[:, 1:2], in1=b2_even[:],
                                         op0=ALU.mult, op1=ALU.add).then_inc(b2_parts, 1)
                dve.wait_ge(tables_in, 16 * (len(sp_loads) + len(act_loads)))

                def step(unit, has, later):
                    if has(2, units):
                        u = unit(2)
                        dve.wait_ge(root_done, u + 1)
                        dve.reciprocal(ln.rstd[:, u.parity], root[:, u.parity]).then_inc(ln.rstd_done, 1)
                        ln.scale(dve, u, scaled[:, u.parity])
                        dve.wait_ge(ln.done, u + 1)
                        dve.tensor_tensor(weighted[:, u.parity], scaled[:, u.parity], per_channel(g.rows[:, 0, :], QUAD),
                                          ALU.mult).then_inc(weighted_done, 1)
                        dve.wait_ge(weighted_done, u + 1)
                        dve.tensor_tensor(of_tiles(g.x, u, QUAD), weighted[:, u.parity],
                                          per_channel(g.rows[:, 1, :], QUAD), ALU.add).then_inc(embedded, 1)
                    if has(0, units):
                        u = unit(0)
                        dve.wait_ge(found_in[u.way], 16 * QUAD * u.lap + 16 * QUAD)
                        if later(0, 2):
                            dve.wait_ge(ln.centred, u - 1)
                        pos = g.pos[:].unsqueeze(1).to_broadcast([T, QUAD // 2, 2, C])
                        dve.tensor_tensor(placed[:, u.parity].rearrange("p (b k) c -> p b k c", k=2),
                                          found[:, u.way].rearrange("p (b k) c -> p b k c", k=2), pos,
                                          ALU.add).then_inc(placed_done, 1)
                        dve.wait_ge(placed_done, u + 1)
                        ln.center(dve, u, placed[:, u.parity], later(0, 2))
                        ln.sum_squares(dve, u)

                run_steps(dve, units + 2, 4, units, step, ways=4)

            @block.gpsimd
            def _(pool):
                pool.memset(g.y_bias[:], 0.0).then_inc(set_up, 1)
                pool.memset(g.ones[:], 1.0).then_inc(set_up, 1)
                pool.memset(g.moe_b2[:], 0.0).then_inc(set_up, 1)
                ln.setup(pool, set_up)
                pool.wait_ge(set_up, 5)
                pool.wait_ge(ids_in, 16)

                def step(unit, has, later):
                    if has(1, units):
                        pool.wait_ge(index_ready, unit(1) + 1)
                    if has(0, units):
                        u = unit(0)
                        if later(0, 4):
                            pool.wait_ge(placed_done, u - 3)
                        pool.tensor_copy(index[:, u.way], g.ids[:, bass.ds(u.n * QUAD, QUAD)]).then_inc(index_ready, 1)
                    if has(1, units):
                        u = unit(1)
                        for j in range(QUAD):
                            pool.indirect_dma_start(
                                out=found[:, u.way, j, :], out_offset=None, in_=d.item_emb,
                                in_offset=bass.IndirectOffsetOnAxis(ap=index[:, u.way, j:j + 1], axis=0),
                            ).then_inc(found_in[u.way], 16)

                run_steps(pool, units + 1, 4, units, step, ways=4)

            @block.tensor
            def _(pe):
                pe.wait_ge(heads_in, 48)
                for n, w in enumerate((wq, wk)):
                    for h in range(NH):
                        pe.transpose(tp[0:DH, n, h * C:(h + 1) * C], w[:, h * DH:(h + 1) * DH], g.ident[0:C, 0:C])\
                          .then_inc(turned, 1)
                pe.wait_ge(turned_copied, 4)
                for h in range(NH):
                    pe.matmul(ap[:, h // 4, (h % 4) * 2 * C:(h % 4 + 1) * 2 * C],
                              wqT[:, h, :, :].rearrange("p a c -> p (a c)"),
                              wkT[:, h, :, :].rearrange("p a c -> p (a c)"), start=True, stop=True).then_inc(folded, 1)
                pe.wait_ge(freq_in, 32)
                for l in range(2):
                    for part in range(2):
                        mm = pe.matmul(kp[:, l, 0:2 * S], freq[:, l, part, :], dft[:, part and part + l, :],
                                       start=(part == 0), stop=(part == 1))
                    mm.then_inc(kernel_done, 1)


def load_circulant(sp, g, d, l, parity, n):
    rows = d.filters[l]
    rows = bass.AP(tensor=rows.tensor, offset=rows.offset + 1, ap=[[1, T], [2 * S, C], [1, S]])
    sp.dma_start(g.circulant[:, parity], rows[:, bass.ds(n * CH, CH), :]).then_inc(g.circulant_in[parity], 16)


def spectral_filter(nc, g, d, l):
    units = C // CH
    start = l * units
    with ExitStack() as ctx:
        def sem(n):
            return ctx.enter_context(nc.semaphore(f"{n}_{l}"))

        circulant = g.circulant
        conv = ctx.enter_context(nc.psum_tensor(f"conv{l}", [T, 2, 2, CH, B], F32))
        convolved = sem("convolved")
        stored = [sem("filtered_first"), sem("filtered_second")]
        x = g.x[:].rearrange("p (b k) c -> p k b c", k=2)

        with nc.Block() as block:
            @block.sync
            def _(sp):
                def step(unit, has, later):
                    u = unit(0)
                    if later(0, 2):
                        sp.wait_ge(convolved, u - 1 - start)
                        load_circulant(sp, g, d, l, u.parity, u - start)

                run_steps(sp, units, 4, units, step, start)

            @block.tensor
            def _(pe):
                def step(unit, has, later):
                    u = unit(0)
                    pe.wait_ge(g.circulant_in[u.parity], 16 * u.half + 16)
                    if later(0, 2):
                        pe.wait_ge(stored[0], u - 1 - start)
                        pe.wait_ge(stored[1], u - 1 - start)
                    for c in range(CH):
                        for k in range(2):
                            for stay in range(2):
                                source = x[:, k if stay else 1 - k, :, bass.ds((u - start) * CH + c, 1)]
                                mm = pe.matmul(conv[:, u.parity, k, c, :],
                                               circulant[:, u.parity, c, stay * T:(stay + 1) * T],
                                               source.rearrange("p b c -> p (b c)"),
                                               start=(stay == 0), stop=(stay == 1))
                    mm.then_inc(convolved, 1)

                run_steps(pe, units, 4, units, step, start)

            def result(u, k):
                return conv[:, u.parity, k].rearrange("p c b -> p b c")

            @block.vector
            def _(dve):
                def step(unit, has, later):
                    u = unit(0)
                    dve.wait_ge(convolved, u + 1 - start)
                    dve.tensor_copy(x[:, 0, :, bass.ds((u - start) * CH, CH)], result(u, 0)).then_inc(stored[0], 1)

                run_steps(dve, units, 4, units, step, start)

            @block.scalar
            def _(act):
                def step(unit, has, later):
                    u = unit(0)
                    act.wait_ge(convolved, u + 1 - start)
                    act.activation(x[:, 1, :, bass.ds((u - start) * CH, CH)], result(u, 1), ACT.Copy).then_inc(stored[1], 1)

                run_steps(act, units, 4, units, step, start)


def feed_forward(nc, g, d, l):
    units = NT // QUAD
    start = l * units
    with ExitStack() as ctx:
        def sb(n, shape, dt=F32):
            return ctx.enter_context(nc.sbuf_tensor(f"{n}_{l}", shape, dt))

        def ps(n, shape):
            return ctx.enter_context(nc.psum_tensor(f"{n}_{l}", shape, F32))

        def sem(n):
            if n not in g.ffn_sems:
                g.ffn_sems[n] = g.ctx.enter_context(nc.semaphore(n))
            return g.ffn_sems[n]

        scaled, weighted = sb("f_scaled", [T, 2, QUAD, C]), sb("f_weighted", [T, 2, QUAD, C])
        base = sb("f_base", [T, 4, QUAD, C])
        x1, x2 = sb("f_x1", [2 * C, 2, 2, PT], F16), sb("f_x2", [2 * C, 2, 2, PT], F16)
        hidden = sb("f_hidden", [128, 2, 2, 2, PT])
        y = sb("f_y", [128, 2, PT])
        scaled2, weighted2 = sb("f_scaled2", [T, 2, QUAD, C]), sb("f_weighted2", [T, 2, QUAD, C])
        xt_ps = ps("f_xt", [128, 2, 512])
        h_ps = ps("f_h", [128, 4, 512])
        y_ps = ps("f_yps", [128, 512])
        back_ps = ps("f_back", [T, QUAD, C])
        ln1 = LayerNorm(nc, ctx, f"fln{l}", QUAD, 1e-12, lambda n: sem(f"f_ln_{n}"))
        ln2 = LayerNorm(nc, ctx, f"iln{l}", QUAD, 1e-12, lambda n: sem(f"f_ln2_{n}"))
        set_up, weighted_done, base_done = sem("f_set_up"), sem("f_weighted_done"), sem("f_base_done")
        turned, x1_done, x2_done = sem("f_turned"), sem("f_x1_done"), sem("f_x2_done")
        up_done, gelu_done, down_done, y_done = sem("f_up_done"), sem("f_gelu_done"), sem("f_down_done"), sem("f_y_done")
        back_done = sem("f_back_done")
        weighted2_done, stored = sem("f_weighted2_done"), sem("f_stored")

        with nc.Block() as block:
            @block.sync
            def _(sp):
                if l == 0:
                    for n in range(2):
                        load_circulant(sp, g, d, 1, n, n)

            @block.gpsimd
            def _(pool):
                ln1.setup(pool, set_up)
                ln2.setup(pool, set_up)
                pool.wait_ge(set_up, 4 * (l + 1))

                def step(unit, has, later):
                    f, n, d = unit(0), unit(1), unit(4)
                    if has(4, units):
                        ln2.root(pool, d)
                    if has(1, units):
                        pool.wait_ge(ln1.done, n + 1)
                        if later(1, 2):
                            pool.wait_ge(base_done, n - 1)
                        pool.tensor_tensor(weighted[:, n.parity], scaled[:, n.parity],
                                           per_channel(g.rows[:, 2 + l, :], QUAD), ALU.mult).then_inc(weighted_done, 1)
                    if has(4, units):
                        pool.wait_ge(ln2.done, d + 1)
                        if later(4, 2):
                            pool.wait_ge(stored, d - 1)
                        pool.tensor_tensor(weighted2[:, d.parity], scaled2[:, d.parity],
                                           per_channel(g.rows[:, 6 + l, :], QUAD), ALU.mult).then_inc(weighted2_done, 1)
                        pool.wait_ge(weighted2_done, d + 1)
                        pool.tensor_tensor(of_tiles(g.x, d, QUAD, start), weighted2[:, d.parity],
                                           per_channel(g.rows[:, 8 + l, :], QUAD), ALU.add).then_inc(stored, 1)
                    if has(0, units):
                        ln1.root(pool, f)

                run_steps(pool, units + 4, 8, units, step, start, 4)

            @block.vector
            def _(dve):
                dve.wait_ge(set_up, 4 * (l + 1))

                def step(unit, has, later):
                    f, n, b, c, d = (unit(k) for k in range(5))
                    if has(0, units):
                        ln1.center(dve, f, of_tiles(g.x, f, QUAD, start), later(0, 2))
                    if has(4, units):
                        ln2.sum_squares(dve, d)
                        ln2.add_eps(dve, d)
                    if has(1, units):
                        if later(1, 2):
                            dve.wait_ge(weighted_done, n - 1)
                        ln1.scale(dve, n, scaled[:, n.parity])
                    if has(2, units):
                        for q in range(2):
                            dve.wait_ge(x1_done, 2 * b.n + q + 1)
                            dve.tensor_tensor(x2[:, b.parity, q], xt_ps[:, q, 0:PT], x1[:, b.parity, q],
                                              ALU.subtract).then_inc(x2_done, 1)
                    if has(4, units):
                        if later(4, 2):
                            dve.wait_ge(weighted2_done, d - 1)
                        ln2.scale(dve, d, scaled2[:, d.parity])
                    if has(0, units):
                        ln1.sum_squares(dve, f)
                        ln1.add_eps(dve, f)
                    if has(1, units):
                        dve.wait_ge(weighted_done, n + 1)
                        if later(1, 4):
                            dve.wait_ge(back_done, 2 * (n - 3))
                        dve.tensor_tensor(base[:, n.way], weighted[:, n.parity],
                                          per_channel(g.rows[:, 4 + l, :], QUAD), ALU.add).then_inc(base_done, 1)
                    if has(3, units):
                        dve.wait_ge(back_done, 2 * c.n + 2)
                        ln2.center(dve, c, back_ps[:], later(3, 2))

                run_steps(dve, units + 4, 8, units, step, start, 4)

            @block.scalar
            def _(act):
                def step(unit, has, later):
                    f, b, c = unit(0), unit(2), unit(3)

                    def high(q):
                        act.wait_ge(turned, 2 * b.n + q + 1)
                        if q == 0 and later(2, 2):
                            act.wait_ge(up_done, 4 * (b - 1))
                        act.activation(x1[:, b.parity, q], xt_ps[:, q, 0:PT], ACT.Copy).then_inc(x1_done, 1)

                    def gelu(q):
                        for half in range(2):
                            act.wait_ge(up_done, 4 * b.n + 2 * q + half + 1)
                            if later(2, 2):
                                act.wait_ge(down_done, 2 * b.n + q - 3)
                            act.activation(hidden[:, b.parity, q, half], h_ps[:, 2 * q + half, 0:PT], ACT.Gelu,
                                           bias=g.ffn_b1[:, l, half:half + 1], scale=1.0 / WS).then_inc(gelu_done, 1)

                    def out_y(q):
                        act.wait_ge(down_done, 2 * c.n + q + 1)
                        if later(3, 1):
                            act.wait_ge(back_done, 2 * c.n + q - 1)
                        act.activation(y[:, q], y_ps[:, 0:PT], ACT.Identity, bias=g.y_bias[:, l:l + 1]).then_inc(y_done, 1)

                    if has(3, units):
                        out_y(0)
                    if has(2, units):
                        high(0)
                        high(1)
                    if has(3, units):
                        out_y(1)
                    if has(0, units):
                        if later(0, 2):
                            act.wait_ge(ln1.squares_summed, f - 1)
                        ln1.square(act, f)
                    if has(2, units):
                        gelu(0)
                        gelu(1)
                    if has(3, units):
                        if later(3, 2):
                            act.wait_ge(ln2.squares_summed, c - 1)
                        ln2.square(act, c)

                run_steps(act, units + 4, 8, units, step, start, 4)

            @block.tensor
            def _(pe):
                def step(unit, has, later):
                    b, c = unit(2), unit(3)

                    def turn(q):
                        if q == 0:
                            pe.wait_ge(base_done, b + 1)
                        if later(2, 1):
                            pe.wait_ge(x2_done, 2 * b.n - 1 + q)
                        for j in range(PAIR):
                            mm = turn_twice(pe, xt_ps[:, q, j * T:(j + 1) * T], base[:, b.way, q * PAIR + j, :], g)
                        mm.then_inc(turned, 1)

                    def up(q):
                        pe.wait_ge(x2_done, 2 * b.n + q + 1)
                        if later(2, 1):
                            pe.wait_ge(gelu_done, 4 * b.n + 2 * q - 2)
                        for half in range(2):
                            w = g.ffn_w1[:, l, half * 128:(half + 1) * 128]
                            out = h_ps[:, 2 * q + half, 0:PT]
                            pe.matmul(out, w, x1[:, b.parity, q], start=True, stop=False)
                            pe.matmul(out, w, x2[:, b.parity, q], start=False, stop=True).then_inc(up_done, 1)

                    def down(q):
                        pe.wait_ge(gelu_done, 4 * c.n + 2 * q + 2)
                        if q == 1:
                            pe.wait_ge(y_done, 2 * c.n + 1)
                        elif later(3, 1):
                            pe.wait_ge(y_done, 2 * c.n)
                        for half in range(2):
                            mm = pe.matmul(y_ps[half * C:(half + 1) * C, 0:PT], g.ffn_w2[:, l, half, :],
                                           hidden[:, c.parity, q, half], start=True, stop=True)
                        mm.then_inc(down_done, 1)

                    def back(q):
                        pe.wait_ge(y_done, 2 * c.n + q + 1)
                        if q == 0 and later(3, 1):
                            pe.wait_ge(ln2.centred, c.n)
                        for j in range(PAIR):
                            tile = q * PAIR + j
                            pe.matmul(back_ps[:, tile, :], y[:, q, j * T:(j + 1) * T], g.fold[:, 0, :],
                                      start=True, stop=False)
                            mm = pe.matmul(back_ps[:, tile, :], g.ident[0:T, 0:T], base[:, c.way, tile, :],
                                           start=False, stop=True)
                        mm.then_inc(back_done, 1)

                    if has(3, units):
                        down(0)
                    if has(2, units):
                        turn(0)
                        turn(1)
                    if has(3, units):
                        down(1)
                        back(0)
                    if has(2, units):
                        up(0)
                    if has(3, units):
                        back(1)
                    if has(2, units):
                        up(1)

                run_steps(pe, units + 4, 8, units, step, start, 4)


def attention(nc, g, d):
    units = NT // PAIR
    with ExitStack() as ctx:
        def sb(n, shape, dt=F32):
            return ctx.enter_context(nc.sbuf_tensor(f"a_{n}", shape, dt))

        def ps(n, shape):
            return ctx.enter_context(nc.psum_tensor(f"a_{n}", shape, F32))

        def sem(n):
            return ctx.enter_context(nc.semaphore(f"a_{n}"))

        xn = sb("xn", [T, 2, PAIR, C])
        x1, x2 = sb("x1", [2 * C, 4, PT], F16), sb("x2", [2 * C, 4, PT], F16)
        gs = sb("gs", [2 * C, 2, NH, PT], F16)
        v = sb("v", [T, 2, PAIR, NH * DH])
        block_max = sb("block_max", [T, 2, NH, 3])
        row_max = sb("row_max", [T, 96])
        max_rows = sb("max_rows", [48, 2, T], BF16)
        probs = sb("probs", [T, 8, 4 * T])
        log_sum, inv_sum = sb("log_sum", [128, 2, S]), sb("inv_sum", [128, 2, S])
        heads_out = sb("heads_out", [128, 2, PT])
        y = sb("y", [128, PT])
        proj = ps("proj", [128, 2, 512])
        max_ps = ps("max_ps", [T, 2, 512])
        score_ps = ps("score_ps", [T, 2, 512])
        pv_ps = ps("pv_ps", [128, 2, 512])
        back_ps = proj[0:T, 1, 0:PAIR * C].rearrange("p (j c) -> p j c", j=PAIR)
        ln = LayerNorm(nc, ctx, "a_ln", PAIR, 1e-5)
        set_up = sem("set_up")
        turned, x1_done, x2_done = sem("turned"), sem("x1_done"), sem("x2_done")
        g_full, g_high, g_low = sem("g_full"), sem("g_high"), sem("g_low")
        v_full, v_done = sem("v_full"), sem("v_done")
        max_full, max_done, row_max_done = sem("max_full"), sem("max_done"), sem("row_max_done")
        max_turned, max_rows_done = sem("max_turned"), sem("max_rows_done")
        max_in = [sem("max_in0"), sem("max_in1")]
        score_full, probs_done, pv_full = sem("score_full"), sem("probs_done"), sem("pv_full")
        blocks_added = sem("blocks_added")
        log_done, inv_done, heads_done = sem("log_done"), sem("inv_done"), sem("heads_done")
        y_full, y_done, back_full, stored = sem("y_full"), sem("y_done"), sem("back_full"), sem("stored")
        slots = 2 * NH

        def of(b, k=0):
            return slice(b * S + k * T, b * S + (k + 1) * T)

        def both(b):
            return slice(b * S, (b + 1) * S)

        def late(s, by, has):
            stage, i = (3, s - by) if s >= by else (4, s - by + slots)
            return (stage, i) if has(stage, units) else None

        def projection(s, has):
            if s % 2 == 0:
                return None
            stage, h = (2, (s + 3) // 2) if s <= 11 else (1, (s - 13) // 2)
            return (stage, h) if has(stage, units) else None

        whole = [(WHOLE, 3, 0), (WHOLE + 4, 3, 1), (WHOLE - 8, 4, 2), (WHOLE - 4, 4, 3)]

        with nc.Block() as block:
            @block.gpsimd
            def _(pool):
                ln.setup(pool, set_up)
                pool.memset(row_max[:], 0.0).then_inc(set_up, 1)
                pool.wait_ge(set_up, 3)

                def step(unit, has, later):
                    for s in range(slots):
                        if late(s, KEY_LAG, has):
                            stage, i = late(s, KEY_LAG, has)
                            pool.wait_ge(probs_done, 16 * unit(stage).n + i + 1)
                            pool.tensor_tensor(probs[:, i % 8, 3 * T:4 * T], probs[:, i % 8, T:S],
                                               probs[:, i % 8, S:3 * T], ALU.add).then_inc(blocks_added, 1)
                        if s == 11 and has(0, units):
                            ln.add_eps(pool, unit(0))
                            ln.root(pool, unit(0))

                run_steps(pool, units + 4, 8, units, step, ways=4)

            @block.sync
            def _(sp):
                def step(unit, has, later):
                    if not has(3, units):
                        return
                    b = unit(3)
                    sp.wait_ge(max_rows_done, b + 1)
                    sp.dma_start(g.table_cols[T:T + 1, b.parity].rearrange("p b h (k t) -> p (b h k) t", t=T),
                                 max_rows[:, b.parity, :]).then_inc(max_in[b.parity], 16)

                run_steps(sp, units + 4, 8, units, step, ways=4)

            @block.scalar
            def _(act):
                act.preload_act_table_set("natural_log_exp_and_others")

                def step(unit, has, later):
                    f, n, a, b, c = (unit(k) for k in range(5))
                    for s in range(slots):
                        if projection(s, has):
                            stage, h = projection(s, has)
                            u = unit(stage)
                            act.wait_ge(g_full, 8 * u.n + h + 1)
                            if later(stage, 2):
                                act.wait_ge(score_full, 16 * u.n - 23 + h)
                            act.activation(gs[:, u.parity, h], proj[:, 0, 0:PT], ACT.Copy, scale=1.0 / WS)\
                               .then_inc(g_high, 1)
                        if late(s, KEY_LAG, has):
                            stage, i = late(s, KEY_LAG, has)
                            u = unit(stage)
                            act.wait_ge(score_full, 16 * u.n + i + 1)
                            if i >= 8 or later(stage, 1):
                                act.wait_ge(pv_full, 16 * u.n + i - 7)
                            act.activation(probs[:, i % 8, 0:3 * T], score_ps[:, i % 2, 0:3 * T], ACT.Exp).then_inc(probs_done, 1)
                        if s == 3 and has(1, units):
                            act.wait_ge(turned, n + 1)
                            if later(1, 4):
                                act.wait_ge(score_full, 16 * (n - 3))
                            act.activation(x1[:, n.way], proj[:, 1, 0:PT], ACT.Copy).then_inc(x1_done, 1)
                        if s in (7, 9) and has(2, units):
                            k = (s - 7) // 2
                            act.wait_ge(v_full, 2 * a.n + k + 1)
                            if k == 0 and later(2, 2):
                                act.wait_ge(pv_full, 16 * (a - 1))
                            act.activation(v[:, a.parity, 2 * k:2 * k + 2, :],
                                           proj[0:T, 1, :].rearrange("p (j n) -> p j n", j=2),
                                           ACT.Copy, scale=1.0 / WS).then_inc(v_done, 1)
                        if s == 1 and has(3, units):
                            act.wait_ge(max_turned, b + 1)
                            if later(3, 2):
                                act.wait_ge(max_in[b.parity], 16 * b.half)
                            act.activation(max_rows[:, b.parity, :], proj[0:48, 1, 0:T], ACT.Copy, scale=-1.0)\
                               .then_inc(max_rows_done, 1)
                        for at, stage, q in whole:
                            if s == at and has(stage, units):
                                u = unit(stage)
                                act.wait_ge(pv_full, 16 * u.n + 4 * q + 4)
                                if q or later(stage, 1):
                                    act.wait_ge(inv_done, 4 * u.n + q)
                                act.activation(log_sum[:, q % 2], pv_ps[:, q % 2, S:2 * S], ACT.Ln).then_inc(log_done, 1)
                                act.wait_ge(log_done, 4 * u.n + q + 1)
                                if q >= 2 or later(stage, 1):
                                    act.wait_ge(heads_done, 4 * u.n + q - 1)
                                act.activation(inv_sum[:, q % 2], log_sum[:, q % 2], ACT.Exp, scale=-1.0)\
                                   .then_inc(inv_done, 1)
                        if s == 9 and has(0, units):
                            if later(0, 2):
                                act.wait_ge(ln.squares_summed, f - 1)
                            ln.square(act, f)
                        if s == 12 and has(4, units):
                            act.wait_ge(y_full, c + 1)
                            if later(4, 1):
                                act.wait_ge(back_full, c.n)
                            act.activation(y[:], proj[:, 1, 0:PT], ACT.Identity, bias=g.y_bias[:, 2:3]).then_inc(y_done, 1)

                run_steps(act, units + 4, 8, units, step, ways=4)

            @block.vector
            def _(dve):
                def step(unit, has, later):
                    f, n, a, b, c = (unit(k) for k in range(5))
                    for s in range(slots):
                        if s == 0 and has(3, units):
                            dve.wait_ge(max_done, 16 * b.n + 16)
                            if later(3, 1):
                                dve.wait_ge(max_turned, b.n)
                            rows = row_max[:, 0:48].rearrange("p (b h k) -> p b h k", b=2, h=NH)
                            dve.tensor_copy(rows[:, :, :, 0], block_max[:, :, :, 0]).then_inc(row_max_done, 1)
                            dve.tensor_tensor(rows[:, :, :, 1:3], bcast(block_max[:, :, :, 1:2], [T, 2, NH, 2]),
                                              bcast(block_max[:, :, :, 2:3], [T, 2, NH, 2]), ALU.max)\
                               .then_inc(row_max_done, 1)
                        if has(2, units):
                            dve.wait_ge(max_full, 16 * a.n + s + 1)
                            if s == 0 and later(2, 1):
                                dve.wait_ge(row_max_done, 2 * a.n)
                            dve.tensor_reduce(block_max[:, s % 2, s // 2, :],
                                              max_ps[:, s % 2, 0:3 * T].rearrange("p (k t) -> p k t", k=3),
                                              AX.X, ALU.max).then_inc(max_done, 1)
                        if projection(s, has):
                            stage, h = projection(s, has)
                            u = unit(stage)
                            dve.wait_ge(g_high, 8 * u.n + h + 1)
                            low = gs[C:2 * C, u.parity, h]
                            dve.scalar_tensor_tensor(out=low, in0=proj[C:2 * C, 0, 0:PT], scalar=1.0 / WS, in1=low,
                                                     op0=ALU.mult, op1=ALU.subtract).then_inc(g_low, 1)
                        if s == 4 and has(1, units):
                            dve.wait_ge(x1_done, n + 1)
                            dve.tensor_tensor(x2[:, n.way], proj[:, 1, 0:PT], x1[:, n.way], ALU.subtract)\
                               .then_inc(x2_done, 1)
                        if s == 8 and has(0, units):
                            ln.center(dve, f, of_tiles(g.x, f, PAIR), later(0, 2))
                        if s == 10 and has(0, units):
                            ln.sum_squares(dve, f)
                        if s == 14 and has(0, units):
                            if later(0, 2):
                                dve.wait_ge(turned, f - 1)
                            ln.scale(dve, f, xn[:, f.parity])
                        for at, stage, q in whole:
                            if s == (at + 1) % slots and has(stage, units):
                                u = unit(stage)
                                dve.wait_ge(inv_done, 4 * u.n + q + 1)
                                if q == 0 and later(3, 1):
                                    dve.wait_ge(y_full, u.n)
                                dve.tensor_tensor(heads_out[:, q % 2, both(q // 2)], pv_ps[:, q % 2, 0:S],
                                                  inv_sum[:, q % 2], ALU.mult).then_inc(heads_done, 1)
                        if s == 15 and has(4, units):
                            dve.wait_ge(back_full, c + 1)
                            x = of_tiles(g.x, c, PAIR)
                            dve.tensor_tensor(x, back_ps, x, ALU.add).then_inc(stored, 1)

                run_steps(dve, units + 4, 8, units, step, ways=4)

            @block.tensor
            def _(pe):
                def step(unit, has, later):
                    n, a, b, c = (unit(k) for k in range(1, 5))

                    def turn():
                        pe.wait_ge(ln.done, n + 1)
                        if later(1, 2):
                            pe.wait_ge(max_rows_done, n - 1)
                        elif later(1, 1):
                            pe.wait_ge(x2_done, n.n)
                        for j in range(PAIR):
                            mm = turn_twice(pe, proj[:, 1, j * T:(j + 1) * T], xn[:, n.parity, j, :], g)
                        mm.then_inc(turned, 1)

                    def project(stage, h):
                        u = unit(stage)
                        if h == 0:
                            pe.wait_ge(x2_done, u + 1)
                        if h or later(stage, 1):
                            pe.wait_ge(g_low, 8 * u.n + h)
                        for part, x in enumerate((x1, x2)):
                            mm = pe.matmul(proj[:, 0, 0:PT], g.w_a[:, h, :], x[:, u.way], start=(part == 0),
                                           stop=(part == 1))
                        mm.then_inc(g_full, 1)

                    def values(k):
                        if k == 1:
                            pe.wait_ge(v_done, 2 * a.n + 1)
                        elif has(1, units):
                            pe.wait_ge(x2_done, a + 2)
                        else:
                            pe.wait_ge(max_rows_done, a.n)
                        for j in range(2):
                            for part, x in enumerate((x1, x2)):
                                mm = pe.matmul(proj[0:T, 1, j * 256:(j + 1) * 256], x[:, a.way, of(k, j)], g.w_v[:],
                                               start=(part == 0), stop=(part == 1))
                        mm.then_inc(v_full, 1)

                    def query_rows(m):
                        h, q = m // 2, m % 2
                        if q == 0:
                            pe.wait_ge(g_low, 8 * a.n + h + 1)
                        if m >= 2 or later(2, 1):
                            pe.wait_ge(max_done, 16 * a.n + m - 1)
                        out = max_ps[:, m % 2, 0:3 * T]
                        pe.matmul(out, g.ident_ones[0:T, :], g.table_rows[:, h, :], start=True, stop=False)
                        pe.matmul(out[:, 0:T], gs[:, a.parity, h, of(q, 0)], x1[:, a.way, of(q, 0)],
                                  start=False, stop=False)
                        pe.matmul(out[:, T:3 * T], gs[:, a.parity, h, of(q, 1)], x1[:, a.way, both(q)],
                                  start=False, stop=True).then_inc(max_full, 1)

                    def turn_maxima():
                        pe.wait_ge(row_max_done, 2 * b.n + 2)
                        if later(3, 2):
                            pe.wait_ge(stored, b - 1)
                        else:
                            pe.wait_ge(v_done, 2 * b.n + 2)
                        pe.transpose(proj[0:96, 1, 0:T], row_max[:], g.ident[0:T, 0:T]).then_inc(max_turned, 1)

                    def key_rows(stage, i):
                        u, h, q = unit(stage), i % NH, i // NH
                        if i == 0:
                            pe.wait_ge(max_in[u.parity], 16 * u.half + 16)
                        if i >= 2 or later(stage, 1):
                            pe.wait_ge(probs_done, 16 * u.n + i - 1)
                        out = score_ps[:, i % 2, 0:3 * T]
                        pe.matmul(out, g.ident_ones[:], g.table_cols[:, u.parity, q, h, :], start=True, stop=False)
                        for part, x in enumerate((x1, x2)):
                            pe.matmul(out[:, 0:S], x[:, u.way, of(q, 0)], gs[:, u.parity, h, both(q)],
                                      start=False, stop=False)
                            mm = pe.matmul(out[:, S:3 * T], x[:, u.way, of(q, 1)], gs[:, u.parity, h, of(q, 1)],
                                           start=False, stop=(part == 1))
                        mm.then_inc(score_full, 1)

                    def weigh(stage, group):
                        u, q = unit(stage), group // 2
                        if group >= 2 or later(stage, 1):
                            pe.wait_ge(heads_done, 4 * u.n + group - 1)
                        pe.wait_ge(probs_done, 16 * u.n + 4 * group + 4)
                        heads = [(j, (4 * group + j) % NH, (4 * group + j) % 8) for j in range(4)]
                        for k in range(2):
                            for j, h, at in heads:
                                p = probs[:, at, 0:S] if k == 0 else probs[:, at, S:3 * T]
                                pe.matmul(pv_ps[32 * j:32 * j + 32, group % 2, k * T:S],
                                          v[:, u.parity, 2 * q + k, h * DH:(h + 1) * DH], p,
                                          start=(k == 0), stop=(k == 1), skip_group_check=True)
                        pe.wait_ge(blocks_added, 16 * u.n + 4 * group + 4)
                        for j, h, at in heads:
                            sums = pv_ps[32 * j:32 * j + 32, group % 2, S:2 * S].rearrange("p (k t) -> p k t", k=2)
                            pe.matmul(sums, g.ones[:], probs[:, at, :].rearrange("p (k t) -> p k t", t=T)[:, 0:4:3, :],
                                      start=False, stop=True, skip_group_check=True).then_inc(pv_full, 1)

                    def out_project():
                        pe.wait_ge(heads_done, 4 * c.n + 4)
                        if has(2, units):
                            pe.wait_ge(v_done, 2 * a.n + 2)
                        elif has(3, units):
                            pe.wait_ge(max_rows_done, b + 1)
                        else:
                            pe.wait_ge(stored, c.n)
                        for half in range(2):
                            mm = pe.matmul(proj[half * C:(half + 1) * C, 1, 0:PT], g.w_o[:, half, :], heads_out[:, half, :],
                                           start=True, stop=True)
                        mm.then_inc(y_full, 1)

                    def turn_back():
                        pe.wait_ge(y_done, c + 1)
                        for j in range(PAIR):
                            mm = pe.matmul(back_ps[:, j, :], y[:, j * T:(j + 1) * T], g.fold[:, 0, :], start=True, stop=True)
                        mm.then_inc(back_full, 1)

                    for s in range(slots):
                        if s == 3 and has(1, units):
                            turn()
                        if projection(s, has):
                            project(*projection(s, has))
                        if has(2, units):
                            query_rows(s)
                        if s == 1 and has(3, units):
                            turn_maxima()
                        if s in (7, 9) and has(2, units):
                            values((s - 7) // 2)
                        if late(s, KEY_LAG, has):
                            key_rows(*late(s, KEY_LAG, has))
                        for at, stage, group in whole:
                            if s == at and has(stage, units):
                                weigh(stage, group)
                        if s == 11 and has(4, units):
                            out_project()
                        if s == 14 and has(4, units):
                            turn_back()

                run_steps(pe, units + 4, 8, units, step, ways=4)


def experts(nc, g, d, out):
    units = NT // PAIR
    with ExitStack() as ctx:
        def sb(n, shape, dt=F32):
            return ctx.enter_context(nc.sbuf_tensor(f"m_{n}", shape, dt))

        def ps(n, shape):
            return ctx.enter_context(nc.psum_tensor(f"m_{n}", shape, F32))

        def sem(n):
            return ctx.enter_context(nc.semaphore(f"m_{n}"))

        xn = sb("xn", [T, 4, PAIR, C])
        x1, x2 = sb("x1", [2 * C, 4, PT], F16), sb("x2", [2 * C, 4, PT], F16)
        logits = sb("logits", [T, PAIR, NE])
        best, best_at = sb("best", [T, PAIR, 8]), sb("best_at", [T, PAIR, 8], U32)
        at = sb("at", [T, PAIR, 2])
        behind, odds, total = sb("behind", [T, PAIR]), sb("odds", [T, PAIR]), sb("total", [T, PAIR])
        share = sb("share", [T, PAIR, 2])
        chosen = sb("chosen", [T, 2, PAIR, NE])
        part = sb("part", [T, 2, PAIR, NE])
        gates = sb("gates", [T, PAIR, 6, NE])
        gate_rows = sb("gate_rows", [96, 2, PT], F16)
        hidden, weighted = sb("hidden", [FE, 4, PT]), sb("weighted", [FE, 8, PT])
        y = sb("y", [128, PT])
        scaled, by_gamma, plus_beta = sb("scaled", [T, PAIR, C]), sb("by_gamma", [T, PAIR, C]), sb("plus_beta", [T, PAIR, C])
        result = sb("result", [T, 2, PAIR, C])
        h_ps, gate_bc = ps("h", [128, 2, 512]), ps("gate_bc", [128, 2, 512])
        y_ps, xt_ps, gate_ps = ps("y_ps", [128, 2, 512]), ps("xt_ps", [128, 512]), ps("gate_ps", [128, 512])
        back_ps = xt_ps[0:T, 0:PAIR * C].rearrange("p (j c) -> p j c", j=PAIR)
        ln1, ln2 = LayerNorm(nc, ctx, "m_ln", PAIR, 1e-5), LayerNorm(nc, ctx, "m_out_ln", PAIR, 1e-5)
        set_up = sem("set_up")
        turned, x1_done, x2_done = sem("turned"), sem("x1_done"), sem("x2_done")
        logits_full, logits_done, best_done, best_at_done = (
            sem("logits_full"), sem("logits_done"), sem("best_done"), sem("best_at_done"))
        at_done, behind_done, odds_done, total_done, share_done = (
            sem("at_done"), sem("behind_done"), sem("odds_done"), sem("total_done"), sem("share_done"))
        chosen_done, part_done, gates_done = sem("chosen_done"), sem("part_done"), sem("gates_done")
        gates_turned, gates_high, gates_low = sem("gates_turned"), sem("gates_high"), sem("gates_low")
        gate_full = sem("gate_full")
        up_full, relu_done, weighted_done, down_done = (
            sem("up_full"), sem("relu_done"), sem("weighted_done"), sem("down_done"))
        y_done, back_full = sem("y_done"), sem("back_full")
        by_gamma_done, plus_beta_done, result_done = sem("by_gamma_done"), sem("plus_beta_done"), sem("result_done")
        stored = [sem("stored0"), sem("stored1")]
        slots = NE
        out_rows = out.rearrange("b (k p) c -> p (b k) c", p=T)

        def weighing(s, has):
            stage, e = (2, s - DOWN_LAG) if s >= DOWN_LAG else (3, s - DOWN_LAG + NE)
            return (stage, e) if s % 2 == 0 and has(stage, units) else None

        with nc.Block() as block:
            @block.gpsimd
            def _(pool):
                ln1.setup(pool, set_up)
                ln2.setup(pool, set_up)
                pool.wait_ge(set_up, 4)

                def step(unit, has, later):
                    if has(0, units):
                        ln1.add_eps(pool, unit(0))
                        ln1.root(pool, unit(0))
                    if has(4, units):
                        d = unit(4)
                        ln2.add_eps(pool, d)
                        ln2.root(pool, d)
                        if later(4, 1):
                            pool.wait_ge(by_gamma_done, d.n)
                        ln2.scale(pool, d, scaled[:])
                        pool.wait_ge(ln2.done, d + 1)
                        if later(4, 1):
                            pool.wait_ge(plus_beta_done, d.n)
                        pool.tensor_tensor(by_gamma[:], scaled[:], per_channel(g.rows[:, 10, :], PAIR), ALU.mult)\
                            .then_inc(by_gamma_done, 1)
                        pool.wait_ge(by_gamma_done, d + 1)
                        if later(4, 1):
                            pool.wait_ge(result_done, d.n)
                        pool.tensor_tensor(plus_beta[:], by_gamma[:], per_channel(g.rows[:, 11, :], PAIR), ALU.add)\
                            .then_inc(plus_beta_done, 1)
                        pool.wait_ge(plus_beta_done, d + 1)
                        if later(4, 2):
                            pool.wait_ge(stored[d.parity], 16 * d.half)
                        pool.tensor_tensor(result[:, d.parity], plus_beta[:], of_tiles(g.x, d, PAIR), ALU.add)\
                            .then_inc(result_done, 1)

                run_steps(pool, units + 4, 8, units, step, ways=4)

            @block.sync
            def _(sp):
                def step(unit, has, later):
                    if has(4, units):
                        d = unit(4)
                        sp.wait_ge(result_done, d + 1)
                        sp.dma_start(out_rows[:, bass.ds(d.n * PAIR, PAIR), :], result[:, d.parity])\
                          .then_inc(stored[d.parity], 16)

                run_steps(sp, units + 4, 8, units, step, ways=4)
                for s in stored:
                    sp.wait_ge(s, 16 * (units // 2))

            @block.scalar
            def _(act):
                def step(unit, has, later):
                    f, n, b, c, d = (unit(k) for k in range(5))
                    for s in range(slots):
                        if has(2, units):
                            act.wait_ge(up_full, NE * b.n + s + 1)
                            if s >= 4 or later(2, 1):
                                act.wait_ge(weighted_done, NE * b.n + s - 3)
                            act.activation(hidden[:, s % 4], h_ps[:, s % 2, 0:PT], ACT.Relu, bias=g.moe_b1[:, s:s + 1],
                                           scale=1.0 / WS).then_inc(relu_done, 1)
                        if s == 14 and has(0, units):
                            act.wait_ge(turned, f + 1)
                            if later(0, 4):
                                act.wait_ge(up_full, NE * (f - 3))
                            act.activation(x1[:, f.way], xt_ps[:, 0:PT], ACT.Copy).then_inc(x1_done, 1)
                        if s == 3 and has(3, units):
                            act.wait_ge(down_done, NE * c.n + NE)
                            if later(3, 1):
                                act.wait_ge(back_full, c.n)
                            act.activation(y[:], y_ps[:, c.parity, 0:PT], ACT.Copy).then_inc(y_done, 1)
                        if s == 1 and has(0, units):
                            if later(0, 2):
                                act.wait_ge(ln1.squares_summed, f - 1)
                            ln1.square(act, f)
                        if s == 2 and has(4, units):
                            if later(4, 2):
                                act.wait_ge(ln2.squares_summed, d - 1)
                            ln2.square(act, d)
                        if s == 5 and has(1, units):
                            act.wait_ge(behind_done, n + 1)
                            if later(1, 1):
                                act.wait_ge(share_done, 2 * n.n)
                            act.activation(odds[:], behind[:], ACT.Exp).then_inc(odds_done, 1)
                        if s == 13 and has(1, units):
                            act.wait_ge(gates_turned, n + 1)
                            act.activation(gate_rows[:, n.parity], gate_ps[0:96, 0:PT], ACT.Copy).then_inc(gates_high, 1)

                run_steps(act, units + 4, 8, units, step, ways=4)

            @block.vector
            def _(dve):
                def step(unit, has, later):
                    f, n, b, c, d = (unit(k) for k in range(5))
                    for s in range(slots):
                        if has(2, units):
                            dve.wait_ge(relu_done, NE * b.n + s + 1)
                            dve.wait_ge(gate_full, NE * b.n + s + 1)
                            if s >= 8 or later(2, 1):
                                dve.wait_ge(down_done, NE * b.n + s - 7)
                            dve.tensor_tensor(weighted[:, s % 8], gate_bc[:, s % 2, 0:PT], hidden[:, s % 4], ALU.mult)\
                               .then_inc(weighted_done, 1)
                        if s == 15 and has(0, units):
                            dve.wait_ge(x1_done, f + 1)
                            dve.tensor_tensor(x2[:, f.way], xt_ps[:, 0:PT], x1[:, f.way], ALU.subtract)\
                               .then_inc(x2_done, 1)
                        if s == 0 and has(0, units):
                            ln1.center(dve, f, of_tiles(g.x, f, PAIR), later(0, 2))
                        if s == 2 and has(1, units):
                            dve.wait_ge(logits_full, n + 1)
                            if later(1, 1):
                                dve.wait_ge(best_at_done, 4 * n.n)
                            dve.scalar_tensor_tensor(
                                out=logits[:], in0=gate_ps[0:T, 0:PAIR * NE].rearrange("p (j e) -> p j e", j=PAIR),
                                scalar=1.0 / WS, in1=per_channel(g.gate_b[:], PAIR, NE), op0=ALU.mult, op1=ALU.add)\
                               .then_inc(logits_done, 1)
                        if s == 3:
                            if has(1, units):
                                dve.wait_ge(logits_done, n + 1)
                            if has(0, units):
                                ln1.sum_squares(dve, f)
                            if has(1, units):
                                for j in range(PAIR):
                                    dve.max(best[:, j, :], logits[:, j, :]).then_inc(best_done, 1)
                        if s == 4:
                            if has(1, units):
                                dve.wait_ge(best_done, 4 * n.n + 4)
                            if has(4, units):
                                ln2.sum_squares(dve, d)
                            if has(1, units):
                                for j in range(PAIR):
                                    dve.max_index(best_at[:, j, :], best[:, j, :], logits[:, j, :])\
                                       .then_inc(best_at_done, 1)
                                dve.tensor_tensor(behind[:], best[:, :, 1], best[:, :, 0], ALU.subtract)\
                                   .then_inc(behind_done, 1)
                        if s == 5 and has(1, units):
                            dve.wait_ge(best_at_done, 4 * n.n + 4)
                            dve.tensor_copy(at[:], best_at[:, :, 0:2]).then_inc(at_done, 1)
                        if s == 6 and has(1, units):
                            dve.wait_ge(odds_done, n + 1)
                            dve.tensor_scalar(total[:], odds[:], 1.0, None, ALU.add).then_inc(total_done, 1)
                            dve.wait_ge(at_done, n + 1)
                            for k in range(2):
                                dve.tensor_tensor(chosen[:, k], per_channel(g.iota[:], PAIR, NE),
                                                  bcast(at[:, :, k:k + 1], [T, PAIR, NE]), ALU.is_equal)\
                                   .then_inc(chosen_done, 1)
                            dve.wait_ge(total_done, n + 1)
                            dve.reciprocal(share[:, :, 0], total[:]).then_inc(share_done, 1)
                        if s == 7 and has(1, units):
                            dve.wait_ge(share_done, 2 * n.n + 1)
                            dve.tensor_tensor(share[:, :, 1], share[:, :, 0], odds[:], ALU.mult).then_inc(share_done, 1)
                        if s == 8 and has(1, units):
                            dve.wait_ge(share_done, 2 * n.n + 2)
                            dve.wait_ge(chosen_done, 2 * n.n + 2)
                            for k in range(2):
                                dve.tensor_tensor(part[:, k], chosen[:, k], bcast(share[:, :, k:k + 1], [T, PAIR, NE]),
                                                  ALU.mult).then_inc(part_done, 1)
                        if s == 9 and has(1, units):
                            dve.wait_ge(part_done, 2 * n.n + 2)
                            if later(1, 1):
                                dve.wait_ge(gates_turned, n.n)
                            six = [T, PAIR, 6, NE]
                            dve.tensor_tensor(gates[:], bcast(part[:, 0].unsqueeze(2), six),
                                              bcast(part[:, 1].unsqueeze(2), six), ALU.add).then_inc(gates_done, 1)
                        if s == 14 and has(1, units):
                            dve.wait_ge(gates_high, n + 1)
                            low = gate_rows[32:64, n.parity]
                            dve.tensor_tensor(low, gate_ps[32:64, 0:PT], low, ALU.subtract).then_inc(gates_low, 1)
                        if s == 7 and has(3, units):
                            dve.wait_ge(back_full, c + 1)
                            if later(3, 2):
                                dve.wait_ge(ln2.done, c - 1)
                            dve.tensor_tensor(ln2.centered[:, c.parity], back_ps, xn[:, c.way], ALU.add)\
                               .then_inc(ln2.centred, 1)
                        if s == 10 and has(0, units):
                            if later(0, 4):
                                dve.wait_ge(ln2.centred, f - 3)
                            ln1.scale(dve, f, xn[:, f.way])

                run_steps(dve, units + 4, 8, units, step, ways=4)

            @block.tensor
            def _(pe):
                def step(unit, has, later):
                    f, n, b, c = (unit(k) for k in range(4))

                    def turn():
                        pe.wait_ge(ln1.done, f + 1)
                        if has(3, units):
                            pe.wait_ge(ln2.centred, c + 1)
                        elif later(0, 1):
                            pe.wait_ge(x2_done, f.n)
                        for j in range(PAIR):
                            mm = turn_twice(pe, xt_ps[:, j * T:(j + 1) * T], xn[:, f.way, j, :], g)
                        mm.then_inc(turned, 1)

                    def gate():
                        pe.wait_ge(x2_done, n + 1)
                        if later(1, 1):
                            pe.wait_ge(gates_low, n.n)
                        for j in range(PAIR):
                            for k, x in enumerate((x1, x2)):
                                mm = pe.matmul(gate_ps[0:T, j * NE:(j + 1) * NE], x[:, n.way, j * T:(j + 1) * T],
                                               g.w_gate[:], start=(k == 0), stop=(k == 1))
                        mm.then_inc(logits_full, 1)

                    def turn_gates():
                        pe.wait_ge(gates_done, n + 1)
                        for j in range(PAIR):
                            mm = pe.transpose(gate_ps[0:96, j * T:(j + 1) * T],
                                              gates[:, j].rearrange("p k e -> p (k e)"), g.ident[0:T, 0:T])
                        mm.then_inc(gates_turned, 1)

                    def up(e):
                        if e >= 2 or later(2, 1):
                            pe.wait_ge(relu_done, NE * b.n + e - 1)
                        for k, x in enumerate((x1, x2)):
                            mm = pe.matmul(h_ps[:, e % 2, 0:PT], g.moe_w1[:, e, :], x[:, b.way], start=(k == 0), stop=(k == 1))
                        mm.then_inc(up_full, 1)

                    def spread_gate(e):
                        if e == 0:
                            pe.wait_ge(gates_low, b + 1)
                        if e >= 2 or later(2, 1):
                            pe.wait_ge(weighted_done, NE * b.n + e - 1)
                        pe.matmul(gate_bc[:, e % 2, 0:PT], g.selector[:, e, :], gate_rows[:, b.parity],
                                  start=True, stop=True).then_inc(gate_full, 1)

                    def down(stage, e):
                        u, half = unit(stage), e % 2
                        out = y_ps[half * C:(half + 1) * C, u.parity, 0:PT]
                        if e == 0:
                            if later(stage, 2):
                                pe.wait_ge(y_done, u - 1)
                            pe.matmul(out, g.moe_b2[:], gate_rows[:, u.parity], start=True, stop=False)
                        pe.wait_ge(weighted_done, NE * u.n + e + 1)
                        pe.matmul(out, g.moe_w2[:, e, :], weighted[:, e % 8], start=(e == 1), stop=(e >= NE - 2))\
                          .then_inc(down_done, 1)

                    def turn_back():
                        pe.wait_ge(y_done, c + 1)
                        if has(1, units):
                            pe.wait_ge(x2_done, n + 1)
                        elif later(3, 1):
                            pe.wait_ge(ln2.centred, c.n)
                        for j in range(PAIR):
                            mm = pe.matmul(back_ps[:, j, :], y[:, j * T:(j + 1) * T], g.fold[:, 1, :], start=True, stop=True)
                        mm.then_inc(back_full, 1)

                    for s in range(slots):
                        if s == 13 and has(0, units):
                            turn()
                        if has(2, units):
                            up(s)
                        if weighing(s, has):
                            stage, e = weighing(s, has)
                            down(stage, e)
                            down(stage, e + 1)
                        if has(2, units):
                            spread_gate(s)
                        if s == 1 and has(1, units):
                            gate()
                        if s == 5 and has(3, units):
                            turn_back()
                        if s == 12 and has(1, units):
                            turn_gates()

                run_steps(pe, units + 4, 8, units, step, ways=4)


_LOADS = {
    "item_emb": "L0_tok_item_emb", "pos_emb": "L0_tok_pos_emb", "ln0_w": "L0_tok_ln0_w", "ln0_b": "L0_tok_ln0_b",
    "fln_w": "L0_tok_fln_w", "fln_b": "L0_tok_fln_b", "d1_w": "L0_tok_d1_w",
    "d1_b": "L0_tok_d1_b", "d2_w": "L0_tok_d2_w", "d2_b": "L0_tok_d2_b", "iln_w": "L0_tok_iln_w",
    "iln_b": "L0_tok_iln_b", "Wq": "L0_attn_Wq", "Wk": "L0_attn_Wk", "Wv": "L0_attn_Wv", "Wo": "L0_attn_Wo",
    "bo": "L0_attn_bo", "gate_w": "L0_ffn_gate_w", "gate_b": "L0_ffn_gate_b", "w1": "L0_ffn_w1", "b1": "L0_ffn_b1",
    "w2": "L0_ffn_w2", "b2": "L0_ffn_b2", "gamma": "L0_ffn_gamma", "beta": "L0_ffn_beta",
}


class Names:
    pass


def build(nc, d, out):
    with ExitStack() as ctx:
        def sb(n, shape, dt=F32):
            return ctx.enter_context(nc.sbuf_tensor(n, shape, dt))

        g = Names()
        g.ctx, g.ffn_sems = ctx, {}
        g.x = sb("x_stream", [T, NT, C])
        g.ids = sb("ids_sb", [T, NT], I32)
        g.ident = sb("ident_sb", [128, 128])
        g.circulant = sb("circulant", [T, 2, CH, S])
        g.circulant_in = [ctx.enter_context(nc.semaphore(f"circulant_in{n}")) for n in range(2)]
        g.fold = sb("fold_sb", [2 * C, 2, C])
        g.ident_ones = sb("ident_ones_sb", [T + 1, T], BF16)
        g.ones = sb("ones_sb", [T, DH])
        g.pos = sb("pos_sb", [T, 2, C])
        g.rows = sb("rows_sb", [T, 12, C])
        g.iota = sb("iota_sb", [T, NE])
        g.parity = sb("parity_sb", [C, 2])
        g.gate_b = sb("gate_b_sb", [T, NE])
        g.table_rows = sb("table_rows_sb", [T, NH, 3 * T], BF16)
        g.table_cols = sb("table_cols_sb", [T + 1, 2, 2, NH, 3 * T], BF16)
        g.selector = sb("selector_sb", [96, NE, 128], F16)
        g.ffn_w1 = sb("ffn_w1_sb", [2 * C, 2, DFF], F16)
        g.ffn_b1 = sb("ffn_b1_sb", [128, 2, 2])
        g.ffn_w2 = sb("ffn_w2_sb", [128, 2, 2, C])
        g.y_bias = sb("y_bias_sb", [128, 3])
        g.w_a = sb("w_a_sb", [2 * C, NH, 2 * C], F16)
        g.w_v = sb("w_v_sb", [2 * C, NH * DH], F16)
        g.w_o = sb("w_o_sb", [128, 2, C])
        g.w_gate = sb("w_gate_sb", [2 * C, NE], F16)
        g.moe_w1 = sb("moe_w1_sb", [2 * C, NE, FE], F16)
        g.moe_b1 = sb("moe_b1_sb", [128, NE])
        g.moe_w2 = sb("moe_w2_sb", [128, NE, C])
        g.moe_b2 = sb("moe_b2_sb", [96, C], F16)
        d.filters = nc.dram_tensor("kernels", [2, C, 2 * S], F32, kind="Internal").ap()
        prepare_and_embed(nc, g, d)
        for l in range(2):
            spectral_filter(nc, g, d, l)
            feed_forward(nc, g, d, l)
        attention(nc, g, d)
        experts(nc, g, d, out)


def shape_constants():
    bf = mybir.dt.np(BF16)
    j, k = np.arange(2 * S)[None, :], np.arange(K)[:, None]
    weight = np.where((k == 0) | (k == S // 2), 1.0, 2.0) / S
    angle = 2 * np.pi * ((k * j) % S) / S
    sine = weight * np.where((k == 0) | (k == S // 2), 0.0, -np.sin(angle))
    dft = np.stack([weight * np.cos(angle), -sine, sine], 1).astype(np.float32)
    slopes = 2.0 ** -(np.arange(NH) + 1.0)
    q, s = np.arange(S)[:, None], np.arange(S)[None, :]
    bias = np.where(s <= q, slopes[:, None, None] * (s - q), NEG)
    table_rows = np.concatenate([bias[:, 0:T, 0:T], bias[:, T:S, 0:T], bias[:, T:S, T:S]], 2).transpose(1, 0, 2)
    keys = bias.transpose(2, 0, 1)
    table_cols = np.concatenate([keys[0:T], keys[T:S, :, T:S]], 2)
    selector = np.zeros((96, NE, 128), np.float16)
    for e in range(NE):
        selector[e, e] = 1
        selector[32 + e, e] = 1
    even = (np.arange(C) // NE) % 2 == 0
    return {
        "dft": dft, "table_rows": table_rows.astype(bf), "table_cols": table_cols.astype(bf), "selector": selector,
        "ident": np.eye(128, dtype=np.float32),
        "fold": np.stack([np.tile(np.eye(C), (2, 1)), np.tile(np.eye(C) - 1 / C, (2, 1))], 1).astype(np.float32),
        "ident_ones": np.concatenate([np.eye(T), np.ones((1, T))]).astype(bf),
        "iota": np.tile(np.arange(NE, dtype=np.float32), (T, 1)),
        "parity": np.stack([even, ~even], 1).astype(np.float32),
    }


def kernel(**inputs):
    import concourse.bacc as bacc
    from concourse.bass_utils import run_bass_kernel_spmd

    nc = bacc.Bacc("TRN2", target_bir_lowering=False, num_devices=1)
    arrays = {name: np.ascontiguousarray(inputs[source]) for name, source in _LOADS.items()}
    arrays["ids"] = np.ascontiguousarray(np.asarray(inputs["x"]).reshape(B, 2, T).transpose(2, 0, 1).reshape(T, NT))
    arrays["cw"] = np.ascontiguousarray(np.asarray(inputs["L0_tok_cw"]).transpose(1, 0, 3, 2))
    arrays["d1_b"] = np.ascontiguousarray(arrays["d1_b"].reshape(2, 2, 128).transpose(2, 0, 1))
    arrays["b1"] = np.ascontiguousarray(arrays["b1"].T)
    arrays.update(shape_constants())
    d = Names()
    for name, a in arrays.items():
        d.__dict__[name] = nc.dram_tensor(f"in_{name}", a.shape, mybir.dt.from_np(a.dtype), kind="ExternalInput").ap()
    out = nc.dram_tensor("out", (B, S, C), F32, kind="ExternalOutput").ap()
    build(nc, d, out)
    result = run_bass_kernel_spmd(nc, [{f"in_{name}": a for name, a in arrays.items()}], core_ids=[0])
    return result.results[0]["out"]
```
